# Optimizing a Trainium2 kernel written in Bass

```python
import numpy as np
import jax
import jax.numpy as jnp

def _softmax(x, axis=-1):
    return jax.nn.softmax(x, axis=axis)

def _gelu(x):
    return jax.nn.gelu(x, approximate=True)

def _silu(x):
    return jax.nn.silu(x)

def _sigmoid(x):
    return jax.nn.sigmoid(x)

def _layernorm(x, axis=-1, eps=1e-05):
    m = jnp.mean(x, axis=axis, keepdims=True)
    v = jnp.var(x, axis=axis, keepdims=True)
    return (x - m) / jnp.sqrt(v + eps)

def _scatter_add(tgt, idx, src, axis=0):
    return tgt.at[idx].add(src)

def _segment_sum(src, seg, n):
    return jax.ops.segment_sum(src, seg, n)
kernel_name = 'mk_seq_postln_d2_jaxref_r8_37b009'

def setup_inputs(seed: int=0):
    np.random.seed(seed)
    _w = jnp.asarray

    def _L0_attn_setup():
        import jax, jax.numpy as jnp
        import numpy as np
        key = jax.random.key(seed)
        B, C, N = (8, 32, 256)
        x = jax.random.normal(key, (B, C, N), dtype=jnp.float32)
        return {'x': x}
    _L0_attn_in = _L0_attn_setup()

    def _L0_ffn_setup():
        import jax, jax.numpy as jnp
        import numpy as np
        BLOCK_SIZE = 32
        HIDDEN_SIZE = 256
        MLP_DIM = 2048
        NVFP4_LUT = jnp.array([0.0, 0.5, 1.0, 1.5, 2.0, 3.0, 4.0, 6.0, 0.0, -0.5, -1.0, -1.5, -2.0, -3.0, -4.0, -6.0], dtype=jnp.float32)

        def dequant_nvfp4(W_packed, scales, block=BLOCK_SIZE):
            N = W_packed.shape[0]
            low = W_packed & 15
            high = W_packed >> 4 & 15
            idx = jnp.stack([low, high], axis=-1).reshape(N, -1)
            vals = NVFP4_LUT[idx]
            K = vals.shape[1]
            vals = vals.reshape(N, K // block, block) * scales[:, :, None]
            return vals.reshape(N, K)
        key = jax.random.key(seed)
        ks = jax.random.split(key, 7)
        x = jax.random.normal(ks[0], (4, 32, HIDDEN_SIZE), dtype=jnp.float32)
        gate_W_packed = jax.random.randint(ks[1], (MLP_DIM, HIDDEN_SIZE // 2), 0, 32, dtype=jnp.int32)
        gate_scales = jax.random.uniform(ks[2], (MLP_DIM, HIDDEN_SIZE // BLOCK_SIZE), dtype=jnp.float32) * 0.1 + 0.001
        up_W_packed = jax.random.randint(ks[3], (MLP_DIM, HIDDEN_SIZE // 2), 0, 32, dtype=jnp.int32)
        up_scales = jax.random.uniform(ks[4], (MLP_DIM, HIDDEN_SIZE // BLOCK_SIZE), dtype=jnp.float32) * 0.1 + 0.001
        down_W_packed = jax.random.randint(ks[5], (HIDDEN_SIZE, MLP_DIM // 2), 0, 32, dtype=jnp.int32)
        down_scales = jax.random.uniform(ks[6], (HIDDEN_SIZE, MLP_DIM // BLOCK_SIZE), dtype=jnp.float32) * 0.1 + 0.001
        return {'x': x, 'gate_W_packed': gate_W_packed, 'gate_scales': gate_scales, 'up_W_packed': up_W_packed, 'up_scales': up_scales, 'down_W_packed': down_W_packed, 'down_scales': down_scales}
    _L0_ffn_in = _L0_ffn_setup()

    def _L1_attn_setup():
        import jax, jax.numpy as jnp
        import numpy as np
        from jax import lax
        D_MODEL = 256
        D_STATE = 64
        D_CONV = 4
        EXPAND = 2
        HEADDIM = 128
        NGROUPS = 1
        CHUNK = 32
        D_INNER = EXPAND * D_MODEL
        NHEADS = D_INNER // HEADDIM
        D_IN_PROJ = 2 * D_INNER + 2 * NGROUPS * D_STATE + NHEADS
        CONV_DIM = D_INNER + 2 * NGROUPS * D_STATE
        EPS = 1e-05

        def segsum(x):
            T = x.shape[-1]
            xr = jnp.broadcast_to(x[..., :, None], x.shape + (T,))
            mask_lo = jnp.tril(jnp.ones((T, T), bool), -1)
            xr = jnp.where(mask_lo, xr, 0.0)
            seg = jnp.cumsum(xr, axis=-2)
            mask = jnp.tril(jnp.ones((T, T), bool), 0)
            return jnp.where(mask, seg, -jnp.inf)

        def ssd_minimal_discrete(X, A, B, C, block_len):
            b, L, h, p = X.shape
            n = B.shape[-1]
            c = L // block_len
            X = X.reshape(b, c, block_len, h, p)
            B = B.reshape(b, c, block_len, h, n)
            C = C.reshape(b, c, block_len, h, n)
            A = A.reshape(b, c, block_len, h).transpose(0, 3, 1, 2)
            A_cumsum = jnp.cumsum(A, axis=-1)
            Lmat = jnp.exp(segsum(A))
            Y_diag = jnp.einsum('bclhn,bcshn,bhcls,bcshp->bclhp', C, B, Lmat, X)
            decay_states = jnp.exp(A_cumsum[:, :, :, -1:] - A_cumsum)
            states = jnp.einsum('bclhn,bhcl,bclhp->bchpn', B, decay_states, X)
            init = jnp.zeros_like(states[:, :1])
            states = jnp.concatenate([init, states], axis=1)
            A_last = jnp.pad(A_cumsum[:, :, :, -1], ((0, 0), (0, 0), (1, 0)))
            decay_chunk = jnp.exp(segsum(A_last))
            new_states = jnp.einsum('bhzc,bchpn->bzhpn', decay_chunk, states)
            states, final_state = (new_states[:, :-1], new_states[:, -1])
            state_decay_out = jnp.exp(A_cumsum)
            Y_off = jnp.einsum('bclhn,bchpn,bhcl->bclhp', C, states, state_decay_out)
            Y = (Y_diag + Y_off).reshape(b, L, h, p)
            return (Y, final_state)
        key = jax.random.key(seed)
        ks = jax.random.split(key, 6)
        Bsz, Lsz = (2, 256)
        return {'u': jax.random.normal(ks[0], (Bsz, Lsz, D_MODEL), jnp.float32), 'W_in': jax.random.normal(ks[1], (D_IN_PROJ, D_MODEL), jnp.float32) * 0.02, 'W_conv': jax.random.normal(ks[2], (CONV_DIM, 1, D_CONV), jnp.float32) * 0.2, 'b_conv': jnp.zeros((CONV_DIM,), jnp.float32), 'dt_bias': jax.random.normal(ks[3], (NHEADS,), jnp.float32) * 0.5, 'A_log': jax.random.uniform(ks[4], (NHEADS,), jnp.float32, 0.0, 2.77), 'D': jnp.ones((NHEADS,), jnp.float32), 'norm_w': jnp.ones((D_INNER,), jnp.float32), 'W_out': jax.random.normal(ks[5], (D_MODEL, D_INNER), jnp.float32) * 0.02}
    _L1_attn_in = _L1_attn_setup()

    def _L1_ffn_setup():
        import jax, jax.numpy as jnp
        import numpy as np

        def _sparsify_2to4(h):
            B, S, I = h.shape
            g = h.reshape(B, S, I // 4, 4)
            a = jnp.abs(g)
            _, idx = jax.lax.top_k(a, 2)
            pos = jnp.arange(4)
            mask = (pos == idx[..., 0:1]) | (pos == idx[..., 1:2])
            return (g * mask.astype(g.dtype)).reshape(B, S, I)
        key = jax.random.key(seed)
        k1, k2, k3, k4 = jax.random.split(key, 4)
        B, S, H, I = (4, 256, 256, 1024)
        x = jax.random.normal(k1, (B, S, H), dtype=jnp.float32)
        w_gate = jax.random.normal(k2, (H, I), dtype=jnp.float32) / np.sqrt(H)
        w_up = jax.random.normal(k3, (H, I), dtype=jnp.float32) / np.sqrt(H)
        w_down = jax.random.normal(k4, (I, H), dtype=jnp.float32) / np.sqrt(I)
        return {'x': x, 'w_gate': w_gate, 'w_up': w_up, 'w_down': w_down}
    _L1_ffn_in = _L1_ffn_setup()
    _d = {'L0_attn_x': _L0_attn_in['x'], 'L0_ffn_gate_W_packed': _L0_ffn_in['gate_W_packed'], 'L0_ffn_gate_scales': _L0_ffn_in['gate_scales'], 'L0_ffn_up_W_packed': _L0_ffn_in['up_W_packed'], 'L0_ffn_up_scales': _L0_ffn_in['up_scales'], 'L0_ffn_down_W_packed': _L0_ffn_in['down_W_packed'], 'L0_ffn_down_scales': _L0_ffn_in['down_scales'], 'L1_attn_W_in': _L1_attn_in['W_in'], 'L1_attn_W_conv': _L1_attn_in['W_conv'], 'L1_attn_b_conv': _L1_attn_in['b_conv'], 'L1_attn_dt_bias': _L1_attn_in['dt_bias'], 'L1_attn_A_log': _L1_attn_in['A_log'], 'L1_attn_D': _L1_attn_in['D'], 'L1_attn_norm_w': _L1_attn_in['norm_w'], 'L1_attn_W_out': _L1_attn_in['W_out'], 'L1_ffn_w_gate': _L1_ffn_in['w_gate'], 'L1_ffn_w_up': _L1_ffn_in['w_up'], 'L1_ffn_w_down': _L1_ffn_in['w_down']}
    _x0 = _d['L0_attn_x']
    _d['L0_attn_x'] = jax.random.normal(jax.random.fold_in(jax.random.key(seed), 1), (2, 2048, 256), dtype=_x0.dtype)
    del _x0
    return _d

def reference(L0_attn_x, L0_ffn_gate_W_packed, L0_ffn_gate_scales, L0_ffn_up_W_packed, L0_ffn_up_scales, L0_ffn_down_W_packed, L0_ffn_down_scales, L1_attn_W_in, L1_attn_W_conv, L1_attn_b_conv, L1_attn_dt_bias, L1_attn_A_log, L1_attn_D, L1_attn_norm_w, L1_attn_W_out, L1_ffn_w_gate, L1_ffn_w_up, L1_ffn_w_down):

    def _L0_attn_ref(x):
        import jax, jax.numpy as jnp
        import numpy as np
        scores = jnp.einsum('bci,bcj->bij', x, x)
        weights = jax.nn.softmax(scores, axis=-1)
        context = jnp.einsum('bij,bcj->bci', weights, x)
        return context

    def _L0_ffn_ref(x, gate_W_packed, gate_scales, up_W_packed, up_scales, down_W_packed, down_scales):
        import jax, jax.numpy as jnp
        import numpy as np
        BLOCK_SIZE = 32
        HIDDEN_SIZE = 256
        MLP_DIM = 2048
        NVFP4_LUT = jnp.array([0.0, 0.5, 1.0, 1.5, 2.0, 3.0, 4.0, 6.0, 0.0, -0.5, -1.0, -1.5, -2.0, -3.0, -4.0, -6.0], dtype=jnp.float32)

        def dequant_nvfp4(W_packed, scales, block=BLOCK_SIZE):
            N = W_packed.shape[0]
            low = W_packed & 15
            high = W_packed >> 4 & 15
            idx = jnp.stack([low, high], axis=-1).reshape(N, -1)
            vals = NVFP4_LUT[idx]
            K = vals.shape[1]
            vals = vals.reshape(N, K // block, block) * scales[:, :, None]
            return vals.reshape(N, K)
        B, S, H = x.shape
        xt = x.reshape(B * S, H)
        Wg = dequant_nvfp4(gate_W_packed, gate_scales)
        Wu = dequant_nvfp4(up_W_packed, up_scales)
        Wd = dequant_nvfp4(down_W_packed, down_scales)
        gate = jnp.einsum('th,nh->tn', xt, Wg)
        up = jnp.einsum('th,nh->tn', xt, Wu)
        gelu = jnp.tanh(0.7978845608028654 * (gate + 0.044715 * gate ** 3)) * gate * 0.5 + gate * 0.5
        inter = gelu * up
        out = jnp.einsum('tn,hn->th', inter, Wd)
        return out.reshape(B, S, H)

    def _L1_attn_ref(u, W_in, W_conv, b_conv, dt_bias, A_log, D, norm_w, W_out):
        import jax, jax.numpy as jnp
        import numpy as np
        from jax import lax
        D_MODEL = 256
        D_STATE = 64
        D_CONV = 4
        EXPAND = 2
        HEADDIM = 128
        NGROUPS = 1
        CHUNK = 32
        D_INNER = EXPAND * D_MODEL
        NHEADS = D_INNER // HEADDIM
        D_IN_PROJ = 2 * D_INNER + 2 * NGROUPS * D_STATE + NHEADS
        CONV_DIM = D_INNER + 2 * NGROUPS * D_STATE
        EPS = 1e-05

        def segsum(x):
            T = x.shape[-1]
            xr = jnp.broadcast_to(x[..., :, None], x.shape + (T,))
            mask_lo = jnp.tril(jnp.ones((T, T), bool), -1)
            xr = jnp.where(mask_lo, xr, 0.0)
            seg = jnp.cumsum(xr, axis=-2)
            mask = jnp.tril(jnp.ones((T, T), bool), 0)
            return jnp.where(mask, seg, -jnp.inf)

        def ssd_minimal_discrete(X, A, B, C, block_len):
            b, L, h, p = X.shape
            n = B.shape[-1]
            c = L // block_len
            X = X.reshape(b, c, block_len, h, p)
            B = B.reshape(b, c, block_len, h, n)
            C = C.reshape(b, c, block_len, h, n)
            A = A.reshape(b, c, block_len, h).transpose(0, 3, 1, 2)
            A_cumsum = jnp.cumsum(A, axis=-1)
            Lmat = jnp.exp(segsum(A))
            Y_diag = jnp.einsum('bclhn,bcshn,bhcls,bcshp->bclhp', C, B, Lmat, X)
            decay_states = jnp.exp(A_cumsum[:, :, :, -1:] - A_cumsum)
            states = jnp.einsum('bclhn,bhcl,bclhp->bchpn', B, decay_states, X)
            init = jnp.zeros_like(states[:, :1])
            states = jnp.concatenate([init, states], axis=1)
            A_last = jnp.pad(A_cumsum[:, :, :, -1], ((0, 0), (0, 0), (1, 0)))
            decay_chunk = jnp.exp(segsum(A_last))
            new_states = jnp.einsum('bhzc,bchpn->bzhpn', decay_chunk, states)
            states, final_state = (new_states[:, :-1], new_states[:, -1])
            state_decay_out = jnp.exp(A_cumsum)
            Y_off = jnp.einsum('bclhn,bchpn,bhcl->bclhp', C, states, state_decay_out)
            Y = (Y_diag + Y_off).reshape(b, L, h, p)
            return (Y, final_state)
        b, L, _ = u.shape
        zxbcdt = u @ W_in.T
        z = zxbcdt[..., :D_INNER]
        xBC = zxbcdt[..., D_INNER:D_INNER + CONV_DIM]
        dt = zxbcdt[..., D_INNER + CONV_DIM:]
        dt = jax.nn.softplus(dt + dt_bias)
        xc = lax.conv_general_dilated(xBC.transpose(0, 2, 1), W_conv, (1,), [(D_CONV - 1, 0)], dimension_numbers=('NCH', 'OIH', 'NCH'), feature_group_count=CONV_DIM)
        xBC = jax.nn.silu((xc + b_conv[None, :, None]).transpose(0, 2, 1))
        x = xBC[..., :D_INNER].reshape(b, L, NHEADS, HEADDIM)
        Bm = xBC[..., D_INNER:D_INNER + NGROUPS * D_STATE]
        Cm = xBC[..., D_INNER + NGROUPS * D_STATE:]
        Bm = jnp.broadcast_to(Bm.reshape(b, L, NGROUPS, D_STATE), (b, L, NHEADS, D_STATE))
        Cm = jnp.broadcast_to(Cm.reshape(b, L, NGROUPS, D_STATE), (b, L, NHEADS, D_STATE))
        A = -jnp.exp(A_log)
        x_scaled = x * dt[..., None]
        A_dt = A[None, None, :] * dt
        Y, _final = ssd_minimal_discrete(x_scaled, A_dt, Bm, Cm, CHUNK)
        y = Y + x * D[None, None, :, None]
        y = y.reshape(b, L, D_INNER)
        g = y * jax.nn.silu(z)
        y = g * lax.rsqrt(jnp.mean(g * g, axis=-1, keepdims=True) + EPS) * norm_w
        return y @ W_out.T

    def _L1_ffn_ref(x, w_gate, w_up, w_down):
        import jax, jax.numpy as jnp
        import numpy as np

        def _sparsify_2to4(h):
            B, S, I = h.shape
            g = h.reshape(B, S, I // 4, 4)
            a = jnp.abs(g)
            _, idx = jax.lax.top_k(a, 2)
            pos = jnp.arange(4)
            mask = (pos == idx[..., 0:1]) | (pos == idx[..., 1:2])
            return (g * mask.astype(g.dtype)).reshape(B, S, I)
        h = jax.nn.silu(jnp.einsum('bsh,hi->bsi', x, w_gate)) * jnp.einsum('bsh,hi->bsi', x, w_up)
        h_sparse = _sparsify_2to4(h)
        return jnp.einsum('bsi,ih->bsh', h_sparse, w_down)
    x = L0_attn_x
    x = _layernorm(x + _L0_attn_ref(x), axis=-1)
    x = _layernorm(x + _L0_ffn_ref(x, L0_ffn_gate_W_packed, L0_ffn_gate_scales, L0_ffn_up_W_packed, L0_ffn_up_scales, L0_ffn_down_W_packed, L0_ffn_down_scales), axis=-1)
    x = _layernorm(x + _L1_attn_ref(x, L1_attn_W_in, L1_attn_W_conv, L1_attn_b_conv, L1_attn_dt_bias, L1_attn_A_log, L1_attn_D, L1_attn_norm_w, L1_attn_W_out), axis=-1)
    x = _layernorm(x + _L1_ffn_ref(x, L1_ffn_w_gate, L1_ffn_w_up, L1_ffn_w_down), axis=-1)
    return x

_drawn_inputs = setup_inputs


def setup_inputs(seed=0):
    import zlib

    import numpy as np

    out = dict(_drawn_inputs(seed))
    spreads = {'L1_attn_b_conv': (0.0, 0.1), 'L1_attn_D': (1.0, 0.2), 'L1_attn_norm_w': (1.0, 0.2)}
    factors = {'L1_attn_dt_bias': 3.426, 'L1_attn_A_log': 8.0}
    for name, (base, spread) in spreads.items():
        noise = np.random.default_rng([zlib.crc32(name.encode()), seed]).standard_normal(out[name].shape)
        drawn = base * np.exp(spread * noise) if base else spread * noise
        out[name] = jnp.asarray(drawn.astype(out[name].dtype))
    for name, factor in factors.items():
        out[name] = (out[name] * factor).astype(out[name].dtype)
    return out
```

```python
from contextlib import ExitStack

import concourse.bass as bass
from concourse import mybir

ALU = mybir.AluOpType
ACT = mybir.ActivationFunctionType
F32 = mybir.dt.float32
F32R = mybir.dt.float32r
BF16 = mybir.dt.bfloat16
I32 = mybir.dt.int32
AX_X = mybir.AxisListType.X

P = 128
BATCH, SEQ, H = 2, 2048, 256
T = BATCH * SEQ
TOK = 512
NT = TOK // P
GROUPS = T // TOK
GPB = GROUPS // BATCH
KT = H // P
EPS = 1e-5

MLP0 = 2048
NB0 = MLP0 // P
JOBS = 12

D_INNER, D_STATE, HEADS, HEADDIM, TAPS = 512, 64, 4, 128, 4
CONV_DIM = D_INNER + 2 * D_STATE
D_IN = 2 * D_INNER + 2 * D_STATE + HEADS
XB = CONV_DIM // P

MLP1 = 1024
RANK = 4
MB = MLP1 // RANK // P
DT_STEPS = 11
DT0, XBC0, Z0, ACS0, SEG0 = 2, 3, 8, 12, 13
RES = 4
W1_PIECE = 3 * KT * MLP1 // GROUPS


def exact3(pe, out, w_hi, w_lo, m_hi, m_lo, start, stop, **kw):
    pe.matmul(out, w_hi, m_lo, start=start, stop=False, **kw)
    pe.matmul(out, w_lo, m_hi, start=False, stop=False, **kw)
    return pe.matmul(out, w_hi, m_hi, start=False, stop=stop, **kw)


def build(nc, x_in, codes, scales, w_in, conv_w, conv_b, dt_bias, a_log, d_skip, norm_w, w_out, w_mlp1, out):
    ctx = ExitStack()
    with ctx:
        def sb(name, shape, dt, stack=ctx):
            return stack.enter_context(nc.sbuf_tensor(name, shape, dt))

        def sem(name):
            return ctx.enter_context(nc.semaphore(name))

        x2_dram = nc.dram_tensor("x2_scratch", (T, H), F32, kind="Internal").ap()
        x3_dram = nc.dram_tensor("x3_scratch", (T, H), F32, kind="Internal").ap()

        bank = [ctx.enter_context(nc.psum_tensor(f"bank{i}", [P, 512], F32)) for i in range(8)]
        ps_gate, ps_up, ps_down, ps_t = bank[0:2], bank[2:4], bank[4:6], bank[6:8]
        small, ps_x, ps_y, ps_yoff, ps_ds, ps_g = bank[2:8]

        def ring(i):
            return bank[i % 2]

        wide_i = sb("wide_i", [P, 3 * P], F32)
        ident = wide_i[:, P:2 * P]
        zero_bf = sb("zero_bf", [P, 512], BF16)
        m_half = sb("m_half", [P, NT], F32)
        eps4 = sb("eps4", [P, NT], F32)

        upto = sb("upto", [P, P], F32)
        below = sb("below", [P, P], F32)
        ones = sb("ones", [P, D_STATE], F32)
        eps_rms = sb("eps_rms", [P, 1], F32)
        cw = sb("cw", [P, XB, TAPS], F32)
        cb = sb("cb", [P, XB], F32)
        dtb = sb("dtb", [P, HEADS], F32)
        a4 = sb("a4", [P, HEADS], F32)
        d4 = sb("d4", [P, HEADS], F32)
        nw = sb("nw", [P, HEADS], F32)

        win_h = sb("win_h", [P, KT, D_IN], F32R)
        win_l = sb("win_l", [P, KT, D_IN], F32R)
        wo_h = sb("wo_h", [P, HEADS, H], F32R)
        wo_l = sb("wo_l", [P, HEADS, H], F32R)

        xg = sb("xg", [P, 2, NT, H], F32)
        xt_h = sb("xt_h", [P, KT, TOK], F32R)
        xt_l = sb("xt_l", [P, KT, TOK], F32R)
        st6 = sb("st6", [P, NT, 6], F32)
        mv = sb("mv", [P, NT, 2], F32)
        ve = sb("ve", [P, NT], F32)
        rstd = sb("rstd", [P, NT], F32)
        st6b = sb("st6b", [P, NT, 6], F32)
        mvb = sb("mvb", [P, NT, 2], F32)
        veb = sb("veb", [P, NT], F32)
        rstdb = sb("rstdb", [P, NT], F32)

        mlp0 = ExitStack()
        w0_hi = sb("w0_hi", [P, JOBS, 2, 512], F32R, mlp0)
        w0_lo = sb("w0_lo", [P, JOBS, 2, 512], F32R, mlp0)
        soft_wt = sb("soft_wt", [P, BATCH, 2, KT * H], F32R, mlp0)
        win_raw = sb("win_raw", [P, KT, D_IN], F32, mlp0)
        wo_raw = sb("wo_raw", [P, HEADS, H], F32, mlp0)
        phase_a = ExitStack()
        xs = sb("xs", [P, 2, NT, 2 * H], F32R, phase_a)
        wq = sb("wq", [P, 2, 512], I32, phase_a)
        sc = sb("sc", [P, 2, 512], F32, phase_a)
        sgn = sb("sgn", [P, 2, 512], I32, phase_a)
        mag = sb("mag", [P, 2, 512], I32, phase_a)
        wf = sb("wf", [P, 2, 2, 512], F32, phase_a)
        s_hl = sb("s_hl", [P, 2, H], F32, phase_a)
        s_full = sb("s_full", [P, 2, H], F32, phase_a)
        nmax = sb("nmax", [P, 2], F32, phase_a)
        rsum = sb("rsum", [P, 2], F32, phase_a)
        rinv = sb("rinv", [P, 2], F32, phase_a)
        phase_a.close()

        phase_b = ExitStack()
        x1 = sb("x1", [P, NT, H], F32, phase_b)
        x1_res = sb("x1_res", [P, NT, H], F32, phase_b)
        at_h = sb("at_h", [P, KT, TOK], F32R, phase_b)
        at_l = sb("at_l", [P, KT, TOK], F32R, phase_b)
        gl = sb("gl", [P, 2, TOK], F32, phase_b)
        hb = sb("hb", [P, 2, TOK], F32, phase_b)
        hh = sb("hh", [P, 2, TOK], F32R, phase_b)
        hl = sb("hl", [P, 2, TOK], F32R, phase_b)
        yb = sb("yb", [P, NT, H], F32, phase_b)
        xo = sb("xo", [P, NT, H], F32, phase_b)
        phase_b.close()
        mlp0.close()

        w1_h = sb("w1_h", [P, GROUPS, W1_PIECE], F32R)
        w1_l = sb("w1_l", [P, GROUPS, W1_PIECE], F32R)
        phase_c = ExitStack()

        def cs(name, shape, dt=F32):
            return sb(name, shape, dt, phase_c)

        w1_raw = cs("w1_raw", [P, 2, W1_PIECE])
        raw = cs("raw", [P, XB, TAPS - 1 + TOK])
        tail = cs("tail", [P, BATCH, XB, TAPS - 1])
        acc = cs("acc", [P, 2, TOK])
        xc = cs("xc", [P, 2, HEADS, TOK])
        bc = cs("bc", [P, 2, TOK])
        ct = cs("ct", [D_STATE, 2, TOK])
        zs = cs("zs", [P, NT, D_INNER])
        ee = cs("ee", [P, NT, HEADS, P])
        d0 = cs("d0", [P, NT, HEADS])
        dax = cs("dax", [P, NT * HEADS])
        de = cs("de", [P, NT * HEADS])
        du = cs("du", [P, NT * HEADS])
        dl = cs("dl", [P, NT * HEADS])
        um = cs("um", [P, NT * HEADS])
        dl2 = cs("dl2", [P, NT * HEADS])
        drec = cs("drec", [P, NT * HEADS])
        dm1 = cs("dm1", [P, NT * HEADS])
        dm2 = cs("dm2", [P, NT * HEADS])
        dden = cs("dden", [P, NT * HEADS])
        dtv = cs("dtv", [P, 2, NT, HEADS])
        adt = cs("adt", [P, NT, HEADS])
        ea = cs("ea", [P, 2, NT, HEADS])
        et = cs("et", [D_STATE, 2, NT, HEADS])
        au = cs("au", [P, 2, HEADS, P])
        gm = cs("gm", [P, 2, P])
        mm_ = cs("mm_", [P, 2, HEADS, P])
        xtk = cs("xtk", [P, 2, HEADS, HEADDIM])
        btk = cs("btk", [P, 2, D_STATE])
        xsd = cs("xsd", [P, 2, HEADS, HEADDIM])
        xdc = cs("xdc", [P, 2, HEADS, HEADDIM])
        xd = cs("xd", [P, 2, HEADS, HEADDIM])
        yo = cs("yo", [P, 2, HEADS, HEADDIM])
        gg = cs("gg", [P, 2, D_INNER])
        ss = cs("ss", [P, 2])
        rr = cs("rr", [P, 2])
        gt_h = cs("gt_h", [P, 2, HEADS, P], F32R)
        gt_l = cs("gt_l", [P, 2, HEADS, P], F32R)
        state = cs("state", [D_STATE, BATCH, HEADS, HEADDIM])
        y3 = cs("y3", [P, NT, H])
        phase_c.close()

        phase_d = ExitStack()

        def ds(name, shape, dt=F32):
            return sb(name, shape, dt, phase_d)

        dt_h = ds("dt_h", [P, KT, TOK], F32R)
        dt_l = ds("dt_l", [P, KT, TOK], F32R)
        dg = ds("dg", [P, 2, TOK])
        dh = ds("dh", [P, MB, RANK, TOK])
        dab = ds("dab", [P, MB, RANK, TOK])
        beats = ds("beats", [P, 6, TOK], BF16)
        rank = ds("rank", [P, RANK, TOK], BF16)
        dhh = ds("dhh", [P, MB, RANK, TOK], F32R)
        dhl = ds("dhl", [P, MB, RANK, TOK], F32R)
        dy = ds("dy", [P, NT, H])
        res = ds("res", [P, RES, NT, H])
        phase_d.close()

        s_const = sem("constants_ready")
        s_x = [sem(f"x_loaded{i}") for i in range(2)]
        s_w = [sem(f"codes_loaded{i}") for i in range(2)]
        s_xs_free = sem("xs_free")
        s_xs_hi = sem("xs_hi_ready")
        s_xs_lo = sem("xs_lo_ready")
        s_sc_mm = sem("scores_done")
        s_sc_free = sem("scores_psum_free")
        s_sm = sem("softmax_steps_dve")
        s_sma = sem("softmax_steps_act")
        s_smt = sem("softmax_transposed")
        s_deq = sem("dequant_steps_dve")
        s_wf = sem("weights_f32_ready")
        s_whi = sem("weights_hi_ready")
        s_wlo = sem("weights_lo_ready")
        s_xg = sem("front_x_loaded")
        s_xt_t = sem("x_transposed")
        s_xt_hi = sem("xt_hi_ready")
        s_xt_lo = sem("xt_lo_ready")
        s_ctx = sem("context_done")
        s_seen = sem("stats_seen")
        s_ln1 = sem("ln1_stats")
        s_ln1r = sem("ln1_rstd")
        s_x1 = sem("x1_ready")
        s_x1r = sem("x1_residual_kept")
        s_at_t = sem("x1_transposed")
        s_at_hi = sem("at_hi_ready")
        s_at_lo = sem("at_lo_ready")
        s_gate = sem("gate_done")
        s_up = sem("up_done")
        s_gelu = sem("gelu_done")
        s_h = sem("h_ready")
        s_hhi = sem("h_hi_ready")
        s_hlo = sem("h_lo_ready")
        s_down = sem("down_done")
        s_y = sem("y_ready")
        s_ln2 = sem("ln2_stats")
        s_ln2r = sem("ln2_rstd")
        s_x2 = sem("x2_ready")
        s_x2st = sem("x2_stored")
        c_wc_raw = sem("ssm_weights_loaded")
        c_wch = sem("ssm_weights_hi")
        c_wcs = sem("ssm_weights_scaled")
        c_small = sem("ssm_constants_loaded")
        c_a4 = sem("decay_rate_ready")
        c_t = sem("x2_transposed")
        c_xth = sem("x2t_hi_ready")
        c_xtl = sem("x2t_lo_ready")
        c_dtp = sem("dt_projected")
        c_dtc = sem("dt_steps_dve")
        c_dta = sem("dt_steps_act")
        c_acs = sem("decay_sums_done")
        c_ea = sem("decays_ready")
        c_au = sem("masked_decay_ready")
        c_seg = sem("segment_sums_done")
        c_e = sem("segment_decay_ready")
        c_zp = sem("z_projected")
        c_zs = sem("z_gate_ready")
        c_xbc = sem("xbc_projected")
        c_xin = sem("xbc_copied")
        c_halo = sem("halo_copied")
        c_cv = sem("conv_steps")
        c_silu = sem("conv_silu_ready")
        c_ct = sem("c_moved")
        c_w1h = sem("mlp1_hi_ready")
        c_w1l = sem("mlp1_lo_ready")
        c_tr = sem("x_token_major")
        c_btk = sem("b_tok_ready")
        c_G = sem("cb_done")
        c_gm = sem("cb_masked")
        c_m = sem("mixing_ready")
        c_xtk = sem("x_tok_ready")
        c_xsd = sem("x_dt_ready")
        c_xdc = sem("x_decayed_ready")
        c_xd = sem("x_skip_ready")
        c_yoff = sem("y_off_done")
        c_y = sem("y_diag_done")
        c_ds = sem("state_add_done")
        c_st = sem("state_ready")
        c_yo = sem("y_off_scaled")
        c_yo2 = sem("y_off_skip_ready")
        c_g1 = sem("y_ready_ssm")
        c_g = sem("g_ready")
        c_ss = sem("g_square_sum")
        c_rr = sem("g_inv_rms")
        c_gT = sem("g_transposed")
        c_gth = sem("gt_hi_ready")
        c_gtl = sem("gt_lo_ready")
        c_o = sem("projected_out")
        c_y3 = sem("y3_ready")
        c_ln3 = sem("ln3_stats")
        c_ln3r = sem("ln3_rstd")
        c_x3 = sem("x3_ready")
        c_x3st = sem("x3_stored")
        c_xg = [sem(f"x2_loaded{i}") for i in range(2)]
        c_w1r = [sem(f"mlp1_piece_loaded{i}") for i in range(2)]
        c_init = sem("ssm_memory_cleared")
        d_x = sem("x3_loaded")
        d_res = sem("x3_residual_kept")
        d_t = sem("x3_transposed")
        d_th = sem("x3t_hi_ready")
        d_tl = sem("x3t_lo_ready")
        d_gate = sem("mlp1_gate_done")
        d_up = sem("mlp1_up_done")
        d_silu = sem("mlp1_silu_ready")
        d_mul = sem("mlp1_gated_ready")
        d_abs = sem("mlp1_abs_ready")
        d_cmp = sem("pairs_compared")
        d_add = sem("ranks_dve")
        d_padd = sem("ranks_pool")
        d_sel = sem("kept_ready")
        d_hi = sem("kept_hi_ready")
        d_lo = sem("kept_lo_ready")
        d_down = sem("mlp1_down_done")
        d_y = sem("mlp1_sum_ready")
        d_ln = sem("ln4_stats")
        d_lnr = sem("ln4_rstd")
        d_out = sem("output_ready")
        d_st = sem("output_stored")

        block = ctx.enter_context(nc.Block())
        x_rows = x_in.rearrange("(g t p) c -> g p t c", p=P, t=NT)
        x2_rows = x2_dram.rearrange("(g t p) c -> g p t c", p=P, t=NT)
        x3_rows = x3_dram.rearrange("(g t p) c -> g p t c", p=P, t=NT)
        out_rows = out.rearrange("(g t p) c -> g p t c", p=P, t=NT)

        PAIRS = [(0, 0, 3), (1, 3, 2), (2, 5, 1)]
        KEEP = [(2.0, ALU.is_ge), (1.0, ALU.is_ge), (0.0, ALU.is_ge), (1.0, ALU.is_le)]

        def for_groups(eng, step):
            with eng.Fori(0, GPB - 1) as i:
                step(2 * i, 0, i, (2 * i + 1, 1, i))
                step(2 * i + 1, 1, i, (2 * i + 2, 0, i + 1))
            i = GPB - 1
            step(2 * i, 0, i, (2 * i + 1, 1, i))
            step(2 * i + 1, 1, i, None)

        FROM_1 = [s_y, c_xtk, c_gm, c_btk, c_yo, c_g1, c_ds, c_y3, c_ss, c_rr, c_yo2, d_y]
        FROM_16 = [s_x2st, c_x3st, d_st]

        @block.sync
        def _(sp):
            def load_x(f, u):
                sp.dma_start(xg[:, u], x_rows[f]).then_inc(s_x[u], 16)

            def load_codes(j, u):
                sp.dma_start(wq[:, u], codes[j]).then_inc(s_w[u], 16)
                for q in range(8):
                    sp.dma_start(sc[16 * q:16 * q + 16, u], scales[j, q:q + 1].broadcast_to([16, 512])).then_inc(s_w[u], 16)

            for s_ in FROM_1:
                sp.sem_inc(s_, 1)
            for s_ in FROM_16:
                sp.sem_inc(s_, 16)
            for u in range(2):
                load_x(u, u)
                load_codes(u, u)
            sp.dma_start(win_raw[:], w_in).then_inc(c_wc_raw, 16)
            sp.dma_start(wo_raw[:], w_out).then_inc(c_wc_raw, 16)
            for dst, src in ((cw[:], conv_w), (cb[:], conv_b), (nw[:], norm_w), (dtb[:], dt_bias.broadcast_to([P, HEADS])),
                             (a4[:], a_log.broadcast_to([P, HEADS])), (d4[:], d_skip.broadcast_to([P, HEADS]))):
                sp.dma_start(dst, src).then_inc(c_small, 16)
            with sp.Fori(0, GROUPS // 2 - 1) as h:
                for u in range(2):
                    sp.wait_ge(s_xs_lo, 2 * h + u + 1)
                    load_x(2 * h + u + 2, u)
                    sp.wait_ge(s_wf, 2 * (2 * h + u + 1))
                    load_codes(2 * h + u + 2, u)
            for j in range(GROUPS, JOBS):
                sp.wait_ge(s_wf, 2 * (j - 1))
                load_codes(j, j % 2)
            sp.wait_ge(s_xs_lo, GROUPS)
            sp.dma_start(xg[:, 0], x_rows[0]).then_inc(s_xg, 16)
            def load_front(g):
                sp.wait_ge(s_xt_t, KT * g)
                sp.dma_start(xg[:, 0], x_rows[g]).then_inc(s_xg, 16)

            def store_x2(g):
                sp.wait_ge(s_x2, NT * (g + 1))
                sp.dma_start(x2_rows[g], xo[:]).then_inc(s_x2st, 16)

            load_front(1)
            with sp.Fori(2, GROUPS) as g:
                load_front(g)
                store_x2(g - 2)
            store_x2(GROUPS - 2)
            store_x2(GROUPS - 1)
            sp.wait_ge(s_x2st, 16 * GROUPS + 16)

            for q in range(2):
                sp.dma_start(xg[:, q], x2_rows[q * GPB]).then_inc(c_xg[q], 16)
                sp.dma_start(w1_raw[:, q], w_mlp1[q]).then_inc(c_w1r[q], 16)

            def step(s, b, i, nxt):
                sp.wait_ge(c_w1l, s + 1)
                if not isinstance(i, int):
                    sp.dma_start(w1_raw[:, b], w_mlp1[s + 2]).then_inc(c_w1r[b], 16)
                sp.wait_ge(c_y3, NT * (s + 1) + 1)
                if not isinstance(i, int):
                    sp.dma_start(xg[:, b], x2_rows[b * GPB + i + 1]).then_inc(c_xg[b], 16)
                sp.wait_ge(c_x3, NT * (s + 1))
                sp.dma_start(x3_rows[b * GPB + i], y3[:]).then_inc(c_x3st, 16)

            for_groups(sp, step)
            sp.wait_ge(c_x3st, 16 * GROUPS + 16)

            sp.dma_start(xg[:, 0], x3_rows[0]).then_inc(d_x, 16)
            def load_x3(g):
                sp.wait_ge(d_t, KT * g)
                sp.wait_ge(d_res, g)
                sp.dma_start(xg[:, 0], x3_rows[g]).then_inc(d_x, 16)

            def store_out(g):
                sp.wait_ge(d_out, NT * (g + 1))
                sp.dma_start(out_rows[g], dy[:]).then_inc(d_st, 16)

            load_x3(1)
            with sp.Fori(2, GROUPS) as g:
                load_x3(g)
                store_out(g - 2)
            store_out(GROUPS - 2)
            store_out(GROUPS - 1)
            sp.wait_ge(d_st, 16 * GROUPS + 16)

        @block.gpsimd
        def _(pool):
            pool.memset(wide_i[:], 0.0).then_inc(s_const, 1)
            pool.memset(zero_bf[:], 0.0).then_inc(s_const, 1)
            pool.memset(m_half[:], -0.5).then_inc(s_const, 1)
            pool.memset(eps4[:], EPS).then_inc(s_const, 1)
            pool.memset(eps_rms[:], EPS * D_INNER).then_inc(s_const, 1)
            pool.memset(upto[:], 1.0).then_inc(s_const, 1)
            pool.memset(below[:], 1.0).then_inc(s_const, 1)
            pool.memset(ones[:], 1.0).then_inc(s_const, 1)
            pool.wait_ge(s_const, 8)
            pool.affine_select(out=ident, in_=ident, compare_op=ALU.not_equal, fill=1.0, base=0,
                               pattern=[[-1, P]], channel_multiplier=1).then_inc(s_const, 1)
            pool.affine_select(out=upto[:], in_=upto[:], compare_op=ALU.is_ge, fill=0.0, base=0,
                               pattern=[[1, P]], channel_multiplier=-1).then_inc(s_const, 1)
            pool.affine_select(out=below[:], in_=below[:], compare_op=ALU.is_gt, fill=0.0, base=0,
                               pattern=[[-1, P]], channel_multiplier=1).then_inc(s_const, 1)

            def weights_lo(j, u):
                for nib in range(2):
                    pool.wait_ge(s_whi, 2 * j + nib + 1)
                    pool.tensor_tensor(w0_lo[:, j, nib], wf[:, u, nib], w0_hi[:, j, nib].bitcast(F32),
                                       ALU.subtract).then_inc(s_wlo, 1)

            pool.sem_inc(s_wlo, 4)
            with pool.Fori(0, JOBS // 2) as h:
                for u in range(2):
                    weights_lo(2 * h + u, u)

            def inv_std(f, mv_, ve_, r_, s_in, s_out):
                pool.wait_ge(s_in, 2 * NT * (f + 1))
                pool.tensor_tensor(ve_[:], mv_[:, :, 1], eps4[:], ALU.add).then_inc(s_out, 1)
                pool.wait_ge(s_out, 2 * f + 1)
                pool.tensor_tensor(r_[:], ve_[:], m_half[:], ALU.pow).then_inc(s_out, 1)

            inv_std(0, mv, ve, rstd, s_ln1, s_ln1r)
            pool.wait_ge(c_wc_raw, 32)
            pool.wait_ge(c_small, 96)
            for k in range(HEADS):
                pool.tensor_scalar(wo_raw[:, k], wo_raw[:, k], nw[:, k:k + 1], float(D_INNER) ** 0.5, ALU.mult,
                                   ALU.mult).then_inc(c_wcs, 1)
            pool.tensor_copy(win_h[:], win_raw[:]).then_inc(c_wch, 1)
            pool.wait_ge(c_wcs, HEADS)
            pool.tensor_copy(wo_h[:], wo_raw[:]).then_inc(c_wch, 1)
            pool.wait_ge(c_wch, 2)
            pool.tensor_tensor(win_l[:], win_raw[:], win_h[:].bitcast(F32), ALU.subtract).then_inc(c_wch, 1)
            pool.tensor_tensor(wo_l[:], wo_raw[:], wo_h[:].bitcast(F32), ALU.subtract).then_inc(c_wch, 1)
            inv_std(1, mv, ve, rstd, s_ln1, s_ln1r)
            with pool.Fori(1, GROUPS - 1) as g:
                inv_std(g - 1, mvb, veb, rstdb, s_ln2, s_ln2r)
                inv_std(g + 1, mv, ve, rstd, s_ln1, s_ln1r)
            for g in (GROUPS - 2, GROUPS - 1):
                inv_std(g, mvb, veb, rstdb, s_ln2, s_ln2r)

            pool.wait_ge(s_x2st, 16 * GROUPS + 16)
            pool.memset(tail[:], 0.0).then_inc(c_init, 1)
            pool.memset(state[:], 0.0).then_inc(c_st, 1)

            def masked_decay(n):
                for t in range(NT):
                    if t == 0:
                        pool.wait_ge(c_dtc, DT_STEPS * (n + 1))
                        pool.wait_ge(c_seg, NT * n)
                    if t > 1:
                        pool.wait_ge(c_seg, NT * n + t - 1)
                    pool.tensor_tensor(au[:, t % 2], upto[:].unsqueeze(1).broadcast_to([P, HEADS, P]),
                                       adt[:, t].unsqueeze(2).broadcast_to([P, HEADS, P]), ALU.mult).then_inc(c_au, 1)

            def step(s, b, i, nxt):
                for c in range(NT):
                    k, u = NT * s + c, c % 2
                    pool.wait_ge(c_xtk, k + 1 + 1)
                    pool.wait_ge(c_yo2, k + 1)
                    pool.tensor_tensor(xd[:, u], xtk[:, u], d4[:].unsqueeze(2).broadcast_to([P, HEADS, P]),
                                       ALU.mult).then_inc(c_xd, 1)
                    if c == 2:
                        pool.wait_ge(c_w1h, s + 1)
                        pool.tensor_tensor(w1_l[:, s], w1_raw[:, b], w1_h[:, s].bitcast(F32), ALU.subtract).then_inc(c_w1l, 1)
                    pool.wait_ge(c_xsd, k + 1)
                    pool.wait_ge(c_ds, (k if c == 0 else k - 1) + 1)
                    pool.tensor_tensor(xdc[:, u], xsd[:, u], ee[:, c, :, P - 1:P].broadcast_to([P, HEADS, HEADDIM]),
                                       ALU.mult).then_inc(c_xdc, 1)
                    pool.wait_ge(c_yo, k + 1 + 1)
                    pool.wait_ge(c_xd, k + 1)
                    pool.wait_ge(c_g1, (k if c == 0 else k - 1) + 1)
                    pool.tensor_tensor(xd[:, u], yo[:, u], xd[:, u], ALU.add).then_inc(c_yo2, 1)
                    pool.wait_ge(c_ss, k + 1 + 1)
                    pool.wait_ge(c_y3, (k if c == 0 else k - 1) + 1)
                    pool.tensor_tensor(rr[:, u:u + 1], ss[:, u:u + 1], eps_rms[:], ALU.add).then_inc(c_rr, 1)
                    pool.wait_ge(c_rr, 2 * k + 1 + 1)
                    pool.tensor_tensor(rr[:, u:u + 1], rr[:, u:u + 1], m_half[:, 0:1], ALU.pow).then_inc(c_rr, 1)
                if nxt:
                    masked_decay(nxt[0])
                inv_std(s, mv, ve, rstd, c_ln3, c_ln3r)

            masked_decay(0)
            for_groups(pool, step)

            pool.wait_ge(c_x3st, 16 * GROUPS + 16)

            def ranks(m):
                pool.wait_ge(d_cmp, len(PAIRS) * (m + 1))
                pool.tensor_tensor(rank[:, 2], beats[:, 5], beats[:, 1], ALU.subtract).then_inc(d_padd, 1)
                pool.tensor_tensor(rank[:, 3], beats[:, 2], beats[:, 4], ALU.add).then_inc(d_padd, 1)
                pool.wait_ge(d_padd, 4 * m + 1)
                pool.tensor_tensor(rank[:, 2], rank[:, 2], beats[:, 3], ALU.subtract).then_inc(d_padd, 1)
                pool.wait_ge(d_padd, 4 * m + 2)
                pool.tensor_tensor(rank[:, 3], rank[:, 3], beats[:, 5], ALU.add).then_inc(d_padd, 1)

            def unit(m, mb):
                ranks(m)
                for r in range(RANK):
                    pool.wait_ge(d_hi, RANK * m + r + 1)
                    pool.tensor_tensor(dhl[:, mb, r], dab[:, mb, r], dhh[:, mb, r].bitcast(F32),
                                       ALU.subtract).then_inc(d_lo, 1)

            for m in range(3):
                unit(m, m % MB)
            with pool.Fori(2, GROUPS) as g:
                inv_std(g - 2, mv, ve, rstd, d_ln, d_lnr)
                unit(MB * g - 1, 1)
                unit(MB * g, 0)
            unit(MB * GROUPS - 1, 1)
            for g in (GROUPS - 2, GROUPS - 1):
                inv_std(g, mv, ve, rstd, d_ln, d_lnr)

        @block.scalar
        def _(act):
            def copy(dst, src):
                return act.activation(dst, src, ACT.Copy)

            def weights_hi(j, u):
                for nib in range(2):
                    act.wait_ge(s_wf, 2 * j + nib + 1)
                    copy(w0_hi[:, j, nib], wf[:, u, nib]).then_inc(s_whi, 1)

            for b in range(BATCH):
                with act.Fori(0, GPB // 2) as h:
                    for u in range(2):
                        f = GPB * b + 2 * h + u
                        act.wait_ge(s_x[u], 16 * (GPB // 2 * b + h + 1))
                        act.wait_ge(s_xs_free, f + 1)
                        copy(xs[:, u, :, 0:H], xg[:, u]).then_inc(s_xs_hi, 1)
                        weights_hi(f, u)
                act.wait_ge(s_sc_mm, b + 1)
                for i in range(2):
                    copy(s_hl[:, i], ps_gate[i][:, H:2 * H]).then_inc(s_sma, 1)
                act.wait_ge(s_sm, 6 * b + 4)
                for i in range(2):
                    act.activation(s_hl[:, i], s_full[:, i], ACT.Exp, bias=nmax[:, i:i + 1],
                                   accum_out=rsum[:, i:i + 1]).then_inc(s_sma, 1)
                act.wait_ge(s_smt, 2 * b + 2)
                copy(soft_wt[:, b, 0], ps_t[1][:]).then_inc(s_sma, 1)
            with act.Fori(GROUPS // 2, JOBS // 2) as h:
                for u in range(2):
                    weights_hi(2 * h + u, u)

            def x_hi(f, k):
                act.wait_ge(s_xt_t, KT * f + k + 1)
                act.wait_ge(s_ctx, NT * f)
                copy(xt_h[:, k], ps_t[k][:]).then_inc(s_xt_hi, 1)

            def a_hi(f, k):
                act.wait_ge(s_at_t, KT * f + k + 1)
                act.wait_ge(s_up, NB0 * f)
                copy(at_h[:, k], ps_t[k][:]).then_inc(s_at_hi, 1)

            def gelu(g, n):
                act.wait_ge(s_gate, NB0 * g + n + 1)
                act.activation(gl[:, n % 2], ps_gate[n % 2][:], ACT.Gelu_apprx_tanh).then_inc(s_gelu, 1)

            def h_hi(g, n):
                act.wait_ge(s_h, NB0 * g + n + 1)
                copy(hh[:, n % 2], hb[:, n % 2]).then_inc(s_hhi, 1)

            def keep_residual(g):
                act.wait_ge(s_y, NT * g + 1)
                act.wait_ge(s_x1, NT * (g + 1))
                copy(x1_res[:], x1[:]).then_inc(s_x1r, 1)

            def group(g, more):
                for n in range(NB0):
                    gelu(g, n)
                    if more and n == NB0 - 1:
                        a_hi(g + 1, 0)
                        a_hi(g + 1, 1)
                    h_hi(g, n)
                    if n == 4:
                        keep_residual(g)
                    if more and n == 2:
                        x_hi(g + 1, 0)
                        x_hi(g + 1, 1)

            for k in range(KT):
                x_hi(0, k)
            for k in range(KT):
                a_hi(0, k)
            with act.Fori(0, GROUPS - 1) as g:
                group(g, True)
            group(GROUPS - 1, False)

            act.wait_ge(s_x2st, 16 * GROUPS + 16)
            act.wait_ge(c_small, 96)
            act.activation(a4[:], a4[:], ACT.Exp).then_inc(c_a4, 1)
            act.wait_ge(c_init, 1)

            def xbc_in(n, b, j):
                act.wait_ge(c_xbc, XB * n + j + 1)
                act.wait_ge(c_silu, XB * n + max(j - 1, 0))
                copy(raw[:, j, TAPS - 1:], ring(XBC0 + j)[:])
                act.activation(acc[:, j % 2], ring(XBC0 + j)[:], ACT.Identity, bias=cb[:, j:j + 1],
                               scale=cw[:, j, TAPS - 1:TAPS]).then_inc(c_xin, 1)

            def conv_silu(n, b, j):
                act.wait_ge(c_cv, (TAPS - 1) * (XB * n + j + 1))
                act.activation(xc[:, b, j] if j < HEADS else bc[:, b], acc[:, j % 2], ACT.Silu).then_inc(c_silu, 1)

            def z_silu(n, b, t):
                act.wait_ge(c_zp, NT * n + t + 1)
                act.activation(zs[:, t], ring(Z0 + t)[:], ACT.Silu).then_inc(c_zs, 1)

            def project(slot, nxt):
                n, b, i = nxt
                if slot == 0:
                    act.wait_ge(c_cv, (TAPS - 1) * XB * n)
                    act.wait_ge(c_halo, 2 * n)
                    copy(raw[:, :, 0:TAPS - 1], tail[:, b]).then_inc(c_halo, 1)
                    for k in range(KT):
                        act.wait_ge(c_t, KT * n + k + 1)
                        copy(xt_h[:, k], ring(k)[:]).then_inc(c_xth, 1)
                    act.wait_ge(c_dtc, DT_STEPS * n + 2)
                    act.activation(de[:], dax[:], ACT.Exp).then_inc(c_dta, 1)
                    act.wait_ge(c_dtc, DT_STEPS * n + 3)
                    act.activation(dl[:], du[:], ACT.Ln).then_inc(c_dta, 1)
                if slot == 1:
                    xbc_in(n, b, 0)
                    xbc_in(n, b, 1)
                    conv_silu(n, b, 0)
                if slot == 2:
                    xbc_in(n, b, 2)
                    conv_silu(n, b, 1)
                    xbc_in(n, b, 3)
                    conv_silu(n, b, 2)
                if slot == 3:
                    xbc_in(n, b, 4)
                    conv_silu(n, b, 3)
                    act.wait_ge(c_xin, XB * (n + 1))
                    act.wait_ge(c_halo, 2 * n + 1)
                    copy(tail[:, b], raw[:, :, TOK:]).then_inc(c_halo, 1)
                    z_silu(n, b, 0)
                    conv_silu(n, b, 4)
                if slot == 4:
                    for t in range(1, NT):
                        z_silu(n, b, t)
                    act.wait_ge(c_acs, n + 1)
                    act.activation(ea[:, b].rearrange("p t h -> p (t h)"), ring(ACS0)[:, 0:16], ACT.Exp).then_inc(c_ea, 1)
                    act.activation(et[:, b].rearrange("p t h -> p (t h)"), ring(ACS0)[0:D_STATE, 16:32], ACT.Exp).then_inc(c_ea, 1)
                    act.wait_ge(c_ds, NT * n + 1)
                    for t in range(NT):
                        act.wait_ge(c_seg, NT * n + t + 1)
                        act.activation(ee[:, t].rearrange("p h l -> p (h l)"), ring(SEG0 + t)[:], ACT.Exp).then_inc(c_e, 1)

            def g_hi(k, u):
                act.wait_ge(c_gT, k + 1)
                copy(gt_h[:, u].rearrange("p h t -> p (h t)"), ps_g[:]).then_inc(c_gth, 1)

            def step(s, b, i, nxt):
                for c in range(NT):
                    k, u = NT * s + c, c % 2
                    act.wait_ge(c_tr, k + 1)
                    copy(xtk[:, u].rearrange("p h d -> p (h d)"), ps_x[:]).then_inc(c_xtk, 1)
                    if c == 1:
                        act.wait_ge(c_w1r[b], 16 * (i + 1))
                        copy(w1_h[:, s], w1_raw[:, b]).then_inc(c_w1h, 1)
                    if nxt:
                        project(c, nxt)
                    if c > 0:
                        g_hi(k - 1, 1 - u)
                    act.wait_ge(c_yoff, k + 1)
                    act.wait_ge(c_ea, 2 * (s + 1))
                    for h in range(HEADS):
                        y = act.activation(yo[:, u, h], ps_yoff[:, h * HEADDIM:(h + 1) * HEADDIM], ACT.Copy,
                                           scale=ea[:, b, c, h:h + 1])
                    y.then_inc(c_yo, 1)
                    act.wait_ge(c_g, k + 1)
                    act.wait_ge(c_ss, k + 1)
                    act.wait_ge(c_rr, 2 * k + 1)
                    act.activation(yo[:, u].rearrange("p h d -> p (h d)"), gg[:, u], ACT.Square, accum_out=ss[:, u:u + 1]).then_inc(c_ss, 1)
                g_hi(NT * s + NT - 1, 1)
                if nxt:
                    project(4, nxt)

            for j in range(5):
                project(j, (0, 0, 0))
            for_groups(act, step)

            act.wait_ge(c_x3st, 16 * GROUPS + 16)

            def keep_x3(g):
                act.wait_ge(d_x, 16 * (g + 1))
                copy(res[:, g & RES - 1], xg[:, 0]).then_inc(d_res, 1)

            def x3_hi(g):
                if not isinstance(g, int) or g > 0:
                    act.wait_ge(d_up, MB * RANK * g)
                for k in range(KT):
                    act.wait_ge(d_t, KT * g + k + 1)
                    copy(dt_h[:, k], ps_t[k][:]).then_inc(d_th, 1)

            def kept_hi(m, mb, r):
                act.wait_ge(d_sel, RANK * m + r + 1)
                copy(dhh[:, mb, r], dab[:, mb, r]).then_inc(d_hi, 1)

            def unit(m, mb, g, back, old, front=None):
                for r in range(RANK):
                    act.wait_ge(d_gate, RANK * m + r + 1)
                    act.activation(dg[:, r % 2], ps_gate[r % 2][:], ACT.Silu).then_inc(d_silu, 1)
                    if front is not None and r == RANK - 1:
                        x3_hi(front)
                    if back and r > 1:
                        kept_hi(m - 1, 1 - mb, 2 * r - 4)
                        kept_hi(m - 1, 1 - mb, 2 * r - 3)
                    act.wait_ge(d_mul, RANK * m + r + 1)
                    if old:
                        act.wait_ge(d_lo, RANK * (m - 2) + r + 1)
                    act.activation(dab[:, mb, r], dh[:, mb, r], ACT.Abs).then_inc(d_abs, 1)
                    if mb == 0 and r == 0:
                        keep_x3(g)

            def group(g, last=False):
                old = not isinstance(g, int) or g > 0
                unit(MB * g, 0, g, old, old)
                unit(MB * g + 1, 1, g, True, old, None if last else g + 1)

            x3_hi(0)
            group(0)
            group(1)
            with act.Fori(2, GROUPS - 1) as g:
                group(g)
            group(GROUPS - 1, last=True)
            for r in range(RANK):
                kept_hi(MB * GROUPS - 1, 1, r)

        @block.vector
        def _(dve):
            def dequant(j, u, q):
                dve.wait_ge(s_w[u], 144 * (q + 1))
                dve.wait_ge(s_wf, 2 * j)
                for nib in range(2):
                    dve.tensor_scalar(sgn[:, nib], wq[:, u], 28 - 4 * nib, -2 ** 31, ALU.logical_shift_left,
                                      ALU.bitwise_and).then_inc(s_deq, 1)
                    dve.tensor_scalar(mag[:, nib], wq[:, u], 22 - 4 * nib, 7 << 22, ALU.logical_shift_left,
                                      ALU.bitwise_and).then_inc(s_deq, 1)
                dve.wait_ge(s_deq, 5 * j + 4)
                dve.tensor_tensor(mag[:], mag[:], sgn[:], ALU.bitwise_or).then_inc(s_deq, 1)
                dve.wait_ge(s_deq, 5 * j + 5)
                for nib in range(2):
                    if nib == 0:
                        dve.wait_ge(s_wlo, 2 * j + 2)
                    dve.scalar_tensor_tensor(wf[:, u, nib], mag[:, nib].bitcast(F32), 2.0 ** 126, sc[:, u],
                                             ALU.mult, ALU.mult).then_inc(s_wf, 1)

            dve.wait_ge(s_const, 11)
            for b in range(BATCH):
                with dve.Fori(0, GPB // 2) as h:
                    for u in range(2):
                        f = GPB * b + 2 * h + u
                        dve.wait_ge(s_xs_hi, f + 1)
                        dve.tensor_tensor(xs[:, u, :, H:2 * H], xg[:, u], xs[:, u, :, 0:H].bitcast(F32),
                                          ALU.subtract).then_inc(s_xs_lo, 1)
                        dequant(f, u, GPB // 2 * b + h)
                for i in range(2):
                    dve.wait_ge(s_sma, 5 * b + i + 1)
                    dve.tensor_tensor(s_full[:, i], ps_gate[i][:, 0:H], s_hl[:, i], ALU.add).then_inc(s_sm, 1)
                dve.wait_ge(s_sm, 6 * b + 2)
                dve.wait_ge(s_smt, 2 * b + 1)
                sf = s_full[:].rearrange("p i j -> p (i j)")
                dve.tensor_tensor(sf, sf, ps_t[0][:], ALU.add).then_inc(s_sm, 1)
                dve.wait_ge(s_sm, 6 * b + 3)
                dve.tensor_reduce(nmax[:], s_full[:], AX_X, ALU.max, negate=True).then_inc(s_sm, 1)
                dve.wait_ge(s_sma, 5 * b + 4)
                dve.reciprocal(rinv[:], rsum[:]).then_inc(s_sm, 1)
                dve.wait_ge(s_sm, 6 * b + 5)
                for i in range(2):
                    w = dve.scalar_tensor_tensor(s_hl[:, i], s_hl[:, i], rinv[:, i:i + 1],
                                                 wide_i[:, P * (1 - i):P * (1 - i) + H], ALU.mult, ALU.add)
                w.then_inc(s_sm, 1)
                dve.wait_ge(s_sma, 5 * b + 5)
                dve.tensor_tensor(soft_wt[:, b, 1], ps_t[1][:], soft_wt[:, b, 0].bitcast(F32),
                                  ALU.subtract).then_inc(s_sc_free, 1)
            with dve.Fori(GROUPS // 2, JOBS // 2) as h:
                for u in range(2):
                    dequant(2 * h + u, u, h)

            def lo_part(dst, src, hi):
                return dve.tensor_tensor(dst, src, hi.bitcast(F32), ALU.subtract)

            def x_lo(f, k):
                dve.wait_ge(s_xt_hi, KT * f + k + 1)
                lo_part(xt_l[:, k], ps_t[k][:], xt_h[:, k]).then_inc(s_xt_lo, 1)

            def a_lo(f, k):
                dve.wait_ge(s_at_hi, KT * f + k + 1)
                lo_part(at_l[:, k], ps_t[k][:], at_h[:, k]).then_inc(s_at_lo, 1)

            def stats(f, src, st_, mv_, s_):
                for t in range(NT):
                    dve.bn_stats(st_[:, t], src[t]).then_inc(s_, 1)
                dve.wait_ge(s_, 2 * NT * f + NT)
                dve.sem_inc(s_seen, 1)
                for t in range(NT):
                    dve.bn_aggr(mv_[:, t], st_[:, t]).then_inc(s_, 1)

            ctx_tile = [ps_t[t // 2][:, t % 2 * H:t % 2 * H + H] for t in range(NT)]
            down_tile = [ps_down[t // 2][:, t % 2 * H:t % 2 * H + H] for t in range(NT)]

            def ln1_stats(f):
                dve.wait_ge(s_ctx, NT * (f + 1))
                stats(f, ctx_tile, st6, mv, s_ln1)

            def ln1_apply(f):
                dve.wait_ge(s_ln1r, 2 * (f + 1))
                if not isinstance(f, int) or f > 0:
                    dve.wait_ge(s_x1r, f)
                for t in range(NT):
                    dve.tensor_scalar(x1[:, t], ctx_tile[t], mv[:, t, 0:1], rstd[:, t:t + 1],
                                      ALU.subtract, ALU.mult).then_inc(s_x1, 1)

            def gated(g, n):
                dve.wait_ge(s_gelu, NB0 * g + n + 1)
                dve.wait_ge(s_up, NB0 * g + n + 1)
                dve.tensor_tensor(hb[:, n % 2], gl[:, n % 2], ps_up[n % 2][:], ALU.mult).then_inc(s_h, 1)

            def h_lo(g, n):
                dve.wait_ge(s_hhi, NB0 * g + n + 1)
                lo_part(hl[:, n % 2], hb[:, n % 2], hh[:, n % 2]).then_inc(s_hlo, 1)

            def add_x1(g):
                dve.wait_ge(s_down, g + 1)
                dve.wait_ge(s_x1r, g + 1)
                for t in range(NT):
                    dve.tensor_tensor(yb[:, t], down_tile[t], x1_res[:, t], ALU.add).then_inc(s_y, 1)

            def ln2_stats(g):
                dve.wait_ge(s_y, NT * (g + 1) + 1)
                stats(g, [yb[:, t] for t in range(NT)], st6b, mvb, s_ln2)

            def ln2_apply(g):
                dve.wait_ge(s_ln2r, 2 * (g + 1))
                dve.wait_ge(s_x2st, 16 * g + 16)
                for t in range(NT):
                    dve.tensor_scalar(xo[:, t], yb[:, t], mvb[:, t, 0:1], rstdb[:, t:t + 1],
                                      ALU.subtract, ALU.mult).then_inc(s_x2, 1)

            def group(g, before, more):
                for n in range(NB0):
                    gated(g, n)
                    if more and n == NB0 - 1:
                        a_lo(g + 1, 0)
                        a_lo(g + 1, 1)
                    h_lo(g, n)
                    if before and n == 0:
                        add_x1(g - 1)
                    if before and n == 1:
                        ln2_stats(g - 1)
                    if before and n == 3:
                        ln2_apply(g - 1)
                    if more and n == 2:
                        x_lo(g + 1, 0)
                        x_lo(g + 1, 1)
                    if more and n == 5:
                        ln1_stats(g + 1)
                    if more and n == 7:
                        ln1_apply(g + 1)

            for k in range(KT):
                x_lo(0, k)
            ln1_stats(0)
            ln1_apply(0)
            for k in range(KT):
                a_lo(0, k)
            group(0, False, True)
            with dve.Fori(1, GROUPS - 1) as g:
                group(g, True, True)
            group(GROUPS - 1, True, False)
            add_x1(GROUPS - 1)
            ln2_stats(GROUPS - 1)
            ln2_apply(GROUPS - 1)

            dve.wait_ge(s_x2st, 16 * GROUPS + 16)
            dve.wait_ge(c_small, 96)
            dve.wait_ge(c_a4, 1)

            def conv(n, b, j):
                dve.wait_ge(c_xin, XB * n + j + 1)
                dve.wait_ge(c_halo, 2 * n + 1)
                for tap in range(TAPS - 1):
                    steps = (TAPS - 1) * (XB * n + j) + tap
                    if tap > 0:
                        dve.wait_ge(c_cv, steps)
                    dve.scalar_tensor_tensor(acc[:, j % 2], raw[:, j, tap:tap + TOK], cw[:, j, tap:tap + 1],
                                             acc[:, j % 2], ALU.mult, ALU.add).then_inc(c_cv, 1)

            def dt_chain(n, b):
                def done(k, ins):
                    ins.then_inc(c_dtc, 1)
                    dve.wait_ge(c_dtc, DT_STEPS * n + k)

                flat = d0[:].rearrange("p t h -> p (t h)")
                dt_flat = dtv[:, b].rearrange("p t h -> p (t h)")
                dve.wait_ge(c_dtp, n + 1)
                done(1, dve.tensor_tensor(d0[:], ring(DT0)[:, 0:16].rearrange("p (t h) -> p t h", h=HEADS),
                                          dtb[:].unsqueeze(1).broadcast_to([P, NT, HEADS]), ALU.add))
                done(2, dve.scalar_tensor_tensor(dax[:], flat, -1.0, flat, ALU.mult, ALU.min))
                dve.wait_ge(c_dta, 2 * n + 1)
                done(3, dve.tensor_scalar(du[:], de[:], 1.0, None, ALU.add))
                done(4, dve.tensor_scalar(um[:], du[:], -1.0, None, ALU.add))
                done(5, dve.scalar_tensor_tensor(dden[:], um[:], 0.0, um[:], ALU.is_equal, ALU.add))
                done(6, dve.reciprocal(drec[:], dden[:]))
                done(7, dve.tensor_tensor(dm1[:], de[:], drec[:], ALU.mult))
                dve.wait_ge(c_dta, 2 * n + 2)
                done(8, dve.scalar_tensor_tensor(dl2[:], um[:], 0.0, dl[:], ALU.is_equal, ALU.add))
                done(9, dve.tensor_tensor(dm2[:], dm1[:], dl2[:], ALU.mult))
                done(10, dve.scalar_tensor_tensor(dt_flat, flat, 0.0, dm2[:], ALU.max, ALU.add))
                done(11, dve.scalar_tensor_tensor(adt[:], dtv[:, b], -1.0, a4[:].unsqueeze(1).broadcast_to([P, NT, HEADS]),
                                                  ALU.mult, ALU.mult))

            def project(slot, nxt):
                n, b, i = nxt
                if slot == 0:
                    for k in range(KT):
                        dve.wait_ge(c_xth, KT * n + k + 1)
                        lo_part(xt_l[:, k], ring(k)[:], xt_h[:, k]).then_inc(c_xtl, 1)
                    dt_chain(n, b)
                if slot in (1, 2):
                    conv(n, b, 2 * slot - 2)
                    conv(n, b, 2 * slot - 1)
                if slot == 3:
                    conv(n, b, 4)
                    dve.wait_ge(c_silu, XB * (n + 1))
                    dve.tensor_copy(ct[:, b], bc[D_STATE:2 * D_STATE, b]).then_inc(c_ct, 1)

            def g_lo(k, u):
                dve.wait_ge(c_gth, k + 1)
                lo_part(gt_l[:, u].rearrange("p h t -> p (h t)"), ps_g[:],
                        gt_h[:, u].rearrange("p h t -> p (h t)")).then_inc(c_gtl, 1)

            def add_out(s, b, k, c, u):
                dve.wait_ge(c_o, k + 1)
                dve.wait_ge(c_rr, 2 * (k + 1) + 1)
                if c == 0:
                    dve.wait_ge(c_x3st, 16 * s + 16)
                dve.scalar_tensor_tensor(y3[:, c], ps_g[:, 0:H], rr[:, u:u + 1], xg[:, b, c], ALU.mult,
                                         ALU.add).then_inc(c_y3, 1)

            def step(s, b, i, nxt):
                for c in range(NT):
                    k, u = NT * s + c, c % 2
                    dve.wait_ge(c_G, k + 1)
                    dve.tensor_tensor(gm[:, u], small[:, P:2 * P], upto[:], ALU.mult).then_inc(c_gm, 1)
                    dve.tensor_copy(btk[:, u], small[:, 0:D_STATE]).then_inc(c_btk, 1)
                    dve.wait_ge(c_gm, k + 1 + 1)
                    dve.wait_ge(c_e, k + 1)
                    dve.tensor_tensor(mm_[:, u], ee[:, c], gm[:, u].unsqueeze(1).broadcast_to([P, HEADS, P]),
                                      ALU.mult).then_inc(c_m, 1)
                    dve.wait_ge(c_xtk, k + 1 + 1)
                    dve.tensor_tensor(xsd[:, u], xtk[:, u], dtv[:, b, c].unsqueeze(2).broadcast_to([P, HEADS, HEADDIM]),
                                      ALU.mult).then_inc(c_xsd, 1)
                    if nxt:
                        project(c, nxt)
                    if c > 0:
                        g_lo(k - 1, 1 - u)
                    dve.wait_ge(c_ds, k + 1 + 1)
                    dve.wait_ge(c_ea, 2 * (s + 1))
                    dve.wait_ge(c_st, k + 1)
                    for h in range(HEADS):
                        st = dve.scalar_tensor_tensor(state[:, b, h], state[:, b, h], et[:, b, c, h:h + 1],
                                                      ps_ds[0:D_STATE, h * HEADDIM:(h + 1) * HEADDIM], ALU.mult, ALU.add)
                    st.then_inc(c_st, 1)
                    dve.wait_ge(c_y, k + 1)
                    dve.wait_ge(c_yo2, k + 1 + 1)
                    dve.tensor_tensor(gg[:, u], ps_y[:], xd[:, u].rearrange("p h d -> p (h d)"), ALU.add).then_inc(c_g1, 1)
                    dve.wait_ge(c_g1, k + 1 + 1)
                    dve.wait_ge(c_zs, k + 1)
                    dve.tensor_tensor(gg[:, u], gg[:, u], zs[:, c], ALU.mult).then_inc(c_g, 1)
                    if c > 0:
                        add_out(s, b, k - 1, c - 1, 1 - u)
                g_lo(NT * s + NT - 1, 1)
                add_out(s, b, NT * s + NT - 1, NT - 1, 1)
                dve.wait_ge(c_y3, NT * (s + 1) + 1)
                stats(s, [y3[:, t] for t in range(NT)], st6, mv, c_ln3)
                dve.wait_ge(c_ln3r, 2 * (s + 1))
                for t in range(NT):
                    dve.tensor_scalar(y3[:, t], y3[:, t], mv[:, t, 0:1], rstd[:, t:t + 1], ALU.subtract,
                                      ALU.mult).then_inc(c_x3, 1)

            for j in range(5):
                project(j, (0, 0, 0))
            for_groups(dve, step)

            dve.wait_ge(c_x3st, 16 * GROUPS + 16)

            def x3_lo(g):
                for k in range(KT):
                    dve.wait_ge(d_th, KT * g + k + 1)
                    lo_part(dt_l[:, k], ps_t[k][:], dt_h[:, k]).then_inc(d_tl, 1)

            def compare(m, mb, i):
                one, to, count = PAIRS[i]
                dve.wait_ge(d_abs, RANK * (m + 1))
                dve.tensor_tensor(beats[:, to:to + count], dab[:, mb, one:one + 1].broadcast_to([P, count, TOK]),
                                  dab[:, mb, one + 1:], ALU.is_ge).then_inc(d_cmp, 1)

            def add_ranks(m):
                dve.wait_ge(d_cmp, len(PAIRS) * (m + 1))
                dve.tensor_tensor(rank[:, 0:2], beats[:, 1:4:2], beats[:, 2:5:2], ALU.add).then_inc(d_add, 1)
                dve.wait_ge(d_add, 3 * m + 1)
                dve.tensor_tensor(rank[:, 0], rank[:, 0], beats[:, 0], ALU.add).then_inc(d_add, 1)
                dve.tensor_tensor(rank[:, 1], rank[:, 1], beats[:, 0], ALU.subtract).then_inc(d_add, 1)

            def keep(m, mb, r):
                if r < 2:
                    dve.wait_ge(d_add, 3 * m + 2 + r)
                else:
                    dve.wait_ge(d_padd, 4 * m + 1 + r)
                value, op = KEEP[r]
                dve.scalar_tensor_tensor(dab[:, mb, r], rank[:, r], value, dh[:, mb, r], op, ALU.mult).then_inc(d_sel, 1)

            def sparsify(m, mb, part):
                if part == 0:
                    compare(m, mb, 0)
                if part == 1:
                    compare(m, mb, 1)
                    compare(m, mb, 2)
                if part == 2:
                    add_ranks(m)
                    keep(m, mb, 0)
                    keep(m, mb, 1)
                if part == 3:
                    keep(m, mb, 2)
                    keep(m, mb, 3)

            def add_x3(g):
                dve.wait_ge(d_down, g + 1)
                if not isinstance(g, int) or g > 0:
                    dve.wait_ge(d_st, 16 * g + 16)
                for t in range(NT):
                    dve.tensor_tensor(dy[:, t], down_tile[t], res[:, g & RES - 1, t], ALU.add).then_inc(d_y, 1)

            def out_stats(g):
                dve.wait_ge(d_y, NT * (g + 1) + 1)
                stats(g, [dy[:, t] for t in range(NT)], st6, mv, d_ln)

            def normalise(g):
                dve.wait_ge(d_lnr, 2 * (g + 1))
                for t in range(NT):
                    dve.tensor_scalar(dy[:, t], dy[:, t], mv[:, t, 0:1], rstd[:, t:t + 1], ALU.subtract,
                                      ALU.mult).then_inc(d_out, 1)

            def unit(m, mb, back, done=None, front=None):
                for r in range(RANK):
                    if done is not None:
                        if r == 0:
                            add_x3(done)
                        if r == 1:
                            out_stats(done)
                        if r == 3:
                            normalise(done)
                    if back:
                        sparsify(m - 1, 1 - mb, r)
                    dve.wait_ge(d_silu, RANK * m + r + 1)
                    dve.wait_ge(d_up, RANK * m + r + 1)
                    dve.tensor_tensor(dh[:, mb, r], dg[:, r % 2], ps_up[r % 2][:], ALU.mult).then_inc(d_mul, 1)
                    if front is not None and r == RANK - 1:
                        x3_lo(front)

            x3_lo(0)
            for g in range(2):
                unit(MB * g, 0, g > 0)
                unit(MB * g + 1, 1, True, front=g + 1)
            with dve.Fori(2, GROUPS - 1) as g:
                unit(MB * g, 0, True, done=g - 2)
                unit(MB * g + 1, 1, True, front=g + 1)
            unit(MB * GROUPS - 2, 0, True, done=GROUPS - 3)
            unit(MB * GROUPS - 1, 1, True)
            add_x3(GROUPS - 2)
            for r in range(RANK):
                sparsify(MB * GROUPS - 1, 1, r)
            out_stats(GROUPS - 2)
            normalise(GROUPS - 2)
            add_x3(GROUPS - 1)
            out_stats(GROUPS - 1)
            normalise(GROUPS - 1)

        @block.tensor
        def _(pe):
            pe.wait_ge(s_const, 11)
            pe.sem_inc(s_xs_free, 2)
            for b in range(BATCH):
                if b > 0:
                    pe.wait_ge(s_sc_free, b)
                for i in range(2):
                    pe.matmul(ps_gate[i][:], zero_bf[:, 0:P], zero_bf[:], start=True, stop=False, skip_group_check=True)
                with pe.Fori(0, GPB // 2) as h:
                    for u in range(2):
                        f = GPB * b + 2 * h + u
                        pe.wait_ge(s_xs_lo, f + 1)
                        for t in range(NT):
                            for i in range(2):
                                mm = pe.matmul(ps_gate[i][:], xs[:, u, t, i * P:i * P + P], xs[:, u, t],
                                               start=False, stop=False, skip_group_check=True)
                        mm.then_inc(s_xs_free, 1)
                pe.matmul(ps_gate[0][:], zero_bf[:, 0:P], zero_bf[:], start=False, stop=True, skip_group_check=True)
                pe.matmul(ps_gate[1][:], zero_bf[:, 0:P], zero_bf[:], start=False, stop=True,
                          skip_group_check=True).then_inc(s_sc_mm, 1)
                pe.wait_ge(s_sma, 5 * b + 2)
                for i in range(2):
                    for k in range(KT):
                        mm = pe.transpose(ps_t[0][:, i * H + k * P:i * H + k * P + P], s_hl[:, k, i * P:i * P + P], ident)
                mm.then_inc(s_smt, 1)
                pe.wait_ge(s_sm, 6 * b + 6)
                for k in range(KT):
                    for i in range(2):
                        mm = pe.transpose(ps_t[1][:, k * H + i * P:k * H + i * P + P], s_hl[:, i, k * P:k * P + P], ident)
                mm.then_inc(s_smt, 1)
            pe.wait_ge(s_sc_free, BATCH)

            ctx_tile = [ps_t[t // 2][:, t % 2 * H:t % 2 * H + H] for t in range(NT)]
            down_tile = [ps_down[t // 2][:, t % 2 * H:t % 2 * H + H] for t in range(NT)]

            def x_transpose(f):
                pe.wait_ge(s_xg, 16 * (f + 1))
                pe.wait_ge(s_at_lo, KT * f)
                for k in range(KT):
                    for t in range(NT):
                        mm = pe.transpose(ps_t[k][:, t * P:t * P + P], xg[:, 0, t, k * P:k * P + P], ident)
                    mm.then_inc(s_xt_t, 1)

            def context(f, b):
                pe.wait_ge(s_xt_lo, KT * (f + 1))
                for t in range(NT):
                    for k in range(KT):
                        mm = exact3(pe, ctx_tile[t], xt_h[:, k, t * P:t * P + P], xt_l[:, k, t * P:t * P + P],
                                    soft_wt[:, b, 0, k * H:k * H + H], soft_wt[:, b, 1, k * H:k * H + H],
                                    start=k == 0, stop=k == KT - 1)
                    mm.then_inc(s_ctx, 1)

            def x1_transpose(f):
                pe.wait_ge(s_x1, NT * (f + 1))
                for k in range(KT):
                    for t in range(NT):
                        mm = pe.transpose(ps_t[k][:, t * P:t * P + P],
                                          x1[:, t].rearrange("p (m k) -> p k m", k=KT)[:, k], ident)
                    mm.then_inc(s_at_t, 1)

            def gate_or_up(ps, which, g, n):
                piece, col = 3 * (n // 4) + which, n % 4 * P
                for k in range(KT):
                    if which == 0 and n == 0:
                        pe.wait_ge(s_at_lo, KT * g + k + 1)
                    mm = exact3(pe, ps[n % 2][:], w0_hi[:, piece, k, col:col + P], w0_lo[:, piece, k, col:col + P],
                                at_h[:, k], at_l[:, k], start=k == 0, stop=k == KT - 1)
                return mm

            def down(g, n):
                pe.wait_ge(s_hlo, NB0 * g + n + 1)
                if n == 0:
                    pe.wait_ge(s_y, NT * g + 1)
                piece, nib, col = 3 * (n // 4) + 2, n % 2, n // 2 % 2 * H
                for t in range(NT):
                    mm = exact3(pe, down_tile[t], hh[:, n % 2, t * P:t * P + P], hl[:, n % 2, t * P:t * P + P],
                                w0_hi[:, piece, nib, col:col + H], w0_lo[:, piece, nib, col:col + H],
                                start=n == 0 and t % 2 == 0, stop=n == NB0 - 1, skip_group_check=True)
                if n == NB0 - 1:
                    mm.then_inc(s_down, 1)

            def group(g, before, more, b=0):
                for n in range(NB0):
                    if n > 1:
                        down(g, n - 2)
                    elif before:
                        down(g - 1, NB0 - 2 + n)
                    if n % 4 == 0:
                        pe.wait_ge(s_wlo, 6 * (n // 4 + 1) + 4)
                    gate_or_up(ps_gate, 0, g, n).then_inc(s_gate, 1)
                    gate_or_up(ps_up, 1, g, n).then_inc(s_up, 1)
                    if more and n == 1:
                        x_transpose(g + 1)
                    if more and n == 4:
                        context(g + 1, b)
                    if more and n == 9:
                        x1_transpose(g + 1)

            x_transpose(0)
            context(0, 0)
            x1_transpose(0)
            group(0, False, True)
            for b in range(BATCH):
                with pe.Fori(max(b * GPB, 1), (b + 1) * GPB - 1) as g:
                    group(g, True, True, b)
                if b < BATCH - 1:
                    group((b + 1) * GPB - 1, True, True, b + 1)
            group(GROUPS - 1, True, False)
            down(GROUPS - 1, NB0 - 2)
            down(GROUPS - 1, NB0 - 1)

            pe.wait_ge(c_wch, 4)
            pe.wait_ge(s_x2st, 16 * GROUPS + 16)

            def in_proj(n, b, first, j):
                cols = slice(D_INNER + j * P, D_INNER + (j + 1) * P)
                for k in range(KT):
                    mm = exact3(pe, ring(XBC0 + j)[:], win_h[:, k, cols], win_l[:, k, cols], xt_h[:, k], xt_l[:, k],
                                start=k == 0, stop=k == KT - 1)
                mm.then_inc(c_xbc, 1)

            def tok_proj(ps, t, cols):
                for k in range(KT):
                    mm = exact3(pe, ps, xt_h[:, k, t * P:(t + 1) * P], xt_l[:, k, t * P:(t + 1) * P],
                                win_h[:, k, cols], win_l[:, k, cols], start=k == 0, stop=k == KT - 1)
                return mm

            def z_proj(n, t):
                if t < 2:
                    pe.wait_ge(c_xin, XB * n + 4 + t)
                else:
                    pe.wait_ge(c_zs, NT * n + t - 1)
                tok_proj(ring(Z0 + t)[:], t, slice(0, D_INNER)).then_inc(c_zp, 1)

            def project(slot, nxt):
                n, b, i = nxt
                if slot == 0:
                    pe.wait_ge(c_xg[b], 16 * (i + 1))
                    pe.wait_ge(c_e, NT * n)
                    for k in range(KT):
                        for t in range(NT):
                            mm = pe.transpose(ring(k)[:, t * P:(t + 1) * P], xg[:, b, t, k * P:(k + 1) * P], ident)
                        mm.then_inc(c_t, 1)
                if slot == 1:
                    in_proj(n, b, False, 0)
                    pe.wait_ge(c_dtc, DT_STEPS * n + 1)
                    in_proj(n, b, False, 1)
                if slot in (2, 3):
                    for j in (2, 3) if slot == 2 else (4,):
                        pe.wait_ge(c_xin, XB * n + j - 1)
                        in_proj(n, b, False, j)
                if slot == 3:
                    z_proj(n, 0)
                if slot == 4:
                    for t in range(1, NT):
                        z_proj(n, t)
                    pe.wait_ge(c_zs, NT * n + 3)
                    pe.wait_ge(c_dtc, DT_STEPS * (n + 1))
                    flat = adt[:].rearrange("p t h -> p (t h)")
                    pe.matmul(ring(ACS0)[:, 0:16], upto[:], flat, start=True, stop=True)
                    pe.matmul(ring(ACS0)[0:D_STATE, 16:32], ones[:], flat, start=True, stop=True).then_inc(c_acs, 1)
                    for t in range(NT):
                        if t == 0:
                            pe.wait_ge(c_zs, NT * (n + 1))
                        elif t == 1:
                            pe.wait_ge(c_ea, 2 * (n + 1))
                        else:
                            pe.wait_ge(c_e, NT * n + t - 1)
                        pe.wait_ge(c_au, NT * n + t + 1)
                        pe.matmul(ring(SEG0 + t)[:], below[:], au[:, t % 2].rearrange("p h l -> p (h l)"),
                                  start=True, stop=True).then_inc(c_seg, 1)

            def dt_proj(nxt):
                n, b, i = nxt
                pe.wait_ge(c_xtl, KT * (n + 1))
                for t in range(NT):
                    mm = tok_proj(ring(DT0)[:, t * HEADS:(t + 1) * HEADS], t, slice(D_IN - HEADS, D_IN))
                mm.then_inc(c_dtp, 1)

            def g_transpose(k, u):
                pe.wait_ge(c_g, k + 1)
                pe.wait_ge(c_y3, k + 1)
                for h in range(HEADS):
                    mm = pe.transpose(ps_g[:, h * P:(h + 1) * P], gg[:, u, h * P:(h + 1) * P], ident)
                mm.then_inc(c_gT, 1)

            def out_proj(k, u):
                pe.wait_ge(c_gtl, k + 1)
                for h in range(HEADS):
                    mm = exact3(pe, ps_g[:, 0:H], gt_h[:, u, h], gt_l[:, u, h], wo_h[:, h], wo_l[:, h],
                                start=h == 0, stop=h == HEADS - 1)
                mm.then_inc(c_o, 1)

            def step(s, b, i, nxt):
                for c in range(NT):
                    k, u, cols = NT * s + c, c % 2, slice(c * P, (c + 1) * P)
                    if c == 0:
                        pe.wait_ge(c_silu, XB * (s + 1))
                        pe.wait_ge(c_ct, s + 1)
                    pe.wait_ge(c_xtk, k + 1)
                    for h in range(HEADS):
                        mm = pe.transpose(ps_x[:, h * P:(h + 1) * P], xc[:, b, h, cols], ident)
                    mm.then_inc(c_tr, 1)
                    pe.wait_ge(c_gm, k + 1)
                    pe.wait_ge(c_btk, k + 1)
                    pe.matmul(small[:, P:2 * P], bc[0:D_STATE, b, cols], ct[:, b, cols], start=True, stop=True)
                    pe.transpose(small[:, 0:D_STATE], bc[0:D_STATE, b, cols],
                                 wide_i[0:D_STATE, P:P + D_STATE]).then_inc(c_G, 1)
                    if nxt:
                        project(c, nxt)
                    if c > 0:
                        g_transpose(k - 1, 1 - u)
                    pe.wait_ge(c_st, k + 1)
                    pe.wait_ge(c_yo, k + 1)
                    pe.matmul(ps_yoff[:], ct[:, b, cols], state[:, b].rearrange("p h d -> p (h d)"),
                              start=True, stop=True).then_inc(c_yoff, 1)
                    pe.wait_ge(c_m, k + 1)
                    pe.wait_ge(c_xsd, k + 1)
                    pe.wait_ge(c_g1, k + 1)
                    for h in range(HEADS):
                        mm = pe.matmul(ps_y[:, h * HEADDIM:(h + 1) * HEADDIM], mm_[:, u, h], xsd[:, u, h],
                                       start=True, stop=True)
                    mm.then_inc(c_y, 1)
                    pe.wait_ge(c_xdc, k + 1)
                    pe.wait_ge(c_btk, k + 1 + 1)
                    pe.matmul(ps_ds[0:D_STATE, :], btk[:, u], xdc[:, u].rearrange("p h d -> p (h d)"),
                              start=True, stop=True).then_inc(c_ds, 1)
                    if nxt and c == 0:
                        dt_proj(nxt)
                    if c > 0:
                        out_proj(k - 1, 1 - u)
                g_transpose(NT * s + NT - 1, 1)
                out_proj(NT * s + NT - 1, 1)
                if nxt:
                    project(4, nxt)

            project(0, (0, 0, 0))
            dt_proj((0, 0, 0))
            for j in range(1, 5):
                project(j, (0, 0, 0))
            for_groups(pe, step)

            pe.wait_ge(c_x3st, 16 * GROUPS + 16)
            pe.wait_ge(c_w1l, GROUPS)
            w1h, w1l = (w[:].rearrange("p a b -> p (a b)") for w in (w1_h, w1_l))

            def x3_transpose(g):
                pe.wait_ge(d_x, 16 * (g + 1))
                pe.wait_ge(d_tl, KT * g)
                for k in range(KT):
                    for t in range(NT):
                        mm = pe.transpose(ps_t[k][:, t * P:(t + 1) * P], xg[:, 0, t, k * P:(k + 1) * P], ident)
                    mm.then_inc(d_t, 1)

            def down1(m, mb, r, g):
                pe.wait_ge(d_lo, RANK * m + r + 1)
                if mb == 0 and r == 0:
                    pe.wait_ge(d_y, NT * g + 1)
                at = 2 * KT * MLP1 + (mb * RANK + r) * H
                for t in range(NT):
                    mm = exact3(pe, down_tile[t], dhh[:, mb, r, t * P:(t + 1) * P], dhl[:, mb, r, t * P:(t + 1) * P],
                                w1h[:, at:at + H], w1l[:, at:at + H], start=mb == 0 and r == 0 and t % 2 == 0,
                                stop=mb == MB - 1 and r == RANK - 1, skip_group_check=True)
                if mb == MB - 1 and r == RANK - 1:
                    mm.then_inc(d_down, 1)

            def unit(m, mb, g, downs=True, front=None):
                for r in range(RANK):
                    if not isinstance(m, int) or m > 0 or r > 1:
                        pe.wait_ge(d_mul, RANK * m + r - 1)
                    for which, ps, s_ in ((0, ps_gate, d_gate), (1, ps_up, d_up)):
                        for k in range(KT):
                            if which == 0 and mb == 0 and r == 0:
                                pe.wait_ge(d_tl, KT * g + k + 1)
                            at = ((which * MB + mb) * RANK + r) * KT * P + k * P
                            mm = exact3(pe, ps[r % 2][:], w1h[:, at:at + P], w1l[:, at:at + P], dt_h[:, k], dt_l[:, k],
                                        start=k == 0, stop=k == KT - 1)
                        mm.then_inc(s_, 1)
                    if r == 1 and front is not None:
                        x3_transpose(front)
                    if downs:
                        down1(m - 2, mb, r, g - 1)

            x3_transpose(0)
            for m in range(2 * MB):
                unit(m, m % MB, m // MB, downs=m >= MB, front=m // MB + 1 if m % MB else None)
            with pe.Fori(2, GROUPS - 1) as g:
                unit(MB * g, 0, g)
                unit(MB * g + 1, 1, g, front=g + 1)
            unit(MB * GROUPS - 2, 0, GROUPS - 1)
            unit(MB * GROUPS - 1, 1, GROUPS - 1)
            for m in range(MB * GROUPS - 2, MB * GROUPS):
                for r in range(RANK):
                    down1(m, m % MB, r, GROUPS - 1)


_INS = ["x", "codes", "scales", "w_in", "conv_w", "conv_b", "dt_bias", "a_log", "d_skip", "norm_w", "w_out",
        "w_mlp1"]


def layout(i):
    import numpy as np

    def by_block(a):
        return a.reshape(a.shape[0], 8, P, 2).transpose(0, 1, 3, 2).reshape(a.shape[0], 4, 512)

    g, u = (by_block(i[f"L0_ffn_{n}_W_packed"].T) for n in ("gate", "up"))
    gs, us = (by_block(i[f"L0_ffn_{n}_scales"].T) for n in ("gate", "up"))
    d = i["L0_ffn_down_W_packed"].T.reshape(4, 2, P, H).transpose(2, 0, 1, 3).reshape(P, 4, 512)
    ds = i["L0_ffn_down_scales"].T.reshape(4, 2, 8, H).transpose(2, 0, 1, 3).reshape(8, 4, 512)
    return {
        "x": i["L0_attn_x"].reshape(T, H),
        "codes": np.stack([g, u, d], 2).reshape(P, JOBS, 512).transpose(1, 0, 2),
        "scales": np.stack([gs, us, ds], 2).reshape(8, JOBS, 512).transpose(1, 0, 2),
        "w_in": i["L1_attn_W_in"].T.reshape(KT, P, D_IN).transpose(1, 0, 2),
        "conv_w": i["L1_attn_W_conv"].reshape(XB, P, TAPS).transpose(1, 0, 2),
        "conv_b": i["L1_attn_b_conv"].reshape(XB, P).T,
        "dt_bias": i["L1_attn_dt_bias"].reshape(1, HEADS),
        "a_log": i["L1_attn_A_log"].reshape(1, HEADS),
        "d_skip": i["L1_attn_D"].reshape(1, HEADS),
        "norm_w": i["L1_attn_norm_w"].reshape(HEADS, HEADDIM).T,
        "w_out": i["L1_attn_W_out"].T.reshape(HEADS, HEADDIM, H).transpose(1, 0, 2),
        "w_mlp1": np.concatenate(
            [i[f"L1_ffn_w_{n}"].reshape(KT, P, MB, P, RANK).transpose(1, 2, 4, 0, 3).reshape(P, -1) for n in ("gate", "up")]
            + [i["L1_ffn_w_down"].reshape(MB, P, RANK, H).transpose(1, 0, 2, 3).reshape(P, -1)], 1)
        .reshape(P, GROUPS, -1).transpose(1, 0, 2),
    }


def kernel(**inputs):
    import numpy as np
    import concourse.bacc as bacc
    from concourse.bass_utils import run_bass_kernel_spmd

    nc = bacc.Bacc("TRN2", target_bir_lowering=False, num_devices=1)
    laid = layout({k: np.asarray(v) for k, v in inputs.items()})
    arrays, args = {}, []
    for name in _INS:
        a = np.ascontiguousarray(laid[name])
        arrays[f"in_{name}"] = a
        args.append(nc.dram_tensor(f"in_{name}", a.shape, mybir.dt.from_np(a.dtype), kind="ExternalInput").ap())
    args.append(nc.dram_tensor("out_0", (T, H), F32, kind="ExternalOutput").ap())
    build(nc, *args)
    r = run_bass_kernel_spmd(nc, [arrays], core_ids=[0])
    return r.results[0]["out_0"].reshape(BATCH, SEQ, H)
```

```python
from contextlib import ExitStack

import concourse.bass as bass
from concourse import mybir

ALU = mybir.AluOpType
ACT = mybir.ActivationFunctionType
F32 = mybir.dt.float32
F32R = mybir.dt.float32r
BF16 = mybir.dt.bfloat16
I32 = mybir.dt.int32
AX_X = mybir.AxisListType.X

P = 128
BATCH, SEQ, H = 2, 2048, 256
T = BATCH * SEQ
TOK = 512
NT = TOK // P
GROUPS = T // TOK
GPB = GROUPS // BATCH
KT = H // P
EPS = 1e-5

MLP0 = 2048
NB0 = MLP0 // P
JOBS = 12

D_INNER, D_STATE, HEADS, HEADDIM, TAPS = 512, 64, 4, 128, 4
CONV_DIM = D_INNER + 2 * D_STATE
D_IN = 2 * D_INNER + 2 * D_STATE + HEADS
XB = CONV_DIM // P

MLP1 = 1024
RANK = 4
MB = MLP1 // RANK // P
DT_STEPS = 11
DT0, XBC0, Z0, ACS0, SEG0 = 2, 3, 8, 10, 11
RES = 4
W1_PIECE = 3 * KT * MLP1 // GROUPS


def exact3(pe, out, w_hi, w_lo, m_hi, m_lo, start, stop, **kw):
    pe.matmul(out, w_hi, m_lo, start=start, stop=False, **kw)
    pe.matmul(out, w_lo, m_hi, start=False, stop=False, **kw)
    return pe.matmul(out, w_hi, m_hi, start=False, stop=stop, **kw)


def build(nc, x_in, codes, scales, w_in, conv_w, conv_b, dt_bias, a_log, d_skip, norm_w, w_out, w_mlp1, out):
    ctx = ExitStack()
    with ctx:
        def sb(name, shape, dt, stack=ctx):
            return stack.enter_context(nc.sbuf_tensor(name, shape, dt))

        def sem(name):
            return ctx.enter_context(nc.semaphore(name))

        x2_dram = nc.dram_tensor("x2_scratch", (T, H), F32, kind="Internal").ap()
        x3_dram = nc.dram_tensor("x3_scratch", (T, H), F32, kind="Internal").ap()

        bank = [ctx.enter_context(nc.psum_tensor(f"bank{i}", [P, 512], F32)) for i in range(8)]
        ps_gate, ps_up, ps_down, ps_t = bank[0:2], bank[2:4], bank[4:6], bank[6:8]
        small, ps_x, ps_y, ps_yoff, ps_ds, ps_g = bank[2:8]

        def ring(i):
            return bank[i % 2]

        def z_place(t):
            return ring((Z0, Z0 + 1, SEG0 + 4, SEG0 + 5)[t])

        wide_i = sb("wide_i", [P, 3 * P], F32)
        ident = wide_i[:, P:2 * P]
        zero_bf = sb("zero_bf", [P, 512], BF16)
        m_half = sb("m_half", [P, NT], F32)
        eps4 = sb("eps4", [P, NT], F32)

        upto = sb("upto", [P, P], F32)
        below = sb("below", [P, P], F32)
        ones = sb("ones", [P, D_STATE], F32)
        eps_rms = sb("eps_rms", [P, 1], F32)
        cw = sb("cw", [P, XB, TAPS], F32)
        cb = sb("cb", [P, XB], F32)
        dtb = sb("dtb", [P, HEADS], F32)
        a4 = sb("a4", [P, HEADS], F32)
        d4 = sb("d4", [P, HEADS], F32)
        nw = sb("nw", [P, HEADS], F32)

        win_h = sb("win_h", [P, KT, D_IN], F32R)
        win_l = sb("win_l", [P, KT, D_IN], F32R)
        wo_h = sb("wo_h", [P, HEADS, H], F32R)
        wo_l = sb("wo_l", [P, HEADS, H], F32R)

        xg = sb("xg", [P, 2, NT, H], F32)
        xt_h = sb("xt_h", [P, KT, TOK], F32R)
        xt_l = sb("xt_l", [P, KT, TOK], F32R)
        st6 = sb("st6", [P, NT, 6], F32)
        mv = sb("mv", [P, NT, 2], F32)
        ve = sb("ve", [P, NT], F32)
        rstd = sb("rstd", [P, NT], F32)
        st6b = sb("st6b", [P, NT, 6], F32)
        mvb = sb("mvb", [P, NT, 2], F32)
        veb = sb("veb", [P, NT], F32)
        rstdb = sb("rstdb", [P, NT], F32)

        mlp0 = ExitStack()
        w0_hi = sb("w0_hi", [P, JOBS, 2, 512], F32R, mlp0)
        w0_lo = sb("w0_lo", [P, JOBS, 2, 512], F32R, mlp0)
        soft_wt = sb("soft_wt", [P, BATCH, 2, KT * H], F32R, mlp0)
        win_raw = sb("win_raw", [P, KT, D_IN], F32, mlp0)
        wo_raw = sb("wo_raw", [P, HEADS, H], F32, mlp0)
        phase_a = ExitStack()
        xs = sb("xs", [P, 2, NT, 2 * H], F32R, phase_a)
        wq = sb("wq", [P, 2, 512], I32, phase_a)
        sc = sb("sc", [P, 2, 512], F32, phase_a)
        sgn = sb("sgn", [P, 2, 512], I32, phase_a)
        mag = sb("mag", [P, 2, 512], I32, phase_a)
        wf = sb("wf", [P, 2, 2, 512], F32, phase_a)
        s_hl = sb("s_hl", [P, 2, H], F32, phase_a)
        s_full = sb("s_full", [P, 2, H], F32, phase_a)
        nmax = sb("nmax", [P, 2], F32, phase_a)
        rsum = sb("rsum", [P, 2], F32, phase_a)
        rinv = sb("rinv", [P, 2], F32, phase_a)
        phase_a.close()

        phase_b = ExitStack()
        x1 = sb("x1", [P, NT, H], F32, phase_b)
        x1_res = sb("x1_res", [P, NT, H], F32, phase_b)
        at_h = sb("at_h", [P, KT, TOK], F32R, phase_b)
        at_l = sb("at_l", [P, KT, TOK], F32R, phase_b)
        gl = sb("gl", [P, 2, TOK], F32, phase_b)
        hb = sb("hb", [P, 2, TOK], F32, phase_b)
        hh = sb("hh", [P, 2, TOK], F32R, phase_b)
        hl = sb("hl", [P, 2, TOK], F32R, phase_b)
        yb = sb("yb", [P, NT, H], F32, phase_b)
        xo = sb("xo", [P, NT, H], F32, phase_b)
        phase_b.close()
        mlp0.close()

        w1_h = sb("w1_h", [P, GROUPS, W1_PIECE], F32R)
        w1_l = sb("w1_l", [P, GROUPS, W1_PIECE], F32R)
        phase_c = ExitStack()

        def cs(name, shape, dt=F32):
            return sb(name, shape, dt, phase_c)

        w1_raw = cs("w1_raw", [P, 2, W1_PIECE])
        raw = cs("raw", [P, XB, TAPS - 1 + TOK])
        tail = cs("tail", [P, BATCH, XB, TAPS - 1])
        acc = cs("acc", [P, 2, TOK])
        xc = cs("xc", [P, 2, HEADS, TOK])
        bc = cs("bc", [P, 2, TOK])
        ct = cs("ct", [D_STATE, 2, TOK])
        zs = cs("zs", [P, NT, D_INNER])
        ee = cs("ee", [P, NT, HEADS, P])
        d0 = cs("d0", [P, NT, HEADS])
        dax = cs("dax", [P, NT * HEADS])
        de = cs("de", [P, NT * HEADS])
        du = cs("du", [P, NT * HEADS])
        dl = cs("dl", [P, NT * HEADS])
        um = cs("um", [P, NT * HEADS])
        dl2 = cs("dl2", [P, NT * HEADS])
        drec = cs("drec", [P, NT * HEADS])
        dm1 = cs("dm1", [P, NT * HEADS])
        dm2 = cs("dm2", [P, NT * HEADS])
        dden = cs("dden", [P, NT * HEADS])
        dtv = cs("dtv", [P, 2, NT, HEADS])
        adt = cs("adt", [P, NT, HEADS])
        ea = cs("ea", [P, 2, NT, HEADS])
        et = cs("et", [D_STATE, 2, NT, HEADS])
        au = cs("au", [P, 2, HEADS, P])
        gm = cs("gm", [P, 2, P])
        mm_ = cs("mm_", [P, 2, HEADS, P])
        xtk = cs("xtk", [P, 2, HEADS, HEADDIM])
        btk = cs("btk", [P, 2, D_STATE])
        xsd = cs("xsd", [P, 2, HEADS, HEADDIM])
        xdc = cs("xdc", [P, 2, HEADS, HEADDIM])
        xd = cs("xd", [P, 2, HEADS, HEADDIM])
        yo = cs("yo", [P, 2, HEADS, HEADDIM])
        gg = cs("gg", [P, 2, D_INNER])
        ss = cs("ss", [P, 2])
        rr = cs("rr", [P, 2])
        gt_h = cs("gt_h", [P, 2, HEADS, P], F32R)
        gt_l = cs("gt_l", [P, 2, HEADS, P], F32R)
        state = cs("state", [D_STATE, BATCH, HEADS, HEADDIM])
        y3 = cs("y3", [P, NT, H])
        rest = cs("rest", [P, 2, H])
        phase_c.close()

        phase_d = ExitStack()

        def ds(name, shape, dt=F32):
            return sb(name, shape, dt, phase_d)

        dt_h = ds("dt_h", [P, KT, TOK], F32R)
        dt_l = ds("dt_l", [P, KT, TOK], F32R)
        dg = ds("dg", [P, 2, TOK])
        dh = ds("dh", [P, MB, RANK, TOK])
        dab = ds("dab", [P, MB, RANK, TOK])
        beats = ds("beats", [P, 6, TOK], BF16)
        rank = ds("rank", [P, RANK, TOK], BF16)
        dhh = ds("dhh", [P, MB, RANK, TOK], F32R)
        dhl = ds("dhl", [P, MB, RANK, TOK], F32R)
        dy = ds("dy", [P, NT, H])
        res = ds("res", [P, RES, NT, H])
        phase_d.close()

        s_const = sem("constants_ready")
        s_x = [sem(f"x_loaded{i}") for i in range(2)]
        s_w = [sem(f"codes_loaded{i}") for i in range(2)]
        s_xs_free = sem("xs_free")
        s_xs_hi = sem("xs_hi_ready")
        s_xs_lo = sem("xs_lo_ready")
        s_sc_mm = sem("scores_done")
        s_sc_free = sem("scores_psum_free")
        s_sm = sem("softmax_steps_dve")
        s_sma = sem("softmax_steps_act")
        s_smt = sem("softmax_transposed")
        s_deq = sem("dequant_steps_dve")
        s_wf = sem("weights_f32_ready")
        s_whi = sem("weights_hi_ready")
        s_wlo = sem("weights_lo_ready")
        s_xg = sem("front_x_loaded")
        s_xt_t = sem("x_transposed")
        s_xt_hi = sem("xt_hi_ready")
        s_xt_lo = sem("xt_lo_ready")
        s_ctx = sem("context_done")
        s_seen = sem("stats_seen")
        s_ln1 = sem("ln1_stats")
        s_ln1r = sem("ln1_rstd")
        s_x1 = sem("x1_ready")
        s_x1r = sem("x1_residual_kept")
        s_at_t = sem("x1_transposed")
        s_at_hi = sem("at_hi_ready")
        s_at_lo = sem("at_lo_ready")
        s_gate = sem("gate_done")
        s_up = sem("up_done")
        s_gelu = sem("gelu_done")
        s_h = sem("h_ready")
        s_hhi = sem("h_hi_ready")
        s_hlo = sem("h_lo_ready")
        s_down = sem("down_done")
        s_y = sem("y_ready")
        s_ln2 = sem("ln2_stats")
        s_ln2r = sem("ln2_rstd")
        s_x2 = sem("x2_ready")
        s_x2st = sem("x2_stored")
        c_wc_raw = sem("ssm_weights_loaded")
        c_wch = sem("ssm_weights_hi")
        c_wcs = sem("ssm_weights_scaled")
        c_small = sem("ssm_constants_loaded")
        c_a4 = sem("decay_rate_ready")
        c_t = sem("x2_transposed")
        c_xth = sem("x2t_hi_ready")
        c_xtl = sem("x2t_lo_ready")
        c_dtp = sem("dt_projected")
        c_dtc = sem("dt_steps_dve")
        c_dta = sem("dt_steps_act")
        c_acs = sem("decay_sums_done")
        c_ea = sem("decays_ready")
        c_au = sem("masked_decay_ready")
        c_seg = sem("segment_sums_done")
        c_e = sem("segment_decay_ready")
        c_zp = sem("z_projected")
        c_zs = sem("z_gate_ready")
        c_xbc = sem("xbc_projected")
        c_xin = sem("xbc_copied")
        c_halo = sem("halo_copied")
        c_cv = sem("conv_steps")
        c_silu = sem("conv_silu_ready")
        c_ct = sem("c_moved")
        c_w1h = sem("mlp1_hi_ready")
        c_w1l = sem("mlp1_lo_ready")
        c_tr = sem("x_token_major")
        c_btk = sem("b_tok_ready")
        c_G = sem("cb_done")
        c_gm = sem("cb_masked")
        c_m = sem("mixing_ready")
        c_xtk = sem("x_tok_ready")
        c_xsd = sem("x_dt_ready")
        c_xdc = sem("x_decayed_ready")
        c_xd = sem("x_skip_ready")
        c_yoff = sem("y_off_done")
        c_y = sem("y_diag_done")
        c_ds = sem("state_add_done")
        c_st = sem("state_ready")
        c_yo = sem("y_off_scaled")
        c_yo2 = sem("y_off_skip_ready")
        c_g1 = sem("y_ready_ssm")
        c_g = sem("g_ready")
        c_ss = sem("g_square_sum")
        c_rr = sem("g_inv_rms")
        c_gT = sem("g_transposed")
        c_gth = sem("gt_hi_ready")
        c_gtl = sem("gt_lo_ready")
        c_o = sem("projected_out")
        c_rest = sem("x2_rest_kept")
        c_y3 = sem("y3_ready")
        c_ln3 = sem("ln3_stats")
        c_ln3r = sem("ln3_rstd")
        c_x3 = sem("x3_ready")
        c_x3st = [sem(f"x3_stored{i}") for i in range(2)]
        c_xg = [sem(f"x2_loaded{i}") for i in range(2)]
        c_w1r = [sem(f"mlp1_piece_loaded{i}") for i in range(2)]
        c_init = sem("ssm_memory_cleared")
        d_x = sem("x3_loaded")
        d_res = sem("x3_residual_kept")
        d_t = sem("x3_transposed")
        d_th = sem("x3t_hi_ready")
        d_tl = sem("x3t_lo_ready")
        d_gate = sem("mlp1_gate_done")
        d_up = sem("mlp1_up_done")
        d_silu = sem("mlp1_silu_ready")
        d_mul = sem("mlp1_gated_ready")
        d_abs = sem("mlp1_abs_ready")
        d_cmp = sem("pairs_compared")
        d_add = sem("ranks_dve")
        d_padd = sem("ranks_pool")
        d_sel = sem("kept_ready")
        d_hi = sem("kept_hi_ready")
        d_lo = sem("kept_lo_ready")
        d_down = sem("mlp1_down_done")
        d_y = sem("mlp1_sum_ready")
        d_ln = sem("ln4_stats")
        d_lnr = sem("ln4_rstd")
        d_out = sem("output_ready")
        d_st = sem("output_stored")

        block = ctx.enter_context(nc.Block())
        x_rows = x_in.rearrange("(g t p) c -> g p t c", p=P, t=NT)
        x2_rows = x2_dram.rearrange("(g t p) c -> g p t c", p=P, t=NT)
        x3_rows = x3_dram.rearrange("(g t p) c -> g p t c", p=P, t=NT)
        out_rows = out.rearrange("(g t p) c -> g p t c", p=P, t=NT)

        PAIRS = [(0, 0, 3), (1, 3, 2), (2, 5, 1)]
        KEEP = [(2.0, ALU.is_ge), (1.0, ALU.is_ge), (0.0, ALU.is_ge), (1.0, ALU.is_le)]

        def for_groups(step):
            def run(eng):
                step(0, 0, 0, (1, 1, 0))
                with eng.Fori(0, GPB - 1) as i:
                    step(2 * i + 1, 1, i, (2 * i + 2, 0, i + 1))
                    step(2 * i + 2, 0, i + 1, (2 * i + 3, 1, i + 1))
                step(GROUPS - 1, 1, GPB - 1, None)
            return run

        FROM_1 = [s_y, c_xtk, c_gm, c_btk, c_yo, c_g1, c_ds, c_y3, c_ss, c_rr, c_yo2, d_y]
        FROM_16 = [s_x2st, d_st, *c_x3st]

        @block.sync
        def _(sp):
            def load_x(f, u):
                sp.dma_start(xg[:, u], x_rows[f]).then_inc(s_x[u], 16)

            def load_codes(j, u):
                sp.dma_start(wq[:, u], codes[j]).then_inc(s_w[u], 16)
                for q in range(8):
                    sp.dma_start(sc[16 * q:16 * q + 16, u], scales[j, q:q + 1].broadcast_to([16, 512])).then_inc(s_w[u], 16)

            for s_ in FROM_1:
                sp.sem_inc(s_, 1)
            for s_ in FROM_16:
                sp.sem_inc(s_, 16)
            for u in range(2):
                load_x(u, u)
                load_codes(u, u)
            sp.dma_start(win_raw[:], w_in).then_inc(c_wc_raw, 16)
            sp.dma_start(wo_raw[:], w_out).then_inc(c_wc_raw, 16)
            for dst, src in ((cw[:], conv_w), (cb[:], conv_b), (nw[:], norm_w), (dtb[:], dt_bias.broadcast_to([P, HEADS])),
                             (a4[:], a_log.broadcast_to([P, HEADS])), (d4[:], d_skip.broadcast_to([P, HEADS]))):
                sp.dma_start(dst, src).then_inc(c_small, 16)
            with sp.Fori(0, GROUPS // 2 - 1) as h:
                for u in range(2):
                    sp.wait_ge(s_xs_lo, 2 * h + u + 1)
                    load_x(2 * h + u + 2, u)
                    sp.wait_ge(s_wf, 2 * (2 * h + u + 1))
                    load_codes(2 * h + u + 2, u)
            for j in range(GROUPS, JOBS):
                sp.wait_ge(s_wf, 2 * (j - 1))
                load_codes(j, j % 2)
                if j == GROUPS:
                    sp.wait_ge(s_xs_lo, GROUPS)
                    sp.dma_start(xg[:, 0], x_rows[0]).then_inc(s_xg, 16)
            def load_front(g):
                sp.wait_ge(s_xt_t, KT * g)
                sp.dma_start(xg[:, 0], x_rows[g]).then_inc(s_xg, 16)

            def store_x2(g):
                sp.wait_ge(s_x2, NT * (g + 1))
                sp.dma_start(x2_rows[g], xo[:]).then_inc(s_x2st, 16)

            load_front(1)
            with sp.Fori(2, GROUPS) as g:
                load_front(g)
                store_x2(g - 2)
            store_x2(GROUPS - 2)
            store_x2(GROUPS - 1)
            sp.wait_ge(s_x2st, 16 * GROUPS + 16)

            for q in range(2):
                sp.dma_start(xg[:, q], x2_rows[q * GPB]).then_inc(c_xg[q], 16)
                sp.dma_start(w1_raw[:, q], w_mlp1[q]).then_inc(c_w1r[q], 16)

            def store_x3(b, i, half, k):
                sp.wait_ge(c_x3, k + 2)
                sp.dma_start(x3_rows[b * GPB + i, :, 2 * half:2 * half + 2], y3[:, 2 * half:2 * half + 2]).then_inc(c_x3st[half], 16)

            def step(s, b, i, more):
                k = NT * s
                if more:
                    sp.wait_ge(c_rest, s + 1)
                    sp.dma_start(xg[:, b], x2_rows[b * GPB + i + 1]).then_inc(c_xg[b], 16)
                store_x3(b, i, 0, k)
                if more:
                    sp.wait_ge(c_w1l, s + 1)
                    sp.dma_start(w1_raw[:, b], w_mlp1[s + 2]).then_inc(c_w1r[b], 16)
                store_x3(b, i, 1, k + 2)

            with sp.Fori(0, GPB - 1) as i:
                step(2 * i, 0, i, True)
                step(2 * i + 1, 1, i, True)
            step(GROUPS - 2, 0, GPB - 1, False)
            step(GROUPS - 1, 1, GPB - 1, False)
            for half in range(2):
                sp.wait_ge(c_x3st[half], 16 * GROUPS + 16)

            sp.dma_start(xg[:, 0], x3_rows[0]).then_inc(d_x, 16)
            def load_x3(g):
                sp.wait_ge(d_t, KT * g)
                sp.wait_ge(d_res, g)
                sp.dma_start(xg[:, 0], x3_rows[g]).then_inc(d_x, 16)

            def store_out(g):
                sp.wait_ge(d_out, NT * (g + 1))
                sp.dma_start(out_rows[g], dy[:]).then_inc(d_st, 16)

            load_x3(1)
            with sp.Fori(2, GROUPS) as g:
                load_x3(g)
                store_out(g - 2)
            store_out(GROUPS - 2)
            store_out(GROUPS - 1)
            sp.wait_ge(d_st, 16 * GROUPS + 16)

        @block.gpsimd
        def _(pool):
            pool.memset(wide_i[:], 0.0).then_inc(s_const, 1)
            pool.memset(zero_bf[:], 0.0).then_inc(s_const, 1)
            pool.memset(m_half[:], -0.5).then_inc(s_const, 1)
            pool.memset(eps4[:], EPS).then_inc(s_const, 1)
            pool.memset(eps_rms[:], EPS * D_INNER).then_inc(s_const, 1)
            pool.memset(upto[:], 1.0).then_inc(s_const, 1)
            pool.memset(below[:], 1.0).then_inc(s_const, 1)
            pool.memset(ones[:], 1.0).then_inc(s_const, 1)
            pool.wait_ge(s_const, 8)
            pool.affine_select(out=ident, in_=ident, compare_op=ALU.not_equal, fill=1.0, base=0,
                               pattern=[[-1, P]], channel_multiplier=1).then_inc(s_const, 1)
            pool.affine_select(out=upto[:], in_=upto[:], compare_op=ALU.is_ge, fill=0.0, base=0,
                               pattern=[[1, P]], channel_multiplier=-1).then_inc(s_const, 1)
            pool.affine_select(out=below[:], in_=below[:], compare_op=ALU.is_gt, fill=0.0, base=0,
                               pattern=[[-1, P]], channel_multiplier=1).then_inc(s_const, 1)

            def weights_lo(j, u):
                for nib in range(2):
                    pool.wait_ge(s_whi, 2 * j + nib + 1)
                    pool.tensor_tensor(w0_lo[:, j, nib], wf[:, u, nib], w0_hi[:, j, nib].bitcast(F32),
                                       ALU.subtract).then_inc(s_wlo, 1)

            pool.sem_inc(s_wlo, 4)
            with pool.Fori(0, JOBS // 2 - 1) as h:
                for u in range(2):
                    weights_lo(2 * h + u, u)

            def inv_std(f, mv_, ve_, r_, s_in, s_out):
                pool.wait_ge(s_in, 2 * NT * (f + 1))
                pool.tensor_tensor(ve_[:], mv_[:, :, 1], eps4[:], ALU.add).then_inc(s_out, 1)
                pool.wait_ge(s_out, 2 * f + 1)
                pool.tensor_tensor(r_[:], ve_[:], m_half[:], ALU.pow).then_inc(s_out, 1)

            inv_std(0, mv, ve, rstd, s_ln1, s_ln1r)
            for j in range(JOBS - 2, JOBS):
                weights_lo(j, j % 2)
            pool.wait_ge(c_wc_raw, 32)
            pool.wait_ge(c_small, 96)
            for k in range(HEADS):
                pool.tensor_scalar(wo_raw[:, k], wo_raw[:, k], nw[:, k:k + 1], float(D_INNER) ** 0.5, ALU.mult,
                                   ALU.mult).then_inc(c_wcs, 1)
            pool.tensor_copy(win_h[:], win_raw[:]).then_inc(c_wch, 1)
            pool.wait_ge(c_wcs, HEADS)
            pool.tensor_copy(wo_h[:], wo_raw[:]).then_inc(c_wch, 1)
            pool.wait_ge(c_wch, 2)
            pool.tensor_tensor(win_l[:], win_raw[:], win_h[:].bitcast(F32), ALU.subtract).then_inc(c_wch, 1)
            pool.tensor_tensor(wo_l[:], wo_raw[:], wo_h[:].bitcast(F32), ALU.subtract).then_inc(c_wch, 1)
            inv_std(1, mv, ve, rstd, s_ln1, s_ln1r)
            with pool.Fori(1, GROUPS - 1) as g:
                inv_std(g - 1, mvb, veb, rstdb, s_ln2, s_ln2r)
                inv_std(g + 1, mv, ve, rstd, s_ln1, s_ln1r)
            for g in (GROUPS - 2, GROUPS - 1):
                inv_std(g, mvb, veb, rstdb, s_ln2, s_ln2r)

            pool.wait_ge(s_x2st, 16 * GROUPS + 16)
            pool.memset(tail[:], 0.0).then_inc(c_init, 1)
            pool.memset(state[:], 0.0).then_inc(c_st, 1)

            def masked_decay(n, t):
                if t == 0:
                    pool.wait_ge(c_dtc, DT_STEPS * (n + 1))
                pool.wait_ge(c_seg, NT * n + max(t - 1, 0))
                pool.tensor_tensor(au[:, t % 2], upto[:].unsqueeze(1).broadcast_to([P, HEADS, P]),
                                   adt[:, t].unsqueeze(2).broadcast_to([P, HEADS, P]), ALU.mult).then_inc(c_au, 1)

            def inv_std_chunk(k, c):
                pool.wait_ge(c_ln3, 2 * k + 2)
                pool.tensor_tensor(ve[:, c:c + 1], mv[:, c, 1:2], eps4[:, 0:1], ALU.add).then_inc(c_ln3r, 1)
                pool.wait_ge(c_ln3r, 2 * k + 1)
                pool.tensor_tensor(rstd[:, c:c + 1], ve[:, c:c + 1], m_half[:, 0:1], ALU.pow).then_inc(c_ln3r, 1)

            def inv_rms(k, u):
                pool.wait_ge(c_ss, k + 1 + 1)
                pool.wait_ge(c_y3, (k if isinstance(k, int) and k == 0 else k - 1) + 1)
                pool.tensor_tensor(rr[:, u:u + 1], ss[:, u:u + 1], eps_rms[:], ALU.add).then_inc(c_rr, 1)
                pool.wait_ge(c_rr, 2 * k + 1 + 1)
                pool.tensor_tensor(rr[:, u:u + 1], rr[:, u:u + 1], m_half[:, 0:1], ALU.pow).then_inc(c_rr, 1)

            def step(s, b, i, nxt):
                for c in range(NT):
                    k, u = NT * s + c, c % 2
                    before = not isinstance(k, int) or k > 0
                    pool.wait_ge(c_xtk, k + 1 + 1)
                    pool.wait_ge(c_yo2, k + 1)
                    pool.tensor_tensor(xsd[:, u], xtk[:, u], dtv[:, b, c].unsqueeze(2).broadcast_to([P, HEADS, HEADDIM]),
                                       ALU.mult).then_inc(c_xsd, 1)
                    pool.wait_ge(c_xsd, k + 1)
                    pool.wait_ge(c_ds, (k if c == 0 else k - 1) + 1)
                    pool.tensor_tensor(xdc[:, u], xsd[:, u], ee[:, c, :, P - 1:P].broadcast_to([P, HEADS, HEADDIM]),
                                       ALU.mult).then_inc(c_xdc, 1)
                    if nxt and c == 3:
                        masked_decay(nxt[0], 3)
                    if before:
                        inv_rms(k - 1, 1 - u)
                    pool.tensor_tensor(xd[:, u], xtk[:, u], d4[:].unsqueeze(2).broadcast_to([P, HEADS, P]),
                                       ALU.mult).then_inc(c_xd, 1)
                    pool.wait_ge(c_yo, k + 1 + 1)
                    pool.wait_ge(c_xd, k + 1)
                    pool.wait_ge(c_g1, (k if c == 0 else k - 1) + 1)
                    pool.tensor_tensor(xd[:, u], yo[:, u], xd[:, u], ALU.add).then_inc(c_yo2, 1)
                    if before and (not isinstance(k, int) or k > 1):
                        inv_std_chunk(k - 2, (c - 2) % NT)
                    if nxt and c == 1:
                        masked_decay(nxt[0], 0)
                        masked_decay(nxt[0], 1)
                    if nxt and c == 2:
                        masked_decay(nxt[0], 2)
                    if c == 3:
                        pool.wait_ge(c_w1h, s + 1)
                        pool.tensor_tensor(w1_l[:, s], w1_raw[:, b], w1_h[:, s].bitcast(F32), ALU.subtract).then_inc(c_w1l, 1)

            for t in range(NT):
                masked_decay(0, t)
            for_groups(step)(pool)
            last = NT * GROUPS - 1
            inv_rms(last, 1)
            inv_std_chunk(last - 1, NT - 2)
            inv_std_chunk(last, NT - 1)

            for half in range(2):
                pool.wait_ge(c_x3st[half], 16 * GROUPS + 16)

            def ranks(m):
                pool.wait_ge(d_cmp, len(PAIRS) * (m + 1))
                pool.tensor_tensor(rank[:, 2], beats[:, 5], beats[:, 1], ALU.subtract).then_inc(d_padd, 1)
                pool.tensor_tensor(rank[:, 3], beats[:, 2], beats[:, 4], ALU.add).then_inc(d_padd, 1)
                pool.wait_ge(d_padd, 4 * m + 1)
                pool.tensor_tensor(rank[:, 2], rank[:, 2], beats[:, 3], ALU.subtract).then_inc(d_padd, 1)
                pool.wait_ge(d_padd, 4 * m + 2)
                pool.tensor_tensor(rank[:, 3], rank[:, 3], beats[:, 5], ALU.add).then_inc(d_padd, 1)

            def unit(m, mb):
                ranks(m)
                for r in range(RANK):
                    pool.wait_ge(d_hi, RANK * m + r + 1)
                    pool.tensor_tensor(dhl[:, mb, r], dab[:, mb, r], dhh[:, mb, r].bitcast(F32),
                                       ALU.subtract).then_inc(d_lo, 1)

            for m in range(3):
                unit(m, m % MB)
            with pool.Fori(2, GROUPS) as g:
                inv_std(g - 2, mv, ve, rstd, d_ln, d_lnr)
                unit(MB * g - 1, 1)
                unit(MB * g, 0)
            unit(MB * GROUPS - 1, 1)
            for g in (GROUPS - 2, GROUPS - 1):
                inv_std(g, mv, ve, rstd, d_ln, d_lnr)

        @block.scalar
        def _(act):
            def copy(dst, src):
                return act.activation(dst, src, ACT.Copy)

            def weights_hi(j, u):
                for nib in range(2):
                    act.wait_ge(s_wf, 2 * j + nib + 1)
                    copy(w0_hi[:, j, nib], wf[:, u, nib]).then_inc(s_whi, 1)

            def xs_hi(f, u, loads):
                act.wait_ge(s_x[u], 16 * loads)
                act.wait_ge(s_xs_free, f + 1)
                copy(xs[:, u, :, 0:H], xg[:, u]).then_inc(s_xs_hi, 1)

            def two_pieces(q, more=True):
                xs_hi(2 * q + 1, 1, q + 1)
                weights_hi(2 * q, 0)
                if more:
                    xs_hi(2 * q + 2, 0, q + 2)
                weights_hi(2 * q + 1, 1)

            xs_hi(0, 0, 1)
            for b in range(BATCH):
                with act.Fori(GPB // 2 * b, GPB // 2 * (b + 1) - b) as q:
                    two_pieces(q)
                if b == BATCH - 1:
                    two_pieces(GROUPS // 2 - 1, more=False)
                act.wait_ge(s_sc_mm, b + 1)
                for i in range(2):
                    copy(s_hl[:, i], ps_gate[i][:, H:2 * H]).then_inc(s_sma, 1)
                act.wait_ge(s_sm, 6 * b + 4)
                for i in range(2):
                    act.activation(s_hl[:, i], s_full[:, i], ACT.Exp, bias=nmax[:, i:i + 1],
                                   accum_out=rsum[:, i:i + 1]).then_inc(s_sma, 1)
                act.wait_ge(s_smt, 2 * b + 2)
                copy(soft_wt[:, b, 0], ps_t[1][:]).then_inc(s_sma, 1)
            def x_hi(f, k):
                act.wait_ge(s_xt_t, KT * f + k + 1)
                act.wait_ge(s_ctx, NT * f)
                copy(xt_h[:, k], ps_t[k][:]).then_inc(s_xt_hi, 1)

            def a_hi(f, k):
                act.wait_ge(s_at_t, KT * f + k + 1)
                act.wait_ge(s_up, NB0 * f)
                copy(at_h[:, k], ps_t[k][:]).then_inc(s_at_hi, 1)

            def gelu(g, n):
                act.wait_ge(s_gate, NB0 * g + n + 1)
                act.activation(gl[:, n % 2], ps_gate[n % 2][:], ACT.Gelu_apprx_tanh).then_inc(s_gelu, 1)

            def h_hi(g, n):
                act.wait_ge(s_h, NB0 * g + n + 1)
                copy(hh[:, n % 2], hb[:, n % 2]).then_inc(s_hhi, 1)

            def keep_residual(g):
                act.wait_ge(s_y, NT * g + 1)
                act.wait_ge(s_x1, NT * (g + 1))
                copy(x1_res[:], x1[:]).then_inc(s_x1r, 1)

            def group(g, more):
                for n in range(NB0):
                    gelu(g, n)
                    if more and n == NB0 - 1:
                        a_hi(g + 1, 0)
                        a_hi(g + 1, 1)
                    h_hi(g, n)
                    if n == 4:
                        keep_residual(g)
                    if more and n == 2:
                        x_hi(g + 1, 0)
                        x_hi(g + 1, 1)

            for k in range(KT):
                x_hi(0, k)
            for j in range(GROUPS, JOBS):
                weights_hi(j, j % 2)
            for k in range(KT):
                a_hi(0, k)
            with act.Fori(0, GROUPS - 1) as g:
                group(g, True)
            group(GROUPS - 1, False)

            act.wait_ge(s_x2st, 16 * GROUPS + 16)
            act.wait_ge(c_small, 96)
            act.activation(a4[:], a4[:], ACT.Exp).then_inc(c_a4, 1)
            act.wait_ge(c_init, 1)

            def xbc_in(n, b, j):
                act.wait_ge(c_xbc, XB * n + j + 1)
                act.wait_ge(c_silu, XB * n + max(j - 1, 0))
                copy(raw[:, j, TAPS - 1:], ring(XBC0 + j)[:])
                act.activation(acc[:, j % 2], ring(XBC0 + j)[:], ACT.Identity, bias=cb[:, j:j + 1],
                               scale=cw[:, j, TAPS - 1:TAPS]).then_inc(c_xin, 1)

            def conv_silu(n, b, j):
                act.wait_ge(c_cv, (TAPS - 1) * (XB * n + j + 1))
                act.activation(xc[:, b, j] if j < HEADS else bc[:, b], acc[:, j % 2], ACT.Silu).then_inc(c_silu, 1)

            def z_silu(n, t):
                act.wait_ge(c_zp, NT * n + t + 1)
                if not isinstance(n, int) or n > 0:
                    act.wait_ge(c_g, NT * n + t - 3)
                act.activation(zs[:, t], z_place(t)[:], ACT.Silu).then_inc(c_zs, 1)

            def x2_hi(n, b):
                act.wait_ge(c_cv, (TAPS - 1) * XB * n)
                act.wait_ge(c_halo, 2 * n)
                copy(raw[:, :, 0:TAPS - 1], tail[:, b]).then_inc(c_halo, 1)
                for k in range(KT):
                    act.wait_ge(c_t, KT * n + k + 1)
                    copy(xt_h[:, k], ring(k)[:]).then_inc(c_xth, 1)

            def dt_exp_ln(n, b):
                act.wait_ge(c_dtc, DT_STEPS * n + 2)
                act.activation(de[:], dax[:], ACT.Exp).then_inc(c_dta, 1)
                xbc_in(n, b, 0)
                act.wait_ge(c_dtc, DT_STEPS * n + 3)
                act.activation(dl[:], du[:], ACT.Ln).then_inc(c_dta, 1)

            def keep_tail(n, b):
                act.wait_ge(c_xin, XB * (n + 1))
                act.wait_ge(c_halo, 2 * n + 1)
                copy(tail[:, b], raw[:, :, TOK:]).then_inc(c_halo, 1)

            def decays(n, b):
                act.wait_ge(c_acs, n + 1)
                act.activation(ea[:, b].rearrange("p t h -> p (t h)"), ring(ACS0)[:, 0:16], ACT.Exp).then_inc(c_ea, 1)
                act.activation(et[:, b].rearrange("p t h -> p (t h)"), ring(ACS0)[0:D_STATE, 16:32], ACT.Exp).then_inc(c_ea, 1)

            def segment_exp(n, t):
                if not isinstance(n, int) or n > 0:
                    act.wait_ge(c_m, NT * n + t - 3)
                    act.wait_ge(c_xdc, NT * n + t - 3)
                act.wait_ge(c_seg, NT * n + t + 1)
                act.activation(ee[:, t].rearrange("p h l -> p (h l)"), ring(SEG0 + t)[:], ACT.Exp).then_inc(c_e, 1)

            def project(slot, nxt, part):
                n, b, i = nxt
                if slot == 0 and part == 0:
                    x2_hi(n, b)
                if slot == 0 and part == 1:
                    dt_exp_ln(n, b)
                    xbc_in(n, b, 1)
                if slot == 1 and part == 0:
                    conv_silu(n, b, 0)
                    xbc_in(n, b, 2)
                    conv_silu(n, b, 1)
                    xbc_in(n, b, 3)
                if slot == 2 and part == 0:
                    conv_silu(n, b, 2)
                    xbc_in(n, b, 4)
                    z_silu(n, 0)
                    conv_silu(n, b, 3)
                    z_silu(n, 1)
                    decays(n, b)
                if slot == 2 and part == 1:
                    segment_exp(n, 0)
                if slot == 3 and part == 0:
                    segment_exp(n, 1)
                    segment_exp(n, 2)
                    keep_tail(n, b)
                    segment_exp(n, 3)
                    conv_silu(n, b, 4)
                    z_silu(n, 2)
                if slot == 3 and part == 1:
                    z_silu(n, 3)

            def g_hi(k, u):
                act.wait_ge(c_gT, k + 1)
                copy(gt_h[:, u].rearrange("p h t -> p (h t)"), ps_g[:]).then_inc(c_gth, 1)

            def step(s, b, i, nxt):
                for c in range(NT):
                    k, u = NT * s + c, c % 2
                    act.wait_ge(c_tr, k + 1)
                    copy(xtk[:, u].rearrange("p h d -> p (h d)"), ps_x[:]).then_inc(c_xtk, 1)
                    if c > 0 or not isinstance(k, int) or k > 0:
                        g_hi(k - 1, 1 - u)
                    act.wait_ge(c_yoff, k + 1)
                    act.wait_ge(c_ea, 2 * (s + 1))
                    for h in range(HEADS):
                        y = act.activation(yo[:, u, h], ps_yoff[:, h * HEADDIM:(h + 1) * HEADDIM], ACT.Copy,
                                           scale=ea[:, b, c, h:h + 1])
                    y.then_inc(c_yo, 1)
                    if nxt:
                        project(c, nxt, 0)
                    act.wait_ge(c_g, k + 1)
                    act.wait_ge(c_ss, k + 1)
                    act.wait_ge(c_rr, 2 * k + 1)
                    act.activation(yo[:, u].rearrange("p h d -> p (h d)"), gg[:, u], ACT.Square, accum_out=ss[:, u:u + 1]).then_inc(c_ss, 1)
                    if c == 1:
                        act.wait_ge(c_w1r[b], 16 * (i + 1))
                        copy(w1_h[:, s], w1_raw[:, b]).then_inc(c_w1h, 1)
                    if c == 2:
                        act.wait_ge(c_y3, k + 1)
                        copy(rest[:], xg[:, b, 2:]).then_inc(c_rest, 1)
                    if nxt:
                        project(c, nxt, 1)

            for j in range(NT):
                for part in range(2):
                    project(j, (0, 0, 0), part)
            for_groups(step)(act)
            g_hi(NT * GROUPS - 1, 1)

            for half in range(2):
                act.wait_ge(c_x3st[half], 16 * GROUPS + 16)

            def keep_x3(g):
                act.wait_ge(d_x, 16 * (g + 1))
                copy(res[:, g & RES - 1], xg[:, 0]).then_inc(d_res, 1)

            def x3_hi(g):
                if not isinstance(g, int) or g > 0:
                    act.wait_ge(d_up, MB * RANK * g)
                for k in range(KT):
                    act.wait_ge(d_t, KT * g + k + 1)
                    copy(dt_h[:, k], ps_t[k][:]).then_inc(d_th, 1)

            def kept_hi(m, mb, r):
                act.wait_ge(d_sel, RANK * m + r + 1)
                copy(dhh[:, mb, r], dab[:, mb, r]).then_inc(d_hi, 1)

            def unit(m, mb, g, back, old, front=None):
                for r in range(RANK):
                    act.wait_ge(d_gate, RANK * m + r + 1)
                    act.activation(dg[:, r % 2], ps_gate[r % 2][:], ACT.Silu).then_inc(d_silu, 1)
                    if front is not None and r == RANK - 1:
                        x3_hi(front)
                    if back and r > 1:
                        kept_hi(m - 1, 1 - mb, 2 * r - 4)
                        kept_hi(m - 1, 1 - mb, 2 * r - 3)
                    act.wait_ge(d_mul, RANK * m + r + 1)
                    if old:
                        act.wait_ge(d_lo, RANK * (m - 2) + r + 1)
                    act.activation(dab[:, mb, r], dh[:, mb, r], ACT.Abs).then_inc(d_abs, 1)
                    if mb == 0 and r == 0:
                        keep_x3(g)

            def group(g, last=False):
                old = not isinstance(g, int) or g > 0
                unit(MB * g, 0, g, old, old)
                unit(MB * g + 1, 1, g, True, old, None if last else g + 1)

            x3_hi(0)
            group(0)
            group(1)
            with act.Fori(2, GROUPS - 1) as g:
                group(g)
            group(GROUPS - 1, last=True)
            for r in range(RANK):
                kept_hi(MB * GROUPS - 1, 1, r)

        @block.vector
        def _(dve):
            def dequant(j, u, q):
                dve.wait_ge(s_w[u], 144 * (q + 1))
                dve.wait_ge(s_wf, 2 * j)
                for nib in range(2):
                    dve.tensor_scalar(sgn[:, nib], wq[:, u], 28 - 4 * nib, -2 ** 31, ALU.logical_shift_left,
                                      ALU.bitwise_and).then_inc(s_deq, 1)
                    dve.tensor_scalar(mag[:, nib], wq[:, u], 22 - 4 * nib, 7 << 22, ALU.logical_shift_left,
                                      ALU.bitwise_and).then_inc(s_deq, 1)
                dve.wait_ge(s_deq, 5 * j + 4)
                dve.tensor_tensor(mag[:], mag[:], sgn[:], ALU.bitwise_or).then_inc(s_deq, 1)
                dve.wait_ge(s_deq, 5 * j + 5)
                for nib in range(2):
                    if nib == 0:
                        dve.wait_ge(s_wlo, 2 * j + 2)
                    dve.scalar_tensor_tensor(wf[:, u, nib], mag[:, nib].bitcast(F32), 2.0 ** 126, sc[:, u],
                                             ALU.mult, ALU.mult).then_inc(s_wf, 1)

            dve.wait_ge(s_const, 11)
            for b in range(BATCH):
                with dve.Fori(0, GPB // 2) as h:
                    for u in range(2):
                        f = GPB * b + 2 * h + u
                        dve.wait_ge(s_xs_hi, f + 1)
                        dve.tensor_tensor(xs[:, u, :, H:2 * H], xg[:, u], xs[:, u, :, 0:H].bitcast(F32),
                                          ALU.subtract).then_inc(s_xs_lo, 1)
                        dequant(f, u, GPB // 2 * b + h)
                for i in range(2):
                    dve.wait_ge(s_sma, 5 * b + i + 1)
                    dve.tensor_tensor(s_full[:, i], ps_gate[i][:, 0:H], s_hl[:, i], ALU.add).then_inc(s_sm, 1)
                dve.wait_ge(s_sm, 6 * b + 2)
                dve.wait_ge(s_smt, 2 * b + 1)
                sf = s_full[:].rearrange("p i j -> p (i j)")
                dve.tensor_tensor(sf, sf, ps_t[0][:], ALU.add).then_inc(s_sm, 1)
                dve.wait_ge(s_sm, 6 * b + 3)
                dve.tensor_reduce(nmax[:], s_full[:], AX_X, ALU.max, negate=True).then_inc(s_sm, 1)
                dve.wait_ge(s_sma, 5 * b + 4)
                dve.reciprocal(rinv[:], rsum[:]).then_inc(s_sm, 1)
                dve.wait_ge(s_sm, 6 * b + 5)
                for i in range(2):
                    w = dve.scalar_tensor_tensor(s_hl[:, i], s_hl[:, i], rinv[:, i:i + 1],
                                                 wide_i[:, P * (1 - i):P * (1 - i) + H], ALU.mult, ALU.add)
                w.then_inc(s_sm, 1)
                dve.wait_ge(s_sma, 5 * b + 5)
                dve.tensor_tensor(soft_wt[:, b, 1], ps_t[1][:], soft_wt[:, b, 0].bitcast(F32),
                                  ALU.subtract).then_inc(s_sc_free, 1)
            def lo_part(dst, src, hi):
                return dve.tensor_tensor(dst, src, hi.bitcast(F32), ALU.subtract)

            def x_lo(f, k):
                dve.wait_ge(s_xt_hi, KT * f + k + 1)
                lo_part(xt_l[:, k], ps_t[k][:], xt_h[:, k]).then_inc(s_xt_lo, 1)

            def a_lo(f, k):
                dve.wait_ge(s_at_hi, KT * f + k + 1)
                lo_part(at_l[:, k], ps_t[k][:], at_h[:, k]).then_inc(s_at_lo, 1)

            def stats(f, src, st_, mv_, s_):
                for t in range(NT):
                    dve.bn_stats(st_[:, t], src[t]).then_inc(s_, 1)
                dve.wait_ge(s_, 2 * NT * f + NT)
                dve.sem_inc(s_seen, 1)
                for t in range(NT):
                    dve.bn_aggr(mv_[:, t], st_[:, t]).then_inc(s_, 1)

            ctx_tile = [ps_t[t // 2][:, t % 2 * H:t % 2 * H + H] for t in range(NT)]
            down_tile = [ps_down[t // 2][:, t % 2 * H:t % 2 * H + H] for t in range(NT)]

            def ln1_stats(f):
                dve.wait_ge(s_ctx, NT * (f + 1))
                stats(f, ctx_tile, st6, mv, s_ln1)

            def ln1_apply(f):
                dve.wait_ge(s_ln1r, 2 * (f + 1))
                if not isinstance(f, int) or f > 0:
                    dve.wait_ge(s_x1r, f)
                for t in range(NT):
                    dve.tensor_scalar(x1[:, t], ctx_tile[t], mv[:, t, 0:1], rstd[:, t:t + 1],
                                      ALU.subtract, ALU.mult).then_inc(s_x1, 1)

            def gated(g, n):
                dve.wait_ge(s_gelu, NB0 * g + n + 1)
                dve.wait_ge(s_up, NB0 * g + n + 1)
                dve.tensor_tensor(hb[:, n % 2], gl[:, n % 2], ps_up[n % 2][:], ALU.mult).then_inc(s_h, 1)

            def h_lo(g, n):
                dve.wait_ge(s_hhi, NB0 * g + n + 1)
                lo_part(hl[:, n % 2], hb[:, n % 2], hh[:, n % 2]).then_inc(s_hlo, 1)

            def add_x1(g):
                dve.wait_ge(s_down, g + 1)
                dve.wait_ge(s_x1r, g + 1)
                for t in range(NT):
                    dve.tensor_tensor(yb[:, t], down_tile[t], x1_res[:, t], ALU.add).then_inc(s_y, 1)

            def ln2_stats(g):
                dve.wait_ge(s_y, NT * (g + 1) + 1)
                stats(g, [yb[:, t] for t in range(NT)], st6b, mvb, s_ln2)

            def ln2_apply(g):
                dve.wait_ge(s_ln2r, 2 * (g + 1))
                dve.wait_ge(s_x2st, 16 * g + 16)
                for t in range(NT):
                    dve.tensor_scalar(xo[:, t], yb[:, t], mvb[:, t, 0:1], rstdb[:, t:t + 1],
                                      ALU.subtract, ALU.mult).then_inc(s_x2, 1)

            def group(g, before, more):
                for n in range(NB0):
                    gated(g, n)
                    if more and n == NB0 - 1:
                        a_lo(g + 1, 0)
                        a_lo(g + 1, 1)
                    h_lo(g, n)
                    if before and n == 0:
                        add_x1(g - 1)
                    if before and n == 1:
                        ln2_stats(g - 1)
                    if before and n == 3:
                        ln2_apply(g - 1)
                    if more and n == 2:
                        x_lo(g + 1, 0)
                        x_lo(g + 1, 1)
                    if more and n == 5:
                        ln1_stats(g + 1)
                    if more and n == 7:
                        ln1_apply(g + 1)

            dequant(GROUPS, 0, GROUPS // 2)
            for k in range(KT):
                x_lo(0, k)
            dequant(GROUPS + 1, 1, GROUPS // 2)
            dequant(GROUPS + 2, 0, GROUPS // 2 + 1)
            ln1_stats(0)
            dequant(GROUPS + 3, 1, GROUPS // 2 + 1)
            ln1_apply(0)
            for k in range(KT):
                a_lo(0, k)
            group(0, False, True)
            with dve.Fori(1, GROUPS - 1) as g:
                group(g, True, True)
            group(GROUPS - 1, True, False)
            add_x1(GROUPS - 1)
            ln2_stats(GROUPS - 1)
            ln2_apply(GROUPS - 1)

            dve.wait_ge(s_x2st, 16 * GROUPS + 16)
            dve.wait_ge(c_small, 96)
            dve.wait_ge(c_a4, 1)

            def conv(n, b, j):
                dve.wait_ge(c_xin, XB * n + j + 1)
                dve.wait_ge(c_halo, 2 * n + 1)
                for tap in range(TAPS - 1):
                    steps = (TAPS - 1) * (XB * n + j) + tap
                    if tap > 0:
                        dve.wait_ge(c_cv, steps)
                    dve.scalar_tensor_tensor(acc[:, j % 2], raw[:, j, tap:tap + TOK], cw[:, j, tap:tap + 1],
                                             acc[:, j % 2], ALU.mult, ALU.add).then_inc(c_cv, 1)

            def dt_chain(n, b):
                def done(k, ins):
                    ins.then_inc(c_dtc, 1)
                    dve.wait_ge(c_dtc, DT_STEPS * n + k)

                flat = d0[:].rearrange("p t h -> p (t h)")
                dt_flat = dtv[:, b].rearrange("p t h -> p (t h)")
                dve.wait_ge(c_dtp, n + 1)
                done(1, dve.tensor_tensor(d0[:], ring(DT0)[:, 0:16].rearrange("p (t h) -> p t h", h=HEADS),
                                          dtb[:].unsqueeze(1).broadcast_to([P, NT, HEADS]), ALU.add))
                done(2, dve.scalar_tensor_tensor(dax[:], flat, -1.0, flat, ALU.mult, ALU.min))
                dve.wait_ge(c_dta, 2 * n + 1)
                done(3, dve.tensor_scalar(du[:], de[:], 1.0, None, ALU.add))
                conv(n, b, 0)
                done(4, dve.tensor_scalar(um[:], du[:], -1.0, None, ALU.add))
                done(5, dve.scalar_tensor_tensor(dden[:], um[:], 0.0, um[:], ALU.is_equal, ALU.add))
                done(6, dve.reciprocal(drec[:], dden[:]))
                done(7, dve.tensor_tensor(dm1[:], de[:], drec[:], ALU.mult))
                dve.wait_ge(c_dta, 2 * n + 2)
                done(8, dve.scalar_tensor_tensor(dl2[:], um[:], 0.0, dl[:], ALU.is_equal, ALU.add))
                done(9, dve.tensor_tensor(dm2[:], dm1[:], dl2[:], ALU.mult))
                done(10, dve.scalar_tensor_tensor(dt_flat, flat, 0.0, dm2[:], ALU.max, ALU.add))
                done(11, dve.scalar_tensor_tensor(adt[:], dtv[:, b], -1.0, a4[:].unsqueeze(1).broadcast_to([P, NT, HEADS]),
                                                  ALU.mult, ALU.mult))

            def project(slot, nxt, part):
                n, b, i = nxt
                if slot == 0 and part == 0:
                    for k in range(KT):
                        dve.wait_ge(c_xth, KT * n + k + 1)
                        lo_part(xt_l[:, k], ring(k)[:], xt_h[:, k]).then_inc(c_xtl, 1)
                if slot == 0 and part == 1:
                    dt_chain(n, b)
                if slot > 0 and (slot < 3 or part == 0) and not (slot == 2 and part == 1):
                    conv(n, b, {(1, 0): 1, (1, 1): 2, (2, 0): 3, (3, 0): 4}[slot, part])
                if slot == 3 and part == 1:
                    dve.wait_ge(c_silu, XB * (n + 1))
                    dve.tensor_copy(ct[:, b], bc[D_STATE:2 * D_STATE, b]).then_inc(c_ct, 1)

            def g_lo(k, u):
                dve.wait_ge(c_gth, k + 1)
                lo_part(gt_l[:, u].rearrange("p h t -> p (h t)"), ps_g[:],
                        gt_h[:, u].rearrange("p h t -> p (h t)")).then_inc(c_gtl, 1)

            def add_out(s, b, k, c, u):
                dve.wait_ge(c_o, k + 1)
                dve.wait_ge(c_rr, 2 * (k + 1) + 1)
                if c % 2 == 0:
                    dve.wait_ge(c_x3st[c // 2], 16 * s + 16)
                if c == 2:
                    dve.wait_ge(c_rest, s + 1)
                dve.scalar_tensor_tensor(y3[:, c], ps_g[:, 0:H], rr[:, u:u + 1], xg[:, b, c] if c < 2 else rest[:, c - 2],
                                         ALU.mult, ALU.add).then_inc(c_y3, 1)
                dve.wait_ge(c_y3, k + 2)
                dve.bn_stats(st6[:, c], y3[:, c]).then_inc(c_ln3, 1)
                dve.wait_ge(c_ln3, 2 * k + 1)
                dve.sem_inc(s_seen, 1)
                dve.bn_aggr(mv[:, c], st6[:, c]).then_inc(c_ln3, 1)

            def ln3_apply(k, c):
                dve.wait_ge(c_ln3r, 2 * k + 2)
                dve.tensor_scalar(y3[:, c], y3[:, c], mv[:, c, 0:1], rstd[:, c:c + 1], ALU.subtract,
                                  ALU.mult).then_inc(c_x3, 1)

            def step(s, b, i, nxt):
                for c in range(NT):
                    k, u = NT * s + c, c % 2
                    later = not isinstance(k, int)
                    dve.wait_ge(c_G, k + 1)
                    dve.tensor_tensor(gm[:, u], small[:, P:2 * P], upto[:], ALU.mult).then_inc(c_gm, 1)
                    dve.tensor_copy(btk[:, u], small[:, 0:D_STATE]).then_inc(c_btk, 1)
                    dve.wait_ge(c_gm, k + 1 + 1)
                    dve.wait_ge(c_e, k + 1)
                    dve.tensor_tensor(mm_[:, u], ee[:, c], gm[:, u].unsqueeze(1).broadcast_to([P, HEADS, P]),
                                      ALU.mult).then_inc(c_m, 1)
                    if later or k > 0:
                        g_lo(k - 1, 1 - u)
                    if nxt:
                        project(c, nxt, 0)
                    dve.wait_ge(c_ds, k + 1 + 1)
                    dve.wait_ge(c_ea, 2 * (s + 1))
                    dve.wait_ge(c_st, k + 1)
                    for h in range(HEADS):
                        st = dve.scalar_tensor_tensor(state[:, b, h], state[:, b, h], et[:, b, c, h:h + 1],
                                                      ps_ds[0:D_STATE, h * HEADDIM:(h + 1) * HEADDIM], ALU.mult, ALU.add)
                    st.then_inc(c_st, 1)
                    dve.wait_ge(c_y, k + 1)
                    dve.wait_ge(c_yo2, k + 1 + 1)
                    dve.tensor_tensor(gg[:, u], ps_y[:], xd[:, u].rearrange("p h d -> p (h d)"), ALU.add).then_inc(c_g1, 1)
                    dve.wait_ge(c_g1, k + 1 + 1)
                    dve.wait_ge(c_zs, k + 1)
                    dve.tensor_tensor(gg[:, u], gg[:, u], zs[:, c], ALU.mult).then_inc(c_g, 1)
                    if later or k > 0:
                        add_out(s, b if c > 0 else 1 - b, k - 1, (c - 1) % NT, 1 - u)
                    if later or k > 1:
                        ln3_apply(k - 2, (c - 2) % NT)
                    if nxt:
                        project(c, nxt, 1)

            for j in range(NT):
                for part in range(2):
                    project(j, (0, 0, 0), part)
            for_groups(step)(dve)
            last = NT * GROUPS - 1
            g_lo(last, 1)
            add_out(GROUPS - 1, 1, last, NT - 1, 1)
            ln3_apply(last - 1, NT - 2)
            ln3_apply(last, NT - 1)

            for half in range(2):
                dve.wait_ge(c_x3st[half], 16 * GROUPS + 16)

            def x3_lo(g):
                for k in range(KT):
                    dve.wait_ge(d_th, KT * g + k + 1)
                    lo_part(dt_l[:, k], ps_t[k][:], dt_h[:, k]).then_inc(d_tl, 1)

            def compare(m, mb, i):
                one, to, count = PAIRS[i]
                dve.wait_ge(d_abs, RANK * (m + 1))
                dve.tensor_tensor(beats[:, to:to + count], dab[:, mb, one:one + 1].broadcast_to([P, count, TOK]),
                                  dab[:, mb, one + 1:], ALU.is_ge).then_inc(d_cmp, 1)

            def add_ranks(m):
                dve.wait_ge(d_cmp, len(PAIRS) * (m + 1))
                dve.tensor_tensor(rank[:, 0:2], beats[:, 1:4:2], beats[:, 2:5:2], ALU.add).then_inc(d_add, 1)
                dve.wait_ge(d_add, 3 * m + 1)
                dve.tensor_tensor(rank[:, 0], rank[:, 0], beats[:, 0], ALU.add).then_inc(d_add, 1)
                dve.tensor_tensor(rank[:, 1], rank[:, 1], beats[:, 0], ALU.subtract).then_inc(d_add, 1)

            def keep(m, mb, r):
                if r < 2:
                    dve.wait_ge(d_add, 3 * m + 2 + r)
                else:
                    dve.wait_ge(d_padd, 4 * m + 1 + r)
                value, op = KEEP[r]
                dve.scalar_tensor_tensor(dab[:, mb, r], rank[:, r], value, dh[:, mb, r], op, ALU.mult).then_inc(d_sel, 1)

            def sparsify(m, mb, part):
                if part == 0:
                    compare(m, mb, 0)
                if part == 1:
                    compare(m, mb, 1)
                    compare(m, mb, 2)
                if part == 2:
                    add_ranks(m)
                    keep(m, mb, 0)
                    keep(m, mb, 1)
                if part == 3:
                    keep(m, mb, 2)
                    keep(m, mb, 3)

            def add_x3(g):
                dve.wait_ge(d_down, g + 1)
                if not isinstance(g, int) or g > 0:
                    dve.wait_ge(d_st, 16 * g + 16)
                for t in range(NT):
                    dve.tensor_tensor(dy[:, t], down_tile[t], res[:, g & RES - 1, t], ALU.add).then_inc(d_y, 1)

            def out_stats(g):
                dve.wait_ge(d_y, NT * (g + 1) + 1)
                stats(g, [dy[:, t] for t in range(NT)], st6, mv, d_ln)

            def normalise(g):
                dve.wait_ge(d_lnr, 2 * (g + 1))
                for t in range(NT):
                    dve.tensor_scalar(dy[:, t], dy[:, t], mv[:, t, 0:1], rstd[:, t:t + 1], ALU.subtract,
                                      ALU.mult).then_inc(d_out, 1)

            def unit(m, mb, back, done=None, front=None):
                for r in range(RANK):
                    if done is not None:
                        if r == 0:
                            add_x3(done)
                        if r == 1:
                            out_stats(done)
                        if r == 3:
                            normalise(done)
                    if back:
                        sparsify(m - 1, 1 - mb, r)
                    dve.wait_ge(d_silu, RANK * m + r + 1)
                    dve.wait_ge(d_up, RANK * m + r + 1)
                    dve.tensor_tensor(dh[:, mb, r], dg[:, r % 2], ps_up[r % 2][:], ALU.mult).then_inc(d_mul, 1)
                    if front is not None and r == RANK - 1:
                        x3_lo(front)

            x3_lo(0)
            for g in range(2):
                unit(MB * g, 0, g > 0)
                unit(MB * g + 1, 1, True, front=g + 1)
            with dve.Fori(2, GROUPS - 1) as g:
                unit(MB * g, 0, True, done=g - 2)
                unit(MB * g + 1, 1, True, front=g + 1)
            unit(MB * GROUPS - 2, 0, True, done=GROUPS - 3)
            unit(MB * GROUPS - 1, 1, True)
            add_x3(GROUPS - 2)
            for r in range(RANK):
                sparsify(MB * GROUPS - 1, 1, r)
            out_stats(GROUPS - 2)
            normalise(GROUPS - 2)
            add_x3(GROUPS - 1)
            out_stats(GROUPS - 1)
            normalise(GROUPS - 1)

        @block.tensor
        def _(pe):
            pe.wait_ge(s_const, 11)
            pe.sem_inc(s_xs_free, 2)
            for b in range(BATCH):
                if b > 0:
                    pe.wait_ge(s_sc_free, b)
                for i in range(2):
                    pe.matmul(ps_gate[i][:], zero_bf[:, 0:P], zero_bf[:], start=True, stop=False, skip_group_check=True)
                with pe.Fori(0, GPB // 2) as h:
                    for u in range(2):
                        f = GPB * b + 2 * h + u
                        pe.wait_ge(s_xs_lo, f + 1)
                        for t in range(NT):
                            for i in range(2):
                                mm = pe.matmul(ps_gate[i][:], xs[:, u, t, i * P:i * P + P], xs[:, u, t],
                                               start=False, stop=False, skip_group_check=True)
                        mm.then_inc(s_xs_free, 1)
                pe.matmul(ps_gate[0][:], zero_bf[:, 0:P], zero_bf[:], start=False, stop=True, skip_group_check=True)
                pe.matmul(ps_gate[1][:], zero_bf[:, 0:P], zero_bf[:], start=False, stop=True,
                          skip_group_check=True).then_inc(s_sc_mm, 1)
                pe.wait_ge(s_sma, 5 * b + 2)
                for i in range(2):
                    for k in range(KT):
                        mm = pe.transpose(ps_t[0][:, i * H + k * P:i * H + k * P + P], s_hl[:, k, i * P:i * P + P], ident)
                mm.then_inc(s_smt, 1)
                pe.wait_ge(s_sm, 6 * b + 6)
                for k in range(KT):
                    for i in range(2):
                        mm = pe.transpose(ps_t[1][:, k * H + i * P:k * H + i * P + P], s_hl[:, i, k * P:k * P + P], ident)
                mm.then_inc(s_smt, 1)
            pe.wait_ge(s_sc_free, BATCH)

            ctx_tile = [ps_t[t // 2][:, t % 2 * H:t % 2 * H + H] for t in range(NT)]
            down_tile = [ps_down[t // 2][:, t % 2 * H:t % 2 * H + H] for t in range(NT)]

            def x_transpose(f):
                pe.wait_ge(s_xg, 16 * (f + 1))
                pe.wait_ge(s_at_lo, KT * f)
                for k in range(KT):
                    for t in range(NT):
                        mm = pe.transpose(ps_t[k][:, t * P:t * P + P], xg[:, 0, t, k * P:k * P + P], ident)
                    mm.then_inc(s_xt_t, 1)

            def context(f, b):
                pe.wait_ge(s_xt_lo, KT * (f + 1))
                for t in range(NT):
                    for k in range(KT):
                        mm = exact3(pe, ctx_tile[t], xt_h[:, k, t * P:t * P + P], xt_l[:, k, t * P:t * P + P],
                                    soft_wt[:, b, 0, k * H:k * H + H], soft_wt[:, b, 1, k * H:k * H + H],
                                    start=k == 0, stop=k == KT - 1)
                    mm.then_inc(s_ctx, 1)

            def x1_transpose(f):
                pe.wait_ge(s_x1, NT * (f + 1))
                for k in range(KT):
                    for t in range(NT):
                        mm = pe.transpose(ps_t[k][:, t * P:t * P + P],
                                          x1[:, t].rearrange("p (m k) -> p k m", k=KT)[:, k], ident)
                    mm.then_inc(s_at_t, 1)

            def gate_or_up(ps, which, g, n):
                piece, col = 3 * (n // 4) + which, n % 4 * P
                for k in range(KT):
                    if which == 0 and n == 0:
                        pe.wait_ge(s_at_lo, KT * g + k + 1)
                    mm = exact3(pe, ps[n % 2][:], w0_hi[:, piece, k, col:col + P], w0_lo[:, piece, k, col:col + P],
                                at_h[:, k], at_l[:, k], start=k == 0, stop=k == KT - 1)
                return mm

            def down(g, n):
                pe.wait_ge(s_hlo, NB0 * g + n + 1)
                if n == 0:
                    pe.wait_ge(s_y, NT * g + 1)
                piece, nib, col = 3 * (n // 4) + 2, n % 2, n // 2 % 2 * H
                for t in range(NT):
                    mm = exact3(pe, down_tile[t], hh[:, n % 2, t * P:t * P + P], hl[:, n % 2, t * P:t * P + P],
                                w0_hi[:, piece, nib, col:col + H], w0_lo[:, piece, nib, col:col + H],
                                start=n == 0 and t % 2 == 0, stop=n == NB0 - 1, skip_group_check=True)
                if n == NB0 - 1:
                    mm.then_inc(s_down, 1)

            def group(g, before, more, b=0):
                for n in range(NB0):
                    if n > 1:
                        down(g, n - 2)
                    elif before:
                        down(g - 1, NB0 - 2 + n)
                    if n % 4 == 0:
                        pe.wait_ge(s_wlo, 6 * (n // 4 + 1) + 4)
                    gate_or_up(ps_gate, 0, g, n).then_inc(s_gate, 1)
                    gate_or_up(ps_up, 1, g, n).then_inc(s_up, 1)
                    if more and n == 1:
                        x_transpose(g + 1)
                    if more and n == 4:
                        context(g + 1, b)
                    if more and n == 9:
                        x1_transpose(g + 1)

            x_transpose(0)
            context(0, 0)
            x1_transpose(0)
            group(0, False, True)
            for b in range(BATCH):
                with pe.Fori(max(b * GPB, 1), (b + 1) * GPB - 1) as g:
                    group(g, True, True, b)
                if b < BATCH - 1:
                    group((b + 1) * GPB - 1, True, True, b + 1)
            group(GROUPS - 1, True, False)
            down(GROUPS - 1, NB0 - 2)
            down(GROUPS - 1, NB0 - 1)

            pe.wait_ge(c_wch, 4)
            pe.wait_ge(s_x2st, 16 * GROUPS + 16)

            def in_proj(n, j):
                cols = slice(D_INNER + j * P, D_INNER + (j + 1) * P)
                for k in range(KT):
                    mm = exact3(pe, ring(XBC0 + j)[:], win_h[:, k, cols], win_l[:, k, cols], xt_h[:, k], xt_l[:, k],
                                start=k == 0, stop=k == KT - 1)
                mm.then_inc(c_xbc, 1)

            def tok_proj(ps, t, cols):
                for k in range(KT):
                    mm = exact3(pe, ps, xt_h[:, k, t * P:(t + 1) * P], xt_l[:, k, t * P:(t + 1) * P],
                                win_h[:, k, cols], win_l[:, k, cols], start=k == 0, stop=k == KT - 1)
                return mm

            def z_proj(n, t):
                if t < 2:
                    pe.wait_ge(c_xin, XB * n + 4 + t)
                else:
                    pe.wait_ge(c_e, NT * n + t + 1)
                tok_proj(z_place(t)[:], t, slice(0, D_INNER)).then_inc(c_zp, 1)

            def decay_sums(n):
                pe.wait_ge(c_zs, NT * n + 1)
                pe.wait_ge(c_dtc, DT_STEPS * (n + 1))
                flat = adt[:].rearrange("p t h -> p (t h)")
                pe.matmul(ring(ACS0)[:, 0:16], upto[:], flat, start=True, stop=True)
                pe.matmul(ring(ACS0)[0:D_STATE, 16:32], ones[:], flat, start=True, stop=True).then_inc(c_acs, 1)

            def segment_sums(n, t):
                if t == 0:
                    pe.wait_ge(c_zs, NT * n + 2)
                elif t == 1:
                    pe.wait_ge(c_ea, 2 * (n + 1))
                else:
                    pe.wait_ge(c_e, NT * n + t - 1)
                pe.wait_ge(c_au, NT * n + t + 1)
                pe.matmul(ring(SEG0 + t)[:], below[:], au[:, t % 2].rearrange("p h l -> p (h l)"),
                          start=True, stop=True).then_inc(c_seg, 1)

            def in_proj_at(n, j):
                if j == 1:
                    pe.wait_ge(c_dtc, DT_STEPS * n + 1)
                if j > 1:
                    pe.wait_ge(c_xin, XB * n + j - 1)
                in_proj(n, j)

            def project(slot, nxt, part):
                n, b, i = nxt
                if slot == 0 and part == 0:
                    pe.wait_ge(c_xg[b], 16 * (i + 1))
                    pe.wait_ge(c_zs, NT * n)
                    for k in range(KT):
                        for t in range(NT):
                            mm = pe.transpose(ring(k)[:, t * P:(t + 1) * P], xg[:, b, t, k * P:(k + 1) * P], ident)
                        mm.then_inc(c_t, 1)
                if slot == 0 and part == 1:
                    dt_proj(nxt)
                    in_proj_at(n, 0)
                    in_proj_at(n, 1)
                if slot == 1:
                    for j in (2, 3) if part == 0 else (4,):
                        in_proj_at(n, j)
                if slot == 2 and part == 0:
                    z_proj(n, 0)
                if slot == 2 and part == 1:
                    z_proj(n, 1)
                    decay_sums(n)
                    segment_sums(n, 0)
                if slot == 3 and part == 0:
                    segment_sums(n, 1)
                    segment_sums(n, 2)
                if slot == 3 and part == 1:
                    segment_sums(n, 3)
                    z_proj(n, 2)
                    z_proj(n, 3)

            def dt_proj(nxt):
                n, b, i = nxt
                pe.wait_ge(c_xtl, KT * (n + 1))
                for t in range(NT):
                    mm = tok_proj(ring(DT0)[:, t * HEADS:(t + 1) * HEADS], t, slice(D_IN - HEADS, D_IN))
                mm.then_inc(c_dtp, 1)

            def g_transpose(k, u):
                pe.wait_ge(c_g, k + 1)
                pe.wait_ge(c_y3, k + 1)
                for h in range(HEADS):
                    mm = pe.transpose(ps_g[:, h * P:(h + 1) * P], gg[:, u, h * P:(h + 1) * P], ident)
                mm.then_inc(c_gT, 1)

            def out_proj(k, u):
                pe.wait_ge(c_gtl, k + 1)
                for h in range(HEADS):
                    mm = exact3(pe, ps_g[:, 0:H], gt_h[:, u, h], gt_l[:, u, h], wo_h[:, h], wo_l[:, h],
                                start=h == 0, stop=h == HEADS - 1)
                mm.then_inc(c_o, 1)

            def step(s, b, i, nxt):
                for c in range(NT):
                    k, u, cols = NT * s + c, c % 2, slice(c * P, (c + 1) * P)
                    before = not isinstance(k, int) or k > 0
                    if c == 0:
                        pe.wait_ge(c_silu, XB * (s + 1))
                        pe.wait_ge(c_ct, s + 1)
                    pe.wait_ge(c_xtk, k + 1)
                    for h in range(HEADS):
                        mm = pe.transpose(ps_x[:, h * P:(h + 1) * P], xc[:, b, h, cols], ident)
                    mm.then_inc(c_tr, 1)
                    pe.wait_ge(c_gm, k + 1)
                    pe.wait_ge(c_btk, k + 1)
                    pe.matmul(small[:, P:2 * P], bc[0:D_STATE, b, cols], ct[:, b, cols], start=True, stop=True)
                    pe.transpose(small[:, 0:D_STATE], bc[0:D_STATE, b, cols],
                                 wide_i[0:D_STATE, P:P + D_STATE]).then_inc(c_G, 1)
                    if before:
                        g_transpose(k - 1, 1 - u)
                    pe.wait_ge(c_st, k + 1)
                    pe.wait_ge(c_yo, k + 1)
                    pe.matmul(ps_yoff[:], ct[:, b, cols], state[:, b].rearrange("p h d -> p (h d)"),
                              start=True, stop=True).then_inc(c_yoff, 1)
                    if nxt:
                        project(c, nxt, 0)
                    pe.wait_ge(c_xdc, k + 1)
                    pe.wait_ge(c_btk, k + 1 + 1)
                    pe.matmul(ps_ds[0:D_STATE, :], btk[:, u], xdc[:, u].rearrange("p h d -> p (h d)"),
                              start=True, stop=True).then_inc(c_ds, 1)
                    pe.wait_ge(c_m, k + 1)
                    pe.wait_ge(c_xsd, k + 1)
                    pe.wait_ge(c_g1, k + 1)
                    for h in range(HEADS):
                        mm = pe.matmul(ps_y[:, h * HEADDIM:(h + 1) * HEADDIM], mm_[:, u, h], xsd[:, u, h],
                                       start=True, stop=True)
                    mm.then_inc(c_y, 1)
                    if before:
                        out_proj(k - 1, 1 - u)
                    if nxt:
                        project(c, nxt, 1)

            for j in range(NT):
                for part in range(2):
                    project(j, (0, 0, 0), part)
            for_groups(step)(pe)
            g_transpose(NT * GROUPS - 1, 1)
            out_proj(NT * GROUPS - 1, 1)

            for half in range(2):
                pe.wait_ge(c_x3st[half], 16 * GROUPS + 16)
            pe.wait_ge(c_w1l, GROUPS)
            w1h, w1l = (w[:].rearrange("p a b -> p (a b)") for w in (w1_h, w1_l))

            def x3_transpose(g):
                pe.wait_ge(d_x, 16 * (g + 1))
                pe.wait_ge(d_tl, KT * g)
                for k in range(KT):
                    for t in range(NT):
                        mm = pe.transpose(ps_t[k][:, t * P:(t + 1) * P], xg[:, 0, t, k * P:(k + 1) * P], ident)
                    mm.then_inc(d_t, 1)

            def down1(m, mb, r, g):
                pe.wait_ge(d_lo, RANK * m + r + 1)
                if mb == 0 and r == 0:
                    pe.wait_ge(d_y, NT * g + 1)
                at = 2 * KT * MLP1 + (mb * RANK + r) * H
                for t in range(NT):
                    mm = exact3(pe, down_tile[t], dhh[:, mb, r, t * P:(t + 1) * P], dhl[:, mb, r, t * P:(t + 1) * P],
                                w1h[:, at:at + H], w1l[:, at:at + H], start=mb == 0 and r == 0 and t % 2 == 0,
                                stop=mb == MB - 1 and r == RANK - 1, skip_group_check=True)
                if mb == MB - 1 and r == RANK - 1:
                    mm.then_inc(d_down, 1)

            def unit(m, mb, g, downs=True, front=None):
                for r in range(RANK):
                    if not isinstance(m, int) or m > 0 or r > 1:
                        pe.wait_ge(d_mul, RANK * m + r - 1)
                    for which, ps, s_ in ((0, ps_gate, d_gate), (1, ps_up, d_up)):
                        for k in range(KT):
                            if which == 0 and mb == 0 and r == 0:
                                pe.wait_ge(d_tl, KT * g + k + 1)
                            at = ((which * MB + mb) * RANK + r) * KT * P + k * P
                            mm = exact3(pe, ps[r % 2][:], w1h[:, at:at + P], w1l[:, at:at + P], dt_h[:, k], dt_l[:, k],
                                        start=k == 0, stop=k == KT - 1)
                        mm.then_inc(s_, 1)
                    if r == 1 and front is not None:
                        x3_transpose(front)
                    if downs:
                        down1(m - 2, mb, r, g - 1)

            x3_transpose(0)
            for m in range(2 * MB):
                unit(m, m % MB, m // MB, downs=m >= MB, front=m // MB + 1 if m % MB else None)
            with pe.Fori(2, GROUPS - 1) as g:
                unit(MB * g, 0, g)
                unit(MB * g + 1, 1, g, front=g + 1)
            unit(MB * GROUPS - 2, 0, GROUPS - 1)
            unit(MB * GROUPS - 1, 1, GROUPS - 1)
            for m in range(MB * GROUPS - 2, MB * GROUPS):
                for r in range(RANK):
                    down1(m, m % MB, r, GROUPS - 1)


_INS = ["x", "codes", "scales", "w_in", "conv_w", "conv_b", "dt_bias", "a_log", "d_skip", "norm_w", "w_out",
        "w_mlp1"]


def layout(i):
    import numpy as np

    def by_block(a):
        return a.reshape(a.shape[0], 8, P, 2).transpose(0, 1, 3, 2).reshape(a.shape[0], 4, 512)

    g, u = (by_block(i[f"L0_ffn_{n}_W_packed"].T) for n in ("gate", "up"))
    gs, us = (by_block(i[f"L0_ffn_{n}_scales"].T) for n in ("gate", "up"))
    d = i["L0_ffn_down_W_packed"].T.reshape(4, 2, P, H).transpose(2, 0, 1, 3).reshape(P, 4, 512)
    ds = i["L0_ffn_down_scales"].T.reshape(4, 2, 8, H).transpose(2, 0, 1, 3).reshape(8, 4, 512)
    return {
        "x": i["L0_attn_x"].reshape(T, H),
        "codes": np.stack([g, u, d], 2).reshape(P, JOBS, 512).transpose(1, 0, 2),
        "scales": np.stack([gs, us, ds], 2).reshape(8, JOBS, 512).transpose(1, 0, 2),
        "w_in": i["L1_attn_W_in"].T.reshape(KT, P, D_IN).transpose(1, 0, 2),
        "conv_w": i["L1_attn_W_conv"].reshape(XB, P, TAPS).transpose(1, 0, 2),
        "conv_b": i["L1_attn_b_conv"].reshape(XB, P).T,
        "dt_bias": i["L1_attn_dt_bias"].reshape(1, HEADS),
        "a_log": i["L1_attn_A_log"].reshape(1, HEADS),
        "d_skip": i["L1_attn_D"].reshape(1, HEADS),
        "norm_w": i["L1_attn_norm_w"].reshape(HEADS, HEADDIM).T,
        "w_out": i["L1_attn_W_out"].T.reshape(HEADS, HEADDIM, H).transpose(1, 0, 2),
        "w_mlp1": np.concatenate(
            [i[f"L1_ffn_w_{n}"].reshape(KT, P, MB, P, RANK).transpose(1, 2, 4, 0, 3).reshape(P, -1) for n in ("gate", "up")]
            + [i["L1_ffn_w_down"].reshape(MB, P, RANK, H).transpose(1, 0, 2, 3).reshape(P, -1)], 1)
        .reshape(P, GROUPS, -1).transpose(1, 0, 2),
    }


def kernel(**inputs):
    import numpy as np
    import concourse.bacc as bacc
    from concourse.bass_utils import run_bass_kernel_spmd

    nc = bacc.Bacc("TRN2", target_bir_lowering=False, num_devices=1)
    laid = layout({k: np.asarray(v) for k, v in inputs.items()})
    arrays, args = {}, []
    for name in _INS:
        a = np.ascontiguousarray(laid[name])
        arrays[f"in_{name}"] = a
        args.append(nc.dram_tensor(f"in_{name}", a.shape, mybir.dt.from_np(a.dtype), kind="ExternalInput").ap())
    args.append(nc.dram_tensor("out_0", (T, H), F32, kind="ExternalOutput").ap())
    build(nc, *args)
    r = run_bass_kernel_spmd(nc, [arrays], core_ids=[0])
    return r.results[0]["out_0"].reshape(BATCH, SEQ, H)
```

```python
from contextlib import ExitStack

import concourse.bass as bass
from concourse import mybir

ALU = mybir.AluOpType
ACT = mybir.ActivationFunctionType
F32 = mybir.dt.float32
F32R = mybir.dt.float32r
BF16 = mybir.dt.bfloat16
I32 = mybir.dt.int32
AX_X = mybir.AxisListType.X

P = 128
BATCH, SEQ, H = 2, 2048, 256
T = BATCH * SEQ
TOK = 512
NT = TOK // P
GROUPS = T // TOK
GPB = GROUPS // BATCH
KT = H // P
EPS = 1e-5

MLP0 = 2048
NB0 = MLP0 // P
JOBS = 12

D_INNER, D_STATE, HEADS, HEADDIM, TAPS = 512, 64, 4, 128, 4
CONV_DIM = D_INNER + 2 * D_STATE
D_IN = 2 * D_INNER + 2 * D_STATE + HEADS
XB = CONV_DIM // P

MLP1 = 1024
RANK = 4
MB = MLP1 // RANK // P
DT_STEPS = 11
DT0, XBC0, Z0, ACS0, SEG0 = 2, 3, 8, 10, 11
RES = 4
W1_PIECE = 3 * KT * MLP1 // GROUPS


def exact3(pe, out, w_hi, w_lo, m_hi, m_lo, start, stop, **kw):
    pe.matmul(out, w_hi, m_lo, start=start, stop=False, **kw)
    pe.matmul(out, w_lo, m_hi, start=False, stop=False, **kw)
    return pe.matmul(out, w_hi, m_hi, start=False, stop=stop, **kw)


def build(nc, x_in, codes, scales, w_in, conv_w, conv_b, dt_bias, a_log, d_skip, norm_w, w_out, w_mlp1, out):
    ctx = ExitStack()
    with ctx:
        def sb(name, shape, dt, stack=ctx):
            return stack.enter_context(nc.sbuf_tensor(name, shape, dt))

        def sem(name):
            return ctx.enter_context(nc.semaphore(name))

        x2_dram = nc.dram_tensor("x2_scratch", (T, H), F32, kind="Internal").ap()
        x3_dram = nc.dram_tensor("x3_scratch", (T, H), F32, kind="Internal").ap()

        bank = [ctx.enter_context(nc.psum_tensor(f"bank{i}", [P, 512], F32)) for i in range(8)]
        ps_gate, ps_up, ps_down, ps_t = bank[0:2], bank[2:4], bank[4:6], bank[6:8]
        small, ps_x, ps_y, ps_yoff, ps_ds, ps_g = bank[2:8]

        def ring(i):
            return bank[i % 2]

        X2_AT, XBC_AT = 6, 9

        def early(i):
            return ps_t[i % 2]

        def z_place(t):
            return ring((Z0, Z0 + 1, SEG0 + 4, SEG0 + 5)[t])

        wide_i = sb("wide_i", [P, 3 * P], F32)
        ident = wide_i[:, P:2 * P]
        m_half = sb("m_half", [P, NT], F32)
        eps4 = sb("eps4", [P, NT], F32)

        upto = sb("upto", [P, P], F32)
        below = sb("below", [P, P], F32)
        ones = sb("ones", [P, D_STATE], F32)
        eps_rms = sb("eps_rms", [P, 1], F32)
        cw = sb("cw", [P, XB, TAPS], F32)
        cb = sb("cb", [P, XB], F32)
        dtb = sb("dtb", [P, HEADS], F32)
        a4 = sb("a4", [P, HEADS], F32)
        d4 = sb("d4", [P, HEADS], F32)
        nw = sb("nw", [P, HEADS], F32)

        win_h = sb("win_h", [P, KT, D_IN], F32R)
        win_l = sb("win_l", [P, KT, D_IN], F32R)
        wo_h = sb("wo_h", [P, HEADS, H], F32R)
        wo_l = sb("wo_l", [P, HEADS, H], F32R)

        xg = sb("xg", [P, 2, NT, H], F32)
        xt_h = sb("xt_h", [P, KT, TOK], F32R)
        xt_l = sb("xt_l", [P, KT, TOK], F32R)
        xo = y3 = dy = sb("rows_out", [P, NT, H], F32)
        st6 = sb("st6", [P, NT, 6], F32)
        mv = sb("mv", [P, NT, 2], F32)
        ve = sb("ve", [P, NT], F32)
        rstd = sb("rstd", [P, NT], F32)
        st6b = sb("st6b", [P, NT, 6], F32)
        mvb = sb("mvb", [P, NT, 2], F32)
        veb = sb("veb", [P, NT], F32)
        rstdb = sb("rstdb", [P, NT], F32)

        mlp0 = ExitStack()
        w0_hi = sb("w0_hi", [P, JOBS, 2, 512], F32R, mlp0)
        w0_lo = sb("w0_lo", [P, JOBS, 2, 512], F32R, mlp0)
        soft_wt = sb("soft_wt", [P, BATCH, 2, KT * H], F32R, mlp0)
        win_raw = sb("win_raw", [P, KT, D_IN], F32, mlp0)
        wo_raw = sb("wo_raw", [P, HEADS, H], F32, mlp0)
        phase_a = ExitStack()
        xs = sb("xs", [P, 2, NT, 2 * H], F32R, phase_a)
        wq = sb("wq", [P, 2, 512], I32, phase_a)
        zero_bf = sb("zero_bf", [P, 512], BF16, phase_a)
        sc = sb("sc", [P, 2, 512], F32, phase_a)
        mag = sb("mag", [P, 2, 512], I32, phase_a)
        wf = sb("wf", [P, 2, 2, 512], F32, phase_a)
        s_hl, s_full = xo[:, 0:2], xo[:, 2:4]
        nmax = sb("nmax", [P, 2], F32, phase_a)
        rsum = sb("rsum", [P, 2], F32, phase_a)
        rinv = sb("rinv", [P, 2], F32, phase_a)
        phase_a.close()

        phase_b = ExitStack()
        x1 = sb("x1", [P, NT, H], F32, phase_b)
        x1_res = sb("x1_res", [P, NT, H], F32, phase_b)
        at_h = sb("at_h", [P, KT, TOK], F32R, phase_b)
        at_l = sb("at_l", [P, KT, TOK], F32R, phase_b)
        gl = sb("gl", [P, 2, TOK], F32, phase_b)
        hb = sb("hb", [P, 2, TOK], F32, phase_b)
        hh = sb("hh", [P, 2, TOK], F32R, phase_b)
        hl = sb("hl", [P, 2, TOK], F32R, phase_b)
        yb = sb("yb", [P, NT, H], F32, phase_b)
        phase_b.close()
        mlp0.close()

        w1_h = sb("w1_h", [P, GROUPS, W1_PIECE], F32R)
        w1_l = sb("w1_l", [P, GROUPS, W1_PIECE], F32R)
        phase_c = ExitStack()

        def cs(name, shape, dt=F32):
            return sb(name, shape, dt, phase_c)

        raw = cs("raw", [P, XB, TAPS - 1 + TOK])
        acc = cs("acc", [P, 2, TOK])
        xc = cs("xc", [P, 2, HEADS, TOK])
        w1_raw = cs("w1_raw", [P, W1_PIECE])
        tail = cs("tail", [P, BATCH, XB, TAPS - 1])
        bc = cs("bc", [P, 2, TOK])
        ct = cs("ct", [D_STATE, 2, TOK])
        zs = cs("zs", [P, NT, D_INNER])
        ee = cs("ee", [P, NT, HEADS, P])
        d0 = cs("d0", [P, NT, HEADS])
        dax = cs("dax", [P, NT * HEADS])
        de = cs("de", [P, NT * HEADS])
        du = cs("du", [P, NT * HEADS])
        dl = cs("dl", [P, NT * HEADS])
        um = cs("um", [P, NT * HEADS])
        dl2 = cs("dl2", [P, NT * HEADS])
        drec = cs("drec", [P, NT * HEADS])
        dm1 = cs("dm1", [P, NT * HEADS])
        dm2 = cs("dm2", [P, NT * HEADS])
        dden = cs("dden", [P, NT * HEADS])
        dtv = cs("dtv", [P, 2, NT, HEADS])
        adt = cs("adt", [P, NT, HEADS])
        ea = cs("ea", [P, 2, NT, HEADS])
        et = cs("et", [D_STATE, 2, NT, HEADS])
        au = cs("au", [P, NT, HEADS, P])
        gm = cs("gm", [P, 2, P])
        mm_ = cs("mm_", [P, 2, HEADS, P])
        xtk = cs("xtk", [P, 2, HEADS, HEADDIM])
        btk = cs("btk", [P, 2, D_STATE])
        xsd = cs("xsd", [P, 2, HEADS, HEADDIM])
        xdc = cs("xdc", [P, 2, HEADS, HEADDIM])
        xd = cs("xd", [P, 2, HEADS, HEADDIM])
        yo = cs("yo", [P, 2, HEADS, HEADDIM])
        gg = cs("gg", [P, 2, D_INNER])
        ss = cs("ss", [P, 2])
        rr = cs("rr", [P, 2])
        gt_h = cs("gt_h", [P, 2, HEADS, P], F32R)
        gt_l = cs("gt_l", [P, 2, HEADS, P], F32R)
        state = cs("state", [D_STATE, BATCH, HEADS, HEADDIM])
        rest = cs("rest", [P, 2, H])
        phase_c.close()

        phase_d = ExitStack()

        def ds(name, shape, dt=F32):
            return sb(name, shape, dt, phase_d)

        dg = ds("dg", [P, 2, TOK])
        dh = ds("dh", [P, MB, RANK, TOK])
        dab = ds("dab", [P, MB, RANK, TOK])
        beats = ds("beats", [P, 6, TOK], BF16)
        rank = ds("rank", [P, RANK, TOK], BF16)
        dhh = ds("dhh", [P, MB, RANK, TOK], F32R)
        dhl = ds("dhl", [P, MB, RANK, TOK], F32R)
        res = ds("res", [P, RES, NT, H])
        phase_d.close()

        s_const = sem("constants_ready")
        s_x = [sem(f"x_loaded{i}") for i in range(2)]
        s_w = [sem(f"codes_loaded{i}") for i in range(2)]
        s_xs_free = sem("xs_free")
        s_xs_hi = sem("xs_hi_ready")
        s_xs_lo = sem("xs_lo_ready")
        s_sc_mm = sem("scores_done")
        s_sc_free = sem("scores_psum_free")
        s_sm = sem("softmax_steps_dve")
        s_sma = sem("softmax_steps_act")
        s_smt = sem("softmax_transposed")
        s_deq = sem("dequant_steps_dve")
        s_wf = sem("weights_f32_ready")
        s_whi = sem("weights_hi_ready")
        s_wlo = sem("weights_lo_ready")
        s_xg = sem("front_x_loaded")
        s_xt_t = sem("x_transposed")
        s_xt_hi = sem("xt_hi_ready")
        s_xt_lo = sem("xt_lo_ready")
        s_ctx = sem("context_done")
        s_seen = sem("stats_seen")
        s_ln1 = sem("ln1_stats")
        s_ln1r = sem("ln1_rstd")
        s_x1 = sem("x1_ready")
        s_x1r = sem("x1_residual_kept")
        s_at_t = sem("x1_transposed")
        s_at_hi = sem("at_hi_ready")
        s_at_lo = sem("at_lo_ready")
        s_gate = sem("gate_done")
        s_up = sem("up_done")
        s_gelu = sem("gelu_done")
        s_h = sem("h_ready")
        s_hhi = sem("h_hi_ready")
        s_hlo = sem("h_lo_ready")
        s_down = sem("down_done")
        s_y = sem("y_ready")
        s_ln2 = sem("ln2_stats")
        s_ln2r = sem("ln2_rstd")
        s_x2 = sem("x2_ready")
        s_x2st = sem("x2_stored")
        c_wc_raw = sem("ssm_weights_loaded")
        c_wch = sem("ssm_weights_hi")
        c_wcs = sem("ssm_weights_scaled")
        c_small = sem("ssm_constants_loaded")
        c_a4 = sem("decay_rate_ready")
        c_t = sem("x2_transposed")
        c_xth = sem("x2t_hi_ready")
        c_xtl = sem("x2t_lo_ready")
        c_dtp = sem("dt_projected")
        c_dtc = sem("dt_steps_dve")
        c_dta = sem("dt_steps_act")
        c_acs = sem("decay_sums_done")
        c_ea = sem("decays_ready")
        c_au = sem("masked_decay_ready")
        c_seg = sem("segment_sums_done")
        c_e = sem("segment_decay_ready")
        c_zp = sem("z_projected")
        c_zs = sem("z_gate_ready")
        c_xbc = sem("xbc_projected")
        c_xin = sem("xbc_copied")
        c_halo = sem("halo_copied")
        c_cv = sem("conv_steps")
        c_silu = sem("conv_silu_ready")
        c_ct = sem("c_moved")
        c_w1h = sem("mlp1_hi_ready")
        c_w1l = sem("mlp1_lo_ready")
        c_tr = sem("x_token_major")
        c_btk = sem("b_tok_ready")
        c_G = sem("cb_done")
        c_gm = sem("cb_masked")
        c_m = sem("mixing_ready")
        c_xtk = sem("x_tok_ready")
        c_xsd = sem("x_dt_ready")
        c_xdc = sem("x_decayed_ready")
        c_xd = sem("x_skip_ready")
        c_yoff = sem("y_off_done")
        c_y = sem("y_diag_done")
        c_ds = sem("state_add_done")
        c_st = sem("state_ready")
        c_yo = sem("y_off_scaled")
        c_yo2 = sem("y_off_skip_ready")
        c_g1 = sem("y_ready_ssm")
        c_g = sem("g_ready")
        c_ss = sem("g_square_sum")
        c_rr = sem("g_inv_rms")
        c_gT = sem("g_transposed")
        c_gth = sem("gt_hi_ready")
        c_gtl = sem("gt_lo_ready")
        c_o = sem("projected_out")
        c_rest = sem("x2_rest_kept")
        c_y3 = sem("y3_ready")
        c_ln3 = sem("ln3_stats")
        c_ln3r = sem("ln3_rstd")
        c_x3 = sem("x3_ready")
        c_x3st = [sem(f"x3_stored{i}") for i in range(2)]
        c_xg = [sem(f"x2_loaded{i}") for i in range(2)]
        c_w1r = sem("mlp1_piece_loaded")
        c_init = sem("ssm_memory_cleared")
        d_x = sem("x3_loaded")
        d_res = sem("x3_residual_kept")
        d_t = sem("x3_transposed")
        d_th = sem("x3t_hi_ready")
        d_tl = sem("x3t_lo_ready")
        d_gate = sem("mlp1_gate_done")
        d_up = sem("mlp1_up_done")
        d_silu = sem("mlp1_silu_ready")
        d_mul = sem("mlp1_gated_ready")
        d_abs = sem("mlp1_abs_ready")
        d_cmp = sem("pairs_compared")
        d_add = sem("ranks_dve")
        d_padd = sem("ranks_pool")
        d_sel = sem("kept_ready")
        d_hi = sem("kept_hi_ready")
        d_lo = sem("kept_lo_ready")
        d_down = sem("mlp1_down_done")
        d_y = sem("mlp1_sum_ready")
        d_ln = sem("ln4_stats")
        d_lnr = sem("ln4_rstd")
        d_out = sem("output_ready")
        d_st = sem("output_stored")

        block = ctx.enter_context(nc.Block())
        x_rows = x_in.rearrange("(g t p) c -> g p t c", p=P, t=NT)
        x2_rows = x2_dram.rearrange("(g t p) c -> g p t c", p=P, t=NT)
        x3_rows = x3_dram.rearrange("(g t p) c -> g p t c", p=P, t=NT)
        out_rows = out.rearrange("(g t p) c -> g p t c", p=P, t=NT)

        PAIRS = [(0, 0, 3), (1, 3, 2), (2, 5, 1)]
        KEEP = [(2.0, ALU.is_ge), (1.0, ALU.is_ge), (0.0, ALU.is_ge), (1.0, ALU.is_le)]

        def for_groups(step):
            def run(eng):
                step(0, 0, 0, (1, 1, 0))
                with eng.Fori(0, GPB - 1) as i:
                    step(2 * i + 1, 1, i, (2 * i + 2, 0, i + 1))
                    step(2 * i + 2, 0, i + 1, (2 * i + 3, 1, i + 1))
                step(GROUPS - 1, 1, GPB - 1, None)
            return run

        FROM_1 = [s_y, c_xtk, c_gm, c_btk, c_yo, c_g1, c_ds, c_y3, c_ss, c_rr, c_yo2, d_y]
        FROM_16 = [s_x2st, d_st, *c_x3st]

        @block.sync
        def _(sp):
            def load_x(f, u):
                sp.dma_start(xg[:, u], x_rows[f]).then_inc(s_x[u], 16)

            def load_codes(j, u):
                sp.dma_start(wq[:, u], codes[j]).then_inc(s_w[u], 16)
                for q in range(8):
                    sp.dma_start(sc[16 * q:16 * q + 16, u], scales[j, q:q + 1].broadcast_to([16, 512])).then_inc(s_w[u], 16)

            for s_ in FROM_1:
                sp.sem_inc(s_, 1)
            for s_ in FROM_16:
                sp.sem_inc(s_, 16)
            for u in range(2):
                load_x(u, u)
                load_codes(u, u)
            with sp.Fori(0, GROUPS // 2 - 1) as h:
                for u in range(2):
                    sp.wait_ge(s_xs_lo, 2 * h + u + 1)
                    load_x(2 * h + u + 2, u)
                    sp.wait_ge(s_wf, 2 * (2 * h + u + 1))
                    load_codes(2 * h + u + 2, u)
            sp.dma_start(win_raw[:], w_in).then_inc(c_wc_raw, 16)
            sp.dma_start(wo_raw[:], w_out).then_inc(c_wc_raw, 16)
            for dst, src in ((cw[:], conv_w), (cb[:], conv_b), (nw[:], norm_w), (dtb[:], dt_bias.broadcast_to([P, HEADS])),
                             (a4[:], a_log.broadcast_to([P, HEADS])), (d4[:], d_skip.broadcast_to([P, HEADS]))):
                sp.dma_start(dst, src).then_inc(c_small, 16)
            for j in range(GROUPS, JOBS):
                sp.wait_ge(s_wf, 2 * (j - 1))
                load_codes(j, j % 2)
                if j == GROUPS:
                    sp.wait_ge(s_xs_lo, GROUPS)
                    sp.dma_start(xg[:, 0], x_rows[0]).then_inc(s_xg, 16)
            def load_front(g):
                sp.wait_ge(s_xt_t, KT * g)
                sp.dma_start(xg[:, 0], x_rows[g]).then_inc(s_xg, 16)

            def store_x2(g):
                sp.wait_ge(s_x2, NT * (g + 1))
                sp.dma_start(x2_rows[g], xo[:]).then_inc(s_x2st, 16)

            load_front(1)
            with sp.Fori(2, GROUPS) as g:
                load_front(g)
                store_x2(g - 2)
            sp.wait_ge(s_xt_t, KT * GROUPS)
            sp.wait_ge(s_x2st, 16 * (GROUPS - 2) + 16)
            for q in range(2):
                sp.dma_start(xg[:, q], x2_rows[q * GPB]).then_inc(c_xg[q], 16)
            store_x2(GROUPS - 2)
            sp.wait_ge(s_down, GROUPS)
            sp.dma_start(w1_raw[:], w_mlp1[0]).then_inc(c_w1r, 16)
            store_x2(GROUPS - 1)
            sp.wait_ge(s_x2st, 16 * GROUPS + 16)

            def store_x3(b, i, half, k):
                sp.wait_ge(c_x3, k + 2)
                sp.dma_start(x3_rows[b * GPB + i, :, 2 * half:2 * half + 2], y3[:, 2 * half:2 * half + 2]).then_inc(c_x3st[half], 16)

            def step(s, b, i, more):
                k = NT * s
                if more:
                    sp.wait_ge(c_rest, s + 1)
                    sp.dma_start(xg[:, b], x2_rows[b * GPB + i + 1]).then_inc(c_xg[b], 16)
                elif b == 0:
                    for half in range(2):
                        sp.wait_ge(c_x3st[half], 16 * s + 16)
                    sp.wait_ge(c_rest, s + 1)
                    sp.dma_start(xg[:, 0], x3_rows[0]).then_inc(d_x, 16)
                store_x3(b, i, 0, k)
                if more or b == 0:
                    sp.wait_ge(c_w1l, s + 1)
                    sp.dma_start(w1_raw[:], w_mlp1[s + 1]).then_inc(c_w1r, 16)
                store_x3(b, i, 1, k + 2)

            with sp.Fori(0, GPB - 1) as i:
                step(2 * i, 0, i, True)
                step(2 * i + 1, 1, i, True)
            step(GROUPS - 2, 0, GPB - 1, False)
            step(GROUPS - 1, 1, GPB - 1, False)
            for half in range(2):
                sp.wait_ge(c_x3st[half], 16 * GROUPS + 16)

            def load_x3(g):
                sp.wait_ge(d_t, KT * g)
                sp.wait_ge(d_res, g)
                sp.dma_start(xg[:, 0], x3_rows[g]).then_inc(d_x, 16)

            def store_out(g):
                sp.wait_ge(d_out, NT * (g + 1))
                sp.dma_start(out_rows[g], dy[:]).then_inc(d_st, 16)

            load_x3(1)
            with sp.Fori(2, GROUPS) as g:
                load_x3(g)
                store_out(g - 2)
            store_out(GROUPS - 2)
            store_out(GROUPS - 1)
            sp.wait_ge(d_st, 16 * GROUPS + 16)

        @block.gpsimd
        def _(pool):
            pool.memset(wide_i[:], 0.0).then_inc(s_const, 1)
            pool.memset(zero_bf[:], 0.0).then_inc(s_const, 1)
            pool.memset(m_half[:], -0.5).then_inc(s_const, 1)
            pool.memset(eps4[:], EPS).then_inc(s_const, 1)
            pool.memset(eps_rms[:], EPS * D_INNER).then_inc(s_const, 1)
            pool.memset(upto[:], 1.0).then_inc(s_const, 1)
            pool.memset(below[:], 1.0).then_inc(s_const, 1)
            pool.memset(ones[:], 1.0).then_inc(s_const, 1)
            pool.wait_ge(s_const, 8)
            pool.affine_select(out=ident, in_=ident, compare_op=ALU.not_equal, fill=1.0, base=0,
                               pattern=[[-1, P]], channel_multiplier=1).then_inc(s_const, 1)
            pool.affine_select(out=upto[:], in_=upto[:], compare_op=ALU.is_ge, fill=0.0, base=0,
                               pattern=[[1, P]], channel_multiplier=-1).then_inc(s_const, 1)
            pool.affine_select(out=below[:], in_=below[:], compare_op=ALU.is_gt, fill=0.0, base=0,
                               pattern=[[-1, P]], channel_multiplier=1).then_inc(s_const, 1)

            def weights_lo(j, u):
                for nib in range(2):
                    pool.wait_ge(s_whi, 2 * j + nib + 1)
                    pool.tensor_tensor(w0_lo[:, j, nib], wf[:, u, nib], w0_hi[:, j, nib].bitcast(F32),
                                       ALU.subtract).then_inc(s_wlo, 1)

            pool.sem_inc(s_wlo, 4)
            with pool.Fori(0, JOBS // 2 - 1) as h:
                for u in range(2):
                    weights_lo(2 * h + u, u)

            def inv_std(f, mv_, ve_, r_, s_in, s_out):
                pool.wait_ge(s_in, 2 * NT * (f + 1))
                pool.tensor_tensor(ve_[:], mv_[:, :, 1], eps4[:], ALU.add).then_inc(s_out, 1)
                pool.wait_ge(s_out, 2 * f + 1)
                pool.tensor_tensor(r_[:], ve_[:], m_half[:], ALU.pow).then_inc(s_out, 1)

            inv_std(0, mv, ve, rstd, s_ln1, s_ln1r)
            for j in range(JOBS - 2, JOBS):
                weights_lo(j, j % 2)
            pool.wait_ge(c_wc_raw, 32)
            pool.wait_ge(c_small, 96)
            for k in range(HEADS):
                pool.tensor_scalar(wo_raw[:, k], wo_raw[:, k], nw[:, k:k + 1], float(D_INNER) ** 0.5, ALU.mult,
                                   ALU.mult).then_inc(c_wcs, 1)
            pool.tensor_copy(win_h[:], win_raw[:]).then_inc(c_wch, 1)
            pool.wait_ge(c_wcs, HEADS)
            pool.tensor_copy(wo_h[:], wo_raw[:]).then_inc(c_wch, 1)
            pool.wait_ge(c_wch, 2)
            pool.tensor_tensor(win_l[:], win_raw[:], win_h[:].bitcast(F32), ALU.subtract).then_inc(c_wch, 1)
            pool.tensor_tensor(wo_l[:], wo_raw[:], wo_h[:].bitcast(F32), ALU.subtract).then_inc(c_wch, 1)
            inv_std(1, mv, ve, rstd, s_ln1, s_ln1r)
            with pool.Fori(1, GROUPS - 1) as g:
                inv_std(g - 1, mvb, veb, rstdb, s_ln2, s_ln2r)
                inv_std(g + 1, mv, ve, rstd, s_ln1, s_ln1r)
            inv_std(GROUPS - 2, mvb, veb, rstdb, s_ln2, s_ln2r)
            pool.wait_ge(c_xbc, 1)
            pool.memset(raw[:, :, 0:TAPS - 1], 0.0).then_inc(c_halo, 1)
            inv_std(GROUPS - 1, mvb, veb, rstdb, s_ln2, s_ln2r)

            pool.wait_ge(s_down, GROUPS)
            pool.memset(tail[:], 0.0).then_inc(c_init, 1)

            def masked_decay(n, t):
                if t == 0:
                    pool.wait_ge(c_dtc, DT_STEPS * (n + 1))
                    pool.wait_ge(c_seg, NT * n)
                pool.tensor_tensor(au[:, t], upto[:].unsqueeze(1).broadcast_to([P, HEADS, P]),
                                   adt[:, t].unsqueeze(2).broadcast_to([P, HEADS, P]), ALU.mult).then_inc(c_au, 1)

            def inv_std_chunk(k, c):
                pool.wait_ge(c_ln3, 2 * k + 2)
                pool.tensor_tensor(ve[:, c:c + 1], mv[:, c, 1:2], eps4[:, 0:1], ALU.add).then_inc(c_ln3r, 1)
                pool.wait_ge(c_ln3r, 2 * k + 1)
                pool.tensor_tensor(rstd[:, c:c + 1], ve[:, c:c + 1], m_half[:, 0:1], ALU.pow).then_inc(c_ln3r, 1)

            def inv_rms(k, u):
                pool.wait_ge(c_ss, k + 1 + 1)
                pool.wait_ge(c_y3, (k if isinstance(k, int) and k == 0 else k - 1) + 1)
                pool.tensor_tensor(rr[:, u:u + 1], ss[:, u:u + 1], eps_rms[:], ALU.add).then_inc(c_rr, 1)
                pool.wait_ge(c_rr, 2 * k + 1 + 1)
                pool.tensor_tensor(rr[:, u:u + 1], rr[:, u:u + 1], m_half[:, 0:1], ALU.pow).then_inc(c_rr, 1)

            def step(s, b, i, nxt):
                for c in range(NT):
                    k, u = NT * s + c, c % 2
                    before = not isinstance(k, int) or k > 0
                    pool.wait_ge(c_xtk, k + 1 + 1)
                    pool.wait_ge(c_yo2, k + 1)
                    pool.tensor_tensor(xsd[:, u], xtk[:, u], dtv[:, b, c].unsqueeze(2).broadcast_to([P, HEADS, HEADDIM]),
                                       ALU.mult).then_inc(c_xsd, 1)
                    pool.wait_ge(c_xsd, k + 1)
                    pool.wait_ge(c_ds, (k if c == 0 else k - 1) + 1)
                    pool.tensor_tensor(xdc[:, u], xsd[:, u], ee[:, c, :, P - 1:P].broadcast_to([P, HEADS, HEADDIM]),
                                       ALU.mult).then_inc(c_xdc, 1)
                    if nxt and c == 2:
                        masked_decay(nxt[0], 0)
                        masked_decay(nxt[0], 1)
                    if before:
                        inv_rms(k - 1, 1 - u)
                    pool.tensor_tensor(xd[:, u], xtk[:, u], d4[:].unsqueeze(2).broadcast_to([P, HEADS, P]),
                                       ALU.mult).then_inc(c_xd, 1)
                    pool.wait_ge(c_yo, k + 1 + 1)
                    pool.wait_ge(c_xd, k + 1)
                    pool.wait_ge(c_g1, (k if c == 0 else k - 1) + 1)
                    pool.tensor_tensor(xd[:, u], yo[:, u], xd[:, u], ALU.add).then_inc(c_yo2, 1)
                    if before and (not isinstance(k, int) or k > 1):
                        inv_std_chunk(k - 2, (c - 2) % NT)
                    if nxt and c == 2:
                        masked_decay(nxt[0], 2)
                        masked_decay(nxt[0], 3)
                    if c == 3:
                        pool.wait_ge(c_w1h, s + 1)
                        pool.tensor_tensor(w1_l[:, s], w1_raw[:], w1_h[:, s].bitcast(F32), ALU.subtract).then_inc(c_w1l, 1)

            for t in range(NT):
                masked_decay(0, t)
            pool.wait_ge(s_x2, NT * GROUPS)
            pool.memset(state[:], 0.0).then_inc(c_st, 1)
            for_groups(step)(pool)
            last = NT * GROUPS - 1
            inv_rms(last, 1)
            inv_std_chunk(last - 1, NT - 2)
            inv_std_chunk(last, NT - 1)

            pool.wait_ge(c_x3, NT * GROUPS)

            def ranks(m):
                pool.wait_ge(d_cmp, len(PAIRS) * (m + 1))
                pool.tensor_tensor(rank[:, 2], beats[:, 5], beats[:, 1], ALU.subtract).then_inc(d_padd, 1)
                pool.tensor_tensor(rank[:, 3], beats[:, 2], beats[:, 4], ALU.add).then_inc(d_padd, 1)
                pool.wait_ge(d_padd, 4 * m + 1)
                pool.tensor_tensor(rank[:, 2], rank[:, 2], beats[:, 3], ALU.subtract).then_inc(d_padd, 1)
                pool.wait_ge(d_padd, 4 * m + 2)
                pool.tensor_tensor(rank[:, 3], rank[:, 3], beats[:, 5], ALU.add).then_inc(d_padd, 1)

            def unit(m, mb):
                ranks(m)
                for r in range(RANK):
                    pool.wait_ge(d_hi, RANK * m + r + 1)
                    pool.tensor_tensor(dhl[:, mb, r], dab[:, mb, r], dhh[:, mb, r].bitcast(F32),
                                       ALU.subtract).then_inc(d_lo, 1)

            for m in range(3):
                unit(m, m % MB)
            with pool.Fori(2, GROUPS) as g:
                inv_std(g - 2, mv, ve, rstd, d_ln, d_lnr)
                unit(MB * g - 1, 1)
                unit(MB * g, 0)
            unit(MB * GROUPS - 1, 1)
            for g in (GROUPS - 2, GROUPS - 1):
                inv_std(g, mv, ve, rstd, d_ln, d_lnr)

        @block.scalar
        def _(act):
            def copy(dst, src):
                return act.activation(dst, src, ACT.Copy)

            def weights_hi(j, u):
                for nib in range(2):
                    act.wait_ge(s_wf, 2 * j + nib + 1)
                    copy(w0_hi[:, j, nib], wf[:, u, nib]).then_inc(s_whi, 1)

            def xs_hi(f, u, loads):
                act.wait_ge(s_x[u], 16 * loads)
                act.wait_ge(s_xs_free, f + 1)
                copy(xs[:, u, :, 0:H], xg[:, u]).then_inc(s_xs_hi, 1)

            def two_pieces(q):
                xs_hi(2 * q + 1, 1, q + 1)
                weights_hi(2 * q, 0)
                xs_hi(2 * q + 2, 0, q + 2)
                weights_hi(2 * q + 1, 1)

            def softmax(b, between):
                act.wait_ge(s_sc_mm, b + 1)
                for i in range(2):
                    copy(s_hl[:, i], ps_gate[i][:, H:2 * H]).then_inc(s_sma, 1)
                act.wait_ge(s_sm, 6 * b + 4)
                for i in range(2):
                    act.activation(s_hl[:, i], s_full[:, i], ACT.Exp, bias=nmax[:, i:i + 1],
                                   accum_out=rsum[:, i:i + 1]).then_inc(s_sma, 1)
                between()
                act.wait_ge(s_smt, 2 * b + 2)
                copy(soft_wt[:, b, 0], ps_t[1][:]).then_inc(s_sma, 1)

            def between_0():
                xs_hi(GPB + 1, 1, GPB // 2 + 1)
                weights_hi(GPB, 0)

            def between_1():
                act.wait_ge(c_small, 96)
                act.activation(a4[:], a4[:], ACT.Exp).then_inc(c_a4, 1)
                weights_hi(GROUPS, 0)

            xs_hi(0, 0, 1)
            with act.Fori(0, GPB // 2) as q:
                two_pieces(q)
            softmax(0, between_0)
            for f in range(GPB + 1, GROUPS):
                if f + 1 < GROUPS:
                    xs_hi(f + 1, (f + 1) % 2, (f + 1) // 2 + 1)
                weights_hi(f, f % 2)
            softmax(1, between_1)

            def x_hi(f, k):
                act.wait_ge(s_xt_t, KT * f + k + 1)
                act.wait_ge(s_ctx, NT * f)
                copy(xt_h[:, k], ps_t[k][:]).then_inc(s_xt_hi, 1)

            def a_hi(f, k):
                act.wait_ge(s_at_t, KT * f + k + 1)
                act.wait_ge(s_up, NB0 * f)
                copy(at_h[:, k], ps_t[k][:]).then_inc(s_at_hi, 1)

            def gelu(g, n):
                act.wait_ge(s_gate, NB0 * g + n + 1)
                act.activation(gl[:, n % 2], ps_gate[n % 2][:], ACT.Gelu_apprx_tanh).then_inc(s_gelu, 1)

            def h_hi(g, n):
                act.wait_ge(s_h, NB0 * g + n + 1)
                copy(hh[:, n % 2], hb[:, n % 2]).then_inc(s_hhi, 1)

            def keep_residual(g):
                act.wait_ge(s_y, NT * g + 1)
                act.wait_ge(s_x1, NT * (g + 1))
                copy(x1_res[:], x1[:]).then_inc(s_x1r, 1)

            def group(g, more):
                for n in range(NB0):
                    gelu(g, n)
                    if more and n == NB0 - 1:
                        a_hi(g + 1, 0)
                        a_hi(g + 1, 1)
                    h_hi(g, n)
                    if n == 4:
                        keep_residual(g)
                    if more and n == 2:
                        x_hi(g + 1, 0)
                        x_hi(g + 1, 1)
                    if not more and n == X2_AT + 1:
                        for k in range(KT):
                            act.wait_ge(c_t, k + 1)
                            copy(xt_h[:, k], early(k)[:]).then_inc(c_xth, 1)
                    if not more and XBC_AT < n <= XBC_AT + XB:
                        xbc_in(0, 0, n - XBC_AT - 1, early(n - XBC_AT - 1), n - XBC_AT - 1 < HEADS)

            for k in range(KT):
                x_hi(0, k)
            for j in range(GROUPS + 1, JOBS):
                weights_hi(j, j % 2)
            for k in range(KT):
                a_hi(0, k)
            act.wait_ge(s_wlo, 2 * JOBS + 4)
            with act.Fori(0, GROUPS - 1) as g:
                group(g, True)

            def xbc_in(n, b, j, place=None, in_xc=False):
                src = place if place is not None else ring(XBC0 + j)
                act.wait_ge(c_xbc, XB * n + j + 1)
                if place is None:
                    act.wait_ge(c_silu, XB * n + max(j - 1, 0))
                copy(raw[:, j, TAPS - 1:], src[:])
                act.activation(xc[:, b, j] if in_xc else acc[:, j % 2], src[:], ACT.Identity, bias=cb[:, j:j + 1],
                               scale=cw[:, j, TAPS - 1:TAPS]).then_inc(c_xin, 1)

            def conv_silu(n, b, j, in_xc=False):
                act.wait_ge(c_cv, (TAPS - 1) * (XB * n + j + 1))
                act.activation(xc[:, b, j] if j < HEADS else bc[:, b], xc[:, b, j] if in_xc else acc[:, j % 2], ACT.Silu).then_inc(c_silu, 1)

            def z_silu(n, t):
                act.wait_ge(c_zp, NT * n + t + 1)
                if not isinstance(n, int) or n > 0:
                    act.wait_ge(c_g, NT * n + t - 3)
                act.activation(zs[:, t], z_place(t)[:], ACT.Silu).then_inc(c_zs, 1)

            def x2_hi(n, b):
                act.wait_ge(c_cv, (TAPS - 1) * XB * n)
                act.wait_ge(c_halo, 2 * n)
                copy(raw[:, :, 0:TAPS - 1], tail[:, b]).then_inc(c_halo, 1)
                for k in range(KT):
                    act.wait_ge(c_t, KT * n + k + 1)
                    copy(xt_h[:, k], ring(k)[:]).then_inc(c_xth, 1)

            def dt_exp_ln(n, b, mid=True):
                act.wait_ge(c_dtc, DT_STEPS * n + 2)
                act.activation(de[:], dax[:], ACT.Exp).then_inc(c_dta, 1)
                if mid:
                    xbc_in(n, b, 0)
                act.wait_ge(c_dtc, DT_STEPS * n + 3)
                act.activation(dl[:], du[:], ACT.Ln).then_inc(c_dta, 1)

            def keep_tail(n, b):
                act.wait_ge(c_xin, XB * (n + 1))
                act.wait_ge(c_halo, 2 * n + 1)
                copy(tail[:, b], raw[:, :, TOK:]).then_inc(c_halo, 1)

            def decays(n, b):
                act.wait_ge(c_acs, n + 1)
                act.activation(ea[:, b].rearrange("p t h -> p (t h)"), ring(ACS0)[:, 0:16], ACT.Exp).then_inc(c_ea, 1)
                act.activation(et[:, b].rearrange("p t h -> p (t h)"), ring(ACS0)[0:D_STATE, 16:32], ACT.Exp).then_inc(c_ea, 1)

            def segment_exp(n, t):
                if not isinstance(n, int) or n > 0:
                    act.wait_ge(c_m, NT * n + t - 3)
                    act.wait_ge(c_xdc, NT * n + t - 3)
                act.wait_ge(c_seg, NT * n + t + 1)
                act.activation(ee[:, t].rearrange("p h l -> p (h l)"), ring(SEG0 + t)[:], ACT.Exp).then_inc(c_e, 1)

            def project(slot, nxt, part):
                n, b, i = nxt
                if slot == 0 and part == 0:
                    x2_hi(n, b)
                if slot == 0 and part == 1:
                    dt_exp_ln(n, b)
                    xbc_in(n, b, 1)
                if slot == 1 and part == 0:
                    conv_silu(n, b, 0)
                    xbc_in(n, b, 2)
                    conv_silu(n, b, 1)
                    xbc_in(n, b, 3)
                if slot == 2 and part == 0:
                    conv_silu(n, b, 2)
                    xbc_in(n, b, 4)
                    z_silu(n, 0)
                    conv_silu(n, b, 3)
                    z_silu(n, 1)
                    decays(n, b)
                if slot == 3 and part == 0:
                    segment_exp(n, 1)
                    segment_exp(n, 2)
                    segment_exp(n, 3)
                    keep_tail(n, b)
                    conv_silu(n, b, 4)
                if slot == 3 and part == 1:
                    z_silu(n, 3)

            def g_hi(k, u):
                act.wait_ge(c_gT, k + 1)
                copy(gt_h[:, u].rearrange("p h t -> p (h t)"), ps_g[:]).then_inc(c_gth, 1)

            def x_token_major(k, u):
                act.wait_ge(c_tr, k + 1)
                copy(xtk[:, u].rearrange("p h d -> p (h d)"), ps_x[:]).then_inc(c_xtk, 1)

            def step(s, b, i, nxt):
                for c in range(NT):
                    k, u = NT * s + c, c % 2
                    if nxt and c == NT - 1:
                        segment_exp(nxt[0], 0)
                    if c > 0 or not isinstance(k, int) or k > 0:
                        g_hi(k - 1, 1 - u)
                    act.wait_ge(c_yoff, k + 1)
                    act.wait_ge(c_ea, 2 * (s + 1))
                    for h in range(HEADS):
                        y = act.activation(yo[:, u, h], ps_yoff[:, h * HEADDIM:(h + 1) * HEADDIM], ACT.Copy,
                                           scale=ea[:, b, c, h:h + 1])
                    y.then_inc(c_yo, 1)
                    if nxt:
                        project(c, nxt, 0)
                    elif c == 0:
                        for j in range(KT):
                            act.wait_ge(d_t, j + 1)
                            copy(xt_h[:, j], bank[j][:]).then_inc(d_th, 1)
                    if c < NT - 1 or nxt:
                        if not isinstance(k, int) or k > 0:
                            act.wait_ge(c_xd, k)
                        x_token_major(k + 1, 1 - u)
                    if nxt and c == NT - 1:
                        z_silu(nxt[0], 2)
                    act.wait_ge(c_g, k + 1)
                    act.wait_ge(c_ss, k + 1)
                    act.wait_ge(c_rr, 2 * k + 1)
                    act.activation(yo[:, u].rearrange("p h d -> p (h d)"), gg[:, u], ACT.Square, accum_out=ss[:, u:u + 1]).then_inc(c_ss, 1)
                    if c == 1:
                        act.wait_ge(c_w1r, 16 * (s + 1))
                        copy(w1_h[:, s], w1_raw[:]).then_inc(c_w1h, 1)
                    if c == 2:
                        act.wait_ge(c_y3, k + 1)
                        copy(rest[:], xg[:, b, 2:]).then_inc(c_rest, 1)
                    if nxt:
                        project(c, nxt, 1)
                    else:
                        silu1(0, c, bank[0], c % 2)

            group(GROUPS - 1, False)
            for j in range(HEADS):
                conv_silu(0, 0, j, in_xc=True)
            act.wait_ge(s_down, GROUPS)
            conv_silu(0, 0, HEADS)
            z_silu(0, 0)
            z_silu(0, 1)
            act.wait_ge(c_init, 1)
            keep_tail(0, 0)
            dt_exp_ln(0, 0, mid=False)
            decays(0, 0)
            for t in range(NT):
                segment_exp(0, t)
            z_silu(0, 2)
            z_silu(0, 3)
            act.wait_ge(s_x2, NT * GROUPS)
            x_token_major(0, 0)

            def silu1(m, r, gate, place):
                act.wait_ge(d_gate, RANK * m + r + 1)
                act.activation(dg[:, place], gate[:], ACT.Silu).then_inc(d_silu, 1)

            for_groups(step)(act)
            g_hi(NT * GROUPS - 1, 1)

            def keep_x3(g):
                act.wait_ge(d_x, 16 * (g + 1))
                copy(res[:, g & RES - 1], xg[:, 0]).then_inc(d_res, 1)

            def x3_hi(g):
                if not isinstance(g, int) or g > 0:
                    act.wait_ge(d_up, MB * RANK * g)
                for k in range(KT):
                    act.wait_ge(d_t, KT * g + k + 1)
                    copy(xt_h[:, k], ps_t[k][:]).then_inc(d_th, 1)

            def kept_hi(m, mb, r):
                act.wait_ge(d_sel, RANK * m + r + 1)
                copy(dhh[:, mb, r], dab[:, mb, r]).then_inc(d_hi, 1)

            def unit(m, mb, g, back, old, front=None):
                for r in range(RANK):
                    silu1(m, r, ps_gate[r % 2], r % 2)
                    if front is not None and r == RANK - 1:
                        x3_hi(front)
                    if back and r > 1:
                        kept_hi(m - 1, 1 - mb, 2 * r - 4)
                        kept_hi(m - 1, 1 - mb, 2 * r - 3)
                    act.wait_ge(d_mul, RANK * m + r + 1)
                    if old:
                        act.wait_ge(d_lo, RANK * (m - 2) + r + 1)
                    act.activation(dab[:, mb, r], dh[:, mb, r], ACT.Abs).then_inc(d_abs, 1)
                    if mb == 0 and r == 0:
                        keep_x3(g)

            def group(g, last=False):
                old = not isinstance(g, int) or g > 0
                unit(MB * g, 0, g, old, old)
                unit(MB * g + 1, 1, g, True, old, None if last else g + 1)

            act.wait_ge(c_x3, NT * GROUPS)
            for r in range(RANK):
                act.wait_ge(d_mul, r + 1)
                act.activation(dab[:, 0, r], dh[:, 0, r], ACT.Abs).then_inc(d_abs, 1)
            keep_x3(0)
            unit(1, 1, 0, True, False, 1)
            group(1)
            with act.Fori(2, GROUPS - 1) as g:
                group(g)
            group(GROUPS - 1, last=True)
            for r in range(RANK):
                kept_hi(MB * GROUPS - 1, 1, r)

        @block.vector
        def _(dve):
            def dequant(j, u, q):
                dve.wait_ge(s_w[u], 144 * (q + 1))
                dve.wait_ge(s_wf, 2 * j)
                for nib in range(2):
                    dve.tensor_scalar(mag[:, nib], wq[:, u], 28 - 4 * nib, 6, ALU.logical_shift_left,
                                      ALU.arith_shift_right).then_inc(s_deq, 1)
                dve.wait_ge(s_deq, 3 * j + 2)
                dve.tensor_scalar(mag[:], mag[:], (7 << 22) - 2 ** 31, None, ALU.bitwise_and).then_inc(s_deq, 1)
                dve.wait_ge(s_deq, 3 * j + 3)
                for nib in range(2):
                    if nib == 0:
                        dve.wait_ge(s_wlo, 2 * j + 2)
                    dve.scalar_tensor_tensor(wf[:, u, nib], mag[:, nib].bitcast(F32), 2.0 ** 126, sc[:, u],
                                             ALU.mult, ALU.mult).then_inc(s_wf, 1)

            dve.wait_ge(s_const, 11)
            def xs_low(f, u):
                dve.wait_ge(s_xs_hi, f + 1)
                dve.tensor_tensor(xs[:, u, :, H:2 * H], xg[:, u], xs[:, u, :, 0:H].bitcast(F32),
                                  ALU.subtract).then_inc(s_xs_lo, 1)

            def softmax(b, first, second):
                for i in range(2):
                    dve.wait_ge(s_sma, 5 * b + i + 1)
                    dve.tensor_tensor(s_full[:, i], ps_gate[i][:, 0:H], s_hl[:, i], ALU.add).then_inc(s_sm, 1)
                first()
                dve.wait_ge(s_sm, 6 * b + 2)
                dve.wait_ge(s_smt, 2 * b + 1)
                sf = s_full[:].rearrange("p i j -> p (i j)")
                dve.tensor_tensor(sf, sf, ps_t[0][:], ALU.add).then_inc(s_sm, 1)
                dve.wait_ge(s_sm, 6 * b + 3)
                dve.tensor_reduce(nmax[:], s_full[:], AX_X, ALU.max, negate=True).then_inc(s_sm, 1)
                second()
                dve.wait_ge(s_sma, 5 * b + 4)
                dve.reciprocal(rinv[:], rsum[:]).then_inc(s_sm, 1)
                dve.wait_ge(s_sm, 6 * b + 5)
                for i in range(2):
                    w = dve.scalar_tensor_tensor(s_hl[:, i], s_hl[:, i], rinv[:, i:i + 1],
                                                 wide_i[:, P * (1 - i):P * (1 - i) + H], ALU.mult, ALU.add)
                w.then_inc(s_sm, 1)
                dve.wait_ge(s_sma, 5 * b + 5)
                dve.tensor_tensor(soft_wt[:, b, 1], ps_t[1][:], soft_wt[:, b, 0].bitcast(F32),
                                  ALU.subtract).then_inc(s_sc_free, 1)

            with dve.Fori(0, GPB // 2) as h:
                for u in range(2):
                    xs_low(2 * h + u, u)
                    dequant(2 * h + u, u, h)
            softmax(0, lambda: xs_low(GPB, 0), lambda: dequant(GPB, 0, GPB // 2))
            for f in range(GPB + 1, GROUPS):
                xs_low(f, f % 2)
                dequant(f, f % 2, f // 2)
            softmax(1, lambda: None, lambda: dequant(GROUPS, 0, GROUPS // 2))

            def lo_part(dst, src, hi):
                return dve.tensor_tensor(dst, src, hi.bitcast(F32), ALU.subtract)

            def x_lo(f, k):
                dve.wait_ge(s_xt_hi, KT * f + k + 1)
                lo_part(xt_l[:, k], ps_t[k][:], xt_h[:, k]).then_inc(s_xt_lo, 1)

            def a_lo(f, k):
                dve.wait_ge(s_at_hi, KT * f + k + 1)
                lo_part(at_l[:, k], ps_t[k][:], at_h[:, k]).then_inc(s_at_lo, 1)

            def stats(f, src, st_, mv_, s_):
                for t in range(NT):
                    dve.bn_stats(st_[:, t], src[t]).then_inc(s_, 1)
                dve.wait_ge(s_, 2 * NT * f + NT)
                dve.sem_inc(s_seen, 1)
                for t in range(NT):
                    dve.bn_aggr(mv_[:, t], st_[:, t]).then_inc(s_, 1)

            ctx_tile = [ps_t[t // 2][:, t % 2 * H:t % 2 * H + H] for t in range(NT)]
            down_tile = [ps_down[t // 2][:, t % 2 * H:t % 2 * H + H] for t in range(NT)]

            def ln1_stats(f):
                dve.wait_ge(s_ctx, NT * (f + 1))
                stats(f, ctx_tile, st6, mv, s_ln1)

            def ln1_apply(f):
                dve.wait_ge(s_ln1r, 2 * (f + 1))
                if not isinstance(f, int) or f > 0:
                    dve.wait_ge(s_x1r, f)
                for t in range(NT):
                    dve.tensor_scalar(x1[:, t], ctx_tile[t], mv[:, t, 0:1], rstd[:, t:t + 1],
                                      ALU.subtract, ALU.mult).then_inc(s_x1, 1)

            def gated(g, n):
                dve.wait_ge(s_gelu, NB0 * g + n + 1)
                dve.wait_ge(s_up, NB0 * g + n + 1)
                dve.tensor_tensor(hb[:, n % 2], gl[:, n % 2], ps_up[n % 2][:], ALU.mult).then_inc(s_h, 1)

            def h_lo(g, n):
                dve.wait_ge(s_hhi, NB0 * g + n + 1)
                lo_part(hl[:, n % 2], hb[:, n % 2], hh[:, n % 2]).then_inc(s_hlo, 1)

            def add_x1(g):
                dve.wait_ge(s_down, g + 1)
                dve.wait_ge(s_x1r, g + 1)
                for t in range(NT):
                    dve.tensor_tensor(yb[:, t], down_tile[t], x1_res[:, t], ALU.add).then_inc(s_y, 1)

            def ln2_stats(g):
                dve.wait_ge(s_y, NT * (g + 1) + 1)
                stats(g, [yb[:, t] for t in range(NT)], st6b, mvb, s_ln2)

            def ln2_apply(g):
                dve.wait_ge(s_ln2r, 2 * (g + 1))
                dve.wait_ge(s_x2st, 16 * g + 16)
                for t in range(NT):
                    dve.tensor_scalar(xo[:, t], yb[:, t], mvb[:, t, 0:1], rstdb[:, t:t + 1],
                                      ALU.subtract, ALU.mult).then_inc(s_x2, 1)

            def group(g, before, more):
                for n in range(NB0):
                    gated(g, n)
                    if more and n == NB0 - 1:
                        a_lo(g + 1, 0)
                        a_lo(g + 1, 1)
                    h_lo(g, n)
                    if before and n == 0:
                        add_x1(g - 1)
                    if before and n == 1:
                        ln2_stats(g - 1)
                    if before and n == 3:
                        ln2_apply(g - 1)
                    if more and n == 2:
                        x_lo(g + 1, 0)
                        x_lo(g + 1, 1)
                    if not more and n == X2_AT + 1:
                        for k in range(KT):
                            dve.wait_ge(c_xth, k + 1)
                            lo_part(xt_l[:, k], early(k)[:], xt_h[:, k]).then_inc(c_xtl, 1)
                    if not more and XBC_AT < n <= XBC_AT + XB:
                        conv(0, 0, n - XBC_AT - 1, in_xc=n - XBC_AT - 1 < HEADS)
                    if more and n == 5:
                        ln1_stats(g + 1)
                    if more and n == 7:
                        ln1_apply(g + 1)

            for k in range(KT):
                x_lo(0, k)
            dequant(GROUPS + 1, 1, GROUPS // 2)
            dequant(GROUPS + 2, 0, GROUPS // 2 + 1)
            ln1_stats(0)
            ln1_apply(0)
            dequant(GROUPS + 3, 1, GROUPS // 2 + 1)
            for k in range(KT):
                a_lo(0, k)
            dve.wait_ge(s_wlo, 2 * JOBS + 4)
            group(0, False, True)
            with dve.Fori(1, GROUPS - 1) as g:
                group(g, True, True)

            def conv(n, b, j, in_xc=False):
                sums = xc[:, b, j] if in_xc else acc[:, j % 2]
                dve.wait_ge(c_xin, XB * n + j + 1)
                dve.wait_ge(c_halo, 2 * n + 1)
                for tap in range(TAPS - 1):
                    steps = (TAPS - 1) * (XB * n + j) + tap
                    if tap > 0:
                        dve.wait_ge(c_cv, steps)
                    dve.scalar_tensor_tensor(sums, raw[:, j, tap:tap + TOK], cw[:, j, tap:tap + 1], sums, ALU.mult, ALU.add).then_inc(c_cv, 1)

            def dt_chain(n, b, mid=True):
                def done(k, ins):
                    ins.then_inc(c_dtc, 1)
                    dve.wait_ge(c_dtc, DT_STEPS * n + k)

                flat = d0[:].rearrange("p t h -> p (t h)")
                dt_flat = dtv[:, b].rearrange("p t h -> p (t h)")
                dve.wait_ge(c_dtp, n + 1)
                done(1, dve.tensor_tensor(d0[:], ring(DT0)[:, 0:16].rearrange("p (t h) -> p t h", h=HEADS),
                                          dtb[:].unsqueeze(1).broadcast_to([P, NT, HEADS]), ALU.add))
                done(2, dve.scalar_tensor_tensor(dax[:], flat, -1.0, flat, ALU.mult, ALU.min))
                dve.wait_ge(c_dta, 2 * n + 1)
                done(3, dve.tensor_scalar(du[:], de[:], 1.0, None, ALU.add))
                if mid:
                    conv(n, b, 0)
                done(4, dve.tensor_scalar(um[:], du[:], -1.0, None, ALU.add))
                done(5, dve.scalar_tensor_tensor(dden[:], um[:], 0.0, um[:], ALU.is_equal, ALU.add))
                done(6, dve.reciprocal(drec[:], dden[:]))
                done(7, dve.tensor_tensor(dm1[:], de[:], drec[:], ALU.mult))
                dve.wait_ge(c_dta, 2 * n + 2)
                done(8, dve.scalar_tensor_tensor(dl2[:], um[:], 0.0, dl[:], ALU.is_equal, ALU.add))
                done(9, dve.tensor_tensor(dm2[:], dm1[:], dl2[:], ALU.mult))
                done(10, dve.scalar_tensor_tensor(dt_flat, flat, 0.0, dm2[:], ALU.max, ALU.add))
                done(11, dve.scalar_tensor_tensor(adt[:], dtv[:, b], -1.0, a4[:].unsqueeze(1).broadcast_to([P, NT, HEADS]),
                                                  ALU.mult, ALU.mult))

            def project(slot, nxt, part):
                n, b, i = nxt
                if slot == 0 and part == 0:
                    for k in range(KT):
                        dve.wait_ge(c_xth, KT * n + k + 1)
                        lo_part(xt_l[:, k], ring(k)[:], xt_h[:, k]).then_inc(c_xtl, 1)
                if slot == 0 and part == 1:
                    dt_chain(n, b)
                if slot > 0 and (slot < 3 or part == 0) and not (slot == 2 and part == 1):
                    conv(n, b, {(1, 0): 1, (1, 1): 2, (2, 0): 3, (3, 0): 4}[slot, part])
                if slot == 3 and part == 1:
                    dve.wait_ge(c_silu, XB * (n + 1))
                    dve.tensor_copy(ct[:, b], bc[D_STATE:2 * D_STATE, b]).then_inc(c_ct, 1)

            def g_lo(k, u):
                dve.wait_ge(c_gth, k + 1)
                lo_part(gt_l[:, u].rearrange("p h t -> p (h t)"), ps_g[:],
                        gt_h[:, u].rearrange("p h t -> p (h t)")).then_inc(c_gtl, 1)

            def add_out(s, b, k, c, u):
                dve.wait_ge(c_o, k + 1)
                dve.wait_ge(c_rr, 2 * (k + 1) + 1)
                if isinstance(k, int) and k == 0:
                    dve.wait_ge(s_x2st, 16 * GROUPS + 16)
                if c % 2 == 0:
                    dve.wait_ge(c_x3st[c // 2], 16 * s + 16)
                if c == 2:
                    dve.wait_ge(c_rest, s + 1)
                dve.scalar_tensor_tensor(y3[:, c], ps_g[:, 0:H], rr[:, u:u + 1], xg[:, b, c] if c < 2 else rest[:, c - 2],
                                         ALU.mult, ALU.add).then_inc(c_y3, 1)
                dve.wait_ge(c_y3, k + 2)
                dve.bn_stats(st6[:, c], y3[:, c]).then_inc(c_ln3, 1)
                dve.wait_ge(c_ln3, 2 * k + 1)
                dve.sem_inc(s_seen, 1)
                dve.bn_aggr(mv[:, c], st6[:, c]).then_inc(c_ln3, 1)

            def ln3_apply(k, c):
                dve.wait_ge(c_ln3r, 2 * k + 2)
                dve.tensor_scalar(y3[:, c], y3[:, c], mv[:, c, 0:1], rstd[:, c:c + 1], ALU.subtract,
                                  ALU.mult).then_inc(c_x3, 1)

            def step(s, b, i, nxt):
                for c in range(NT):
                    k, u = NT * s + c, c % 2
                    later = not isinstance(k, int)
                    dve.wait_ge(c_G, k + 1)
                    dve.tensor_tensor(gm[:, u], small[:, P:2 * P], upto[:], ALU.mult).then_inc(c_gm, 1)
                    dve.tensor_copy(btk[:, u], small[:, 0:D_STATE]).then_inc(c_btk, 1)
                    dve.wait_ge(c_gm, k + 1 + 1)
                    dve.wait_ge(c_e, k + 1)
                    dve.tensor_tensor(mm_[:, u], ee[:, c], gm[:, u].unsqueeze(1).broadcast_to([P, HEADS, P]),
                                      ALU.mult).then_inc(c_m, 1)
                    if later or k > 0:
                        g_lo(k - 1, 1 - u)
                    if nxt:
                        project(c, nxt, 0)
                    elif c == 0:
                        for j in range(KT):
                            dve.wait_ge(d_th, j + 1)
                            lo_part(xt_l[:, j], bank[j][:], xt_h[:, j]).then_inc(d_tl, 1)
                    else:
                        gated1(0, 0, c - 1, bank[1])
                    dve.wait_ge(c_ds, k + 1 + 1)
                    dve.wait_ge(c_ea, 2 * (s + 1))
                    dve.wait_ge(c_st, k + 1)
                    for h in range(HEADS):
                        st = dve.scalar_tensor_tensor(state[:, b, h], state[:, b, h], et[:, b, c, h:h + 1],
                                                      ps_ds[0:D_STATE, h * HEADDIM:(h + 1) * HEADDIM], ALU.mult, ALU.add)
                    st.then_inc(c_st, 1)
                    dve.wait_ge(c_y, k + 1)
                    dve.wait_ge(c_yo2, k + 1 + 1)
                    dve.tensor_tensor(gg[:, u], ps_y[:], xd[:, u].rearrange("p h d -> p (h d)"), ALU.add).then_inc(c_g1, 1)
                    dve.wait_ge(c_g1, k + 1 + 1)
                    dve.wait_ge(c_zs, k + 1)
                    dve.tensor_tensor(gg[:, u], gg[:, u], zs[:, c], ALU.mult).then_inc(c_g, 1)
                    if later or k > 0:
                        add_out(s, b if c > 0 else 1 - b, k - 1, (c - 1) % NT, 1 - u)
                    if later or k > 1:
                        ln3_apply(k - 2, (c - 2) % NT)
                    if nxt:
                        project(c, nxt, 1)

            dve.wait_ge(c_small, 96)
            group(GROUPS - 1, True, False)
            add_x1(GROUPS - 1)
            ln2_stats(GROUPS - 1)
            dve.wait_ge(c_silu, XB)
            dve.tensor_copy(ct[:, 0], bc[D_STATE:2 * D_STATE, 0]).then_inc(c_ct, 1)
            dve.wait_ge(c_a4, 1)
            dt_chain(0, 0, mid=False)
            ln2_apply(GROUPS - 1)

            def gated1(m, mb, r, up):
                dve.wait_ge(d_silu, RANK * m + r + 1)
                dve.wait_ge(d_up, RANK * m + r + 1)
                dve.tensor_tensor(dh[:, mb, r], dg[:, r % 2], up[:], ALU.mult).then_inc(d_mul, 1)

            for_groups(step)(dve)
            last = NT * GROUPS - 1
            gated1(0, 0, RANK - 1, bank[1])
            g_lo(last, 1)
            add_out(GROUPS - 1, 1, last, NT - 1, 1)
            ln3_apply(last - 1, NT - 2)
            ln3_apply(last, NT - 1)


            def x3_lo(g):
                for k in range(KT):
                    dve.wait_ge(d_th, KT * g + k + 1)
                    lo_part(xt_l[:, k], ps_t[k][:], xt_h[:, k]).then_inc(d_tl, 1)

            def compare(m, mb, i):
                one, to, count = PAIRS[i]
                dve.wait_ge(d_abs, RANK * (m + 1))
                dve.tensor_tensor(beats[:, to:to + count], dab[:, mb, one:one + 1].broadcast_to([P, count, TOK]),
                                  dab[:, mb, one + 1:], ALU.is_ge).then_inc(d_cmp, 1)

            def add_ranks(m):
                dve.wait_ge(d_cmp, len(PAIRS) * (m + 1))
                dve.tensor_tensor(rank[:, 0:2], beats[:, 1:4:2], beats[:, 2:5:2], ALU.add).then_inc(d_add, 1)
                dve.wait_ge(d_add, 3 * m + 1)
                dve.tensor_tensor(rank[:, 0], rank[:, 0], beats[:, 0], ALU.add).then_inc(d_add, 1)
                dve.tensor_tensor(rank[:, 1], rank[:, 1], beats[:, 0], ALU.subtract).then_inc(d_add, 1)

            def keep(m, mb, r):
                if r < 2:
                    dve.wait_ge(d_add, 3 * m + 2 + r)
                else:
                    dve.wait_ge(d_padd, 4 * m + 1 + r)
                value, op = KEEP[r]
                dve.scalar_tensor_tensor(dab[:, mb, r], rank[:, r], value, dh[:, mb, r], op, ALU.mult).then_inc(d_sel, 1)

            def sparsify(m, mb, part):
                if part == 0:
                    compare(m, mb, 0)
                if part == 1:
                    compare(m, mb, 1)
                    compare(m, mb, 2)
                if part == 2:
                    add_ranks(m)
                    keep(m, mb, 0)
                    keep(m, mb, 1)
                if part == 3:
                    keep(m, mb, 2)
                    keep(m, mb, 3)

            def add_x3(g):
                dve.wait_ge(d_down, g + 1)
                if isinstance(g, int) and g == 0:
                    for half in range(2):
                        dve.wait_ge(c_x3st[half], 16 * GROUPS + 16)
                else:
                    dve.wait_ge(d_st, 16 * g + 16)
                for t in range(NT):
                    dve.tensor_tensor(dy[:, t], down_tile[t], res[:, g & RES - 1, t], ALU.add).then_inc(d_y, 1)

            def out_stats(g):
                dve.wait_ge(d_y, NT * (g + 1) + 1)
                stats(g, [dy[:, t] for t in range(NT)], st6, mv, d_ln)

            def normalise(g):
                dve.wait_ge(d_lnr, 2 * (g + 1))
                for t in range(NT):
                    dve.tensor_scalar(dy[:, t], dy[:, t], mv[:, t, 0:1], rstd[:, t:t + 1], ALU.subtract,
                                      ALU.mult).then_inc(d_out, 1)

            def unit(m, mb, back, done=None, front=None):
                for r in range(RANK):
                    if done is not None:
                        if r == 0:
                            add_x3(done)
                        if r == 1:
                            out_stats(done)
                        if r == 3:
                            normalise(done)
                    if back:
                        sparsify(m - 1, 1 - mb, r)
                    gated1(m, mb, r, ps_up[r % 2])
                    if front is not None and r == RANK - 1:
                        x3_lo(front)

            unit(1, 1, True, front=1)
            unit(2, 0, True)
            unit(3, 1, True, front=2)
            with dve.Fori(2, GROUPS - 1) as g:
                unit(MB * g, 0, True, done=g - 2)
                unit(MB * g + 1, 1, True, front=g + 1)
            unit(MB * GROUPS - 2, 0, True, done=GROUPS - 3)
            unit(MB * GROUPS - 1, 1, True)
            add_x3(GROUPS - 2)
            for r in range(RANK):
                sparsify(MB * GROUPS - 1, 1, r)
            out_stats(GROUPS - 2)
            normalise(GROUPS - 2)
            add_x3(GROUPS - 1)
            out_stats(GROUPS - 1)
            normalise(GROUPS - 1)

        @block.tensor
        def _(pe):
            pe.wait_ge(s_const, 11)
            pe.sem_inc(s_xs_free, 2)
            for b in range(BATCH):
                if b > 0:
                    pe.wait_ge(s_sc_free, b)
                for i in range(2):
                    pe.matmul(ps_gate[i][:], zero_bf[:, 0:P], zero_bf[:], start=True, stop=False, skip_group_check=True)
                with pe.Fori(0, GPB // 2) as h:
                    for u in range(2):
                        f = GPB * b + 2 * h + u
                        pe.wait_ge(s_xs_lo, f + 1)
                        for t in range(NT):
                            for i in range(2):
                                mm = pe.matmul(ps_gate[i][:], xs[:, u, t, i * P:i * P + P], xs[:, u, t],
                                               start=False, stop=False, skip_group_check=True)
                        mm.then_inc(s_xs_free, 1)
                pe.matmul(ps_gate[0][:], zero_bf[:, 0:P], zero_bf[:], start=False, stop=True, skip_group_check=True)
                pe.matmul(ps_gate[1][:], zero_bf[:, 0:P], zero_bf[:], start=False, stop=True,
                          skip_group_check=True).then_inc(s_sc_mm, 1)
                pe.wait_ge(s_sma, 5 * b + 2)
                for i in range(2):
                    for k in range(KT):
                        mm = pe.transpose(ps_t[0][:, i * H + k * P:i * H + k * P + P], s_hl[:, k, i * P:i * P + P], ident)
                mm.then_inc(s_smt, 1)
                pe.wait_ge(s_sm, 6 * b + 6)
                for k in range(KT):
                    for i in range(2):
                        mm = pe.transpose(ps_t[1][:, k * H + i * P:k * H + i * P + P], s_hl[:, i, k * P:k * P + P], ident)
                mm.then_inc(s_smt, 1)
            pe.wait_ge(s_sc_free, BATCH)

            ctx_tile = [ps_t[t // 2][:, t % 2 * H:t % 2 * H + H] for t in range(NT)]
            down_tile = [ps_down[t // 2][:, t % 2 * H:t % 2 * H + H] for t in range(NT)]

            def x_transpose(f):
                pe.wait_ge(s_xg, 16 * (f + 1))
                pe.wait_ge(s_at_lo, KT * f)
                for k in range(KT):
                    for t in range(NT):
                        mm = pe.transpose(ps_t[k][:, t * P:t * P + P], xg[:, 0, t, k * P:k * P + P], ident)
                    mm.then_inc(s_xt_t, 1)

            def context(f, b):
                pe.wait_ge(s_xt_lo, KT * (f + 1))
                for t in range(NT):
                    for k in range(KT):
                        mm = exact3(pe, ctx_tile[t], xt_h[:, k, t * P:t * P + P], xt_l[:, k, t * P:t * P + P],
                                    soft_wt[:, b, 0, k * H:k * H + H], soft_wt[:, b, 1, k * H:k * H + H],
                                    start=k == 0, stop=k == KT - 1)
                    mm.then_inc(s_ctx, 1)

            def x1_transpose(f):
                pe.wait_ge(s_x1, NT * (f + 1))
                for k in range(KT):
                    for t in range(NT):
                        mm = pe.transpose(ps_t[k][:, t * P:t * P + P],
                                          x1[:, t].rearrange("p (m k) -> p k m", k=KT)[:, k], ident)
                    mm.then_inc(s_at_t, 1)

            def gate_or_up(ps, which, g, n):
                piece, col = 3 * (n // 4) + which, n % 4 * P
                for k in range(KT):
                    if which == 0 and n == 0:
                        pe.wait_ge(s_at_lo, KT * g + k + 1)
                    mm = exact3(pe, ps[n % 2][:], w0_hi[:, piece, k, col:col + P], w0_lo[:, piece, k, col:col + P],
                                at_h[:, k], at_l[:, k], start=k == 0, stop=k == KT - 1)
                return mm

            def down(g, n):
                pe.wait_ge(s_hlo, NB0 * g + n + 1)
                if n == 0:
                    pe.wait_ge(s_y, NT * g + 1)
                piece, nib, col = 3 * (n // 4) + 2, n % 2, n // 2 % 2 * H
                for t in range(NT):
                    mm = exact3(pe, down_tile[t], hh[:, n % 2, t * P:t * P + P], hl[:, n % 2, t * P:t * P + P],
                                w0_hi[:, piece, nib, col:col + H], w0_lo[:, piece, nib, col:col + H],
                                start=n == 0 and t % 2 == 0, stop=n == NB0 - 1, skip_group_check=True)
                if n == NB0 - 1:
                    mm.then_inc(s_down, 1)

            def group(g, before, more, b=0):
                for n in range(NB0):
                    if n > 1:
                        down(g, n - 2)
                    elif before:
                        down(g - 1, NB0 - 2 + n)
                    if n % 4 == 0:
                        pe.wait_ge(s_wlo, 6 * (n // 4 + 1) + 4)
                    gate_or_up(ps_gate, 0, g, n).then_inc(s_gate, 1)
                    gate_or_up(ps_up, 1, g, n).then_inc(s_up, 1)
                    if more and n == 1:
                        x_transpose(g + 1)
                    if not more and n == X2_AT:
                        x2_transpose(0, 0, 0, early)
                    if not more and XBC_AT <= n < XBC_AT + XB:
                        j = n - XBC_AT
                        if j < 2:
                            pe.wait_ge(c_xtl, KT)
                        else:
                            pe.wait_ge(c_xin, j - 1)
                        in_proj(0, j, early(j))
                    if more and n == 4:
                        context(g + 1, b)
                    if more and n == 9:
                        x1_transpose(g + 1)

            x_transpose(0)
            context(0, 0)
            x1_transpose(0)
            group(0, False, True)
            for b in range(BATCH):
                with pe.Fori(max(b * GPB, 1), (b + 1) * GPB - 1) as g:
                    group(g, True, True, b)
                if b < BATCH - 1:
                    group((b + 1) * GPB - 1, True, True, b + 1)

            def x2_transpose(n, b, i, place):
                pe.wait_ge(c_xg[b], 16 * (i + 1))
                for k in range(KT):
                    for t in range(NT):
                        mm = pe.transpose(place(k)[:, t * P:(t + 1) * P], xg[:, b, t, k * P:(k + 1) * P], ident)
                    mm.then_inc(c_t, 1)

            def in_proj(n, j, place):
                cols = slice(D_INNER + j * P, D_INNER + (j + 1) * P)
                for k in range(KT):
                    mm = exact3(pe, place[:], win_h[:, k, cols], win_l[:, k, cols], xt_h[:, k], xt_l[:, k],
                                start=k == 0, stop=k == KT - 1)
                mm.then_inc(c_xbc, 1)

            def tok_proj(ps, t, cols):
                for k in range(KT):
                    mm = exact3(pe, ps, xt_h[:, k, t * P:(t + 1) * P], xt_l[:, k, t * P:(t + 1) * P],
                                win_h[:, k, cols], win_l[:, k, cols], start=k == 0, stop=k == KT - 1)
                return mm

            def z_proj(n, t):
                if t < 2:
                    pe.wait_ge(c_xin, XB * n + 4 + t)
                else:
                    pe.wait_ge(c_e, NT * n + t + 1)
                tok_proj(z_place(t)[:], t, slice(0, D_INNER)).then_inc(c_zp, 1)

            def decay_sums(n):
                pe.wait_ge(c_zs, NT * n + 1)
                pe.wait_ge(c_dtc, DT_STEPS * (n + 1))
                flat = adt[:].rearrange("p t h -> p (t h)")
                pe.matmul(ring(ACS0)[:, 0:16], upto[:], flat, start=True, stop=True)
                pe.matmul(ring(ACS0)[0:D_STATE, 16:32], ones[:], flat, start=True, stop=True).then_inc(c_acs, 1)

            def segment_sums(n, t):
                if t == 0:
                    pe.wait_ge(c_zs, NT * n + 2)
                elif t == 1:
                    pe.wait_ge(c_ea, 2 * (n + 1))
                else:
                    pe.wait_ge(c_e, NT * n + t - 1)
                pe.wait_ge(c_au, NT * n + t + 1)
                pe.matmul(ring(SEG0 + t)[:], below[:], au[:, t].rearrange("p h l -> p (h l)"),
                          start=True, stop=True).then_inc(c_seg, 1)

            def in_proj_at(n, j):
                if j == 1:
                    pe.wait_ge(c_dtc, DT_STEPS * n + 1)
                if j > 1:
                    pe.wait_ge(c_xin, XB * n + j - 1)
                in_proj(n, j, ring(XBC0 + j))

            def project(slot, nxt, part):
                n, b, i = nxt
                if slot == 0 and part == 0:
                    pe.wait_ge(c_zs, NT * n)
                    x2_transpose(n, b, i, ring)
                if slot == 0 and part == 1:
                    dt_proj(nxt)
                    in_proj_at(n, 0)
                    in_proj_at(n, 1)
                if slot == 1:
                    for j in (2, 3) if part == 0 else (4,):
                        in_proj_at(n, j)
                if slot == 2 and part == 0:
                    z_proj(n, 0)
                if slot == 2 and part == 1:
                    z_proj(n, 1)
                    decay_sums(n)
                    segment_sums(n, 0)
                if slot == 3 and part == 0:
                    segment_sums(n, 1)
                    segment_sums(n, 2)
                    segment_sums(n, 3)
                if slot == 3 and part == 1:
                    z_proj(n, 2)
                    z_proj(n, 3)

            def dt_proj(nxt):
                n, b, i = nxt
                pe.wait_ge(c_xtl, KT * (n + 1))
                for t in range(NT):
                    mm = tok_proj(ring(DT0)[:, t * HEADS:(t + 1) * HEADS], t, slice(D_IN - HEADS, D_IN))
                mm.then_inc(c_dtp, 1)

            def g_transpose(k, u):
                pe.wait_ge(c_g, k + 1)
                pe.wait_ge(c_y3, k + 1)
                for h in range(HEADS):
                    mm = pe.transpose(ps_g[:, h * P:(h + 1) * P], gg[:, u, h * P:(h + 1) * P], ident)
                mm.then_inc(c_gT, 1)

            def out_proj(k, u):
                pe.wait_ge(c_gtl, k + 1)
                for h in range(HEADS):
                    mm = exact3(pe, ps_g[:, 0:H], gt_h[:, u, h], gt_l[:, u, h], wo_h[:, h], wo_l[:, h],
                                start=h == 0, stop=h == HEADS - 1)
                mm.then_inc(c_o, 1)

            w1h, w1l = (w[:].rearrange("p a b -> p (a b)") for w in (w1_h, w1_l))
            def x3_transpose(g, place):
                pe.wait_ge(d_x, 16 * (g + 1))
                pe.wait_ge(d_tl, KT * g)
                for k in range(KT):
                    for t in range(NT):
                        mm = pe.transpose(place[k][:, t * P:(t + 1) * P], xg[:, 0, t, k * P:(k + 1) * P], ident)
                    mm.then_inc(d_t, 1)

            def gate_and_up(m, mb, r, g, gate, up):
                for which, ps, s_ in ((0, gate, d_gate), (1, up, d_up)):
                    for k in range(KT):
                        if which == 0 and mb == 0 and r == 0:
                            pe.wait_ge(d_tl, KT * g + k + 1)
                        at = ((which * MB + mb) * RANK + r) * KT * P + k * P
                        mm = exact3(pe, ps[:], w1h[:, at:at + P], w1l[:, at:at + P], xt_h[:, k], xt_l[:, k],
                                    start=k == 0, stop=k == KT - 1)
                    mm.then_inc(s_, 1)

            def x_token_major(k, b, c):
                pe.wait_ge(c_xtk, k + 1)
                for h in range(HEADS):
                    mm = pe.transpose(ps_x[:, h * P:(h + 1) * P], xc[:, b, h, c * P:(c + 1) * P], ident)
                mm.then_inc(c_tr, 1)

            def step(s, b, i, nxt):
                for c in range(NT):
                    k, u, cols = NT * s + c, c % 2, slice(c * P, (c + 1) * P)
                    before = not isinstance(k, int) or k > 0
                    if c == 0:
                        pe.wait_ge(c_silu, XB * (s + 1))
                        pe.wait_ge(c_ct, s + 1)
                    pe.wait_ge(c_gm, k + 1)
                    pe.wait_ge(c_btk, k + 1)
                    pe.matmul(small[:, P:2 * P], bc[0:D_STATE, b, cols], ct[:, b, cols], start=True, stop=True)
                    pe.transpose(small[:, 0:D_STATE], bc[0:D_STATE, b, cols],
                                 wide_i[0:D_STATE, P:P + D_STATE]).then_inc(c_G, 1)
                    if before:
                        g_transpose(k - 1, 1 - u)
                    pe.wait_ge(c_st, k + 1)
                    pe.wait_ge(c_yo, k + 1)
                    pe.matmul(ps_yoff[:], ct[:, b, cols], state[:, b].rearrange("p h d -> p (h d)"),
                              start=True, stop=True).then_inc(c_yoff, 1)
                    if nxt:
                        project(c, nxt, 0)
                    elif c == 0:
                        pe.wait_ge(c_zs, NT * GROUPS)
                        x3_transpose(0, bank)
                    pe.wait_ge(c_xdc, k + 1)
                    pe.wait_ge(c_btk, k + 1 + 1)
                    pe.matmul(ps_ds[0:D_STATE, :], btk[:, u], xdc[:, u].rearrange("p h d -> p (h d)"),
                              start=True, stop=True).then_inc(c_ds, 1)
                    pe.wait_ge(c_m, k + 1)
                    pe.wait_ge(c_xsd, k + 1)
                    pe.wait_ge(c_g1, k + 1)
                    for h in range(HEADS):
                        mm = pe.matmul(ps_y[:, h * HEADDIM:(h + 1) * HEADDIM], mm_[:, u, h], xsd[:, u, h],
                                       start=True, stop=True)
                    mm.then_inc(c_y, 1)
                    if before:
                        out_proj(k - 1, 1 - u)
                    if c < NT - 1:
                        x_token_major(k + 1, b, c + 1)
                    elif nxt:
                        pe.wait_ge(c_silu, XB * nxt[0] + HEADS)
                        x_token_major(k + 1, nxt[1], 0)
                    if nxt:
                        project(c, nxt, 1)
                    else:
                        if c > 0:
                            pe.wait_ge(d_mul, c)
                        gate_and_up(0, 0, c, 0, bank[0], bank[1])

            pe.wait_ge(c_wch, 4)
            group(GROUPS - 1, True, False)
            down(GROUPS - 1, NB0 - 2)
            z_proj(0, 0)
            down(GROUPS - 1, NB0 - 1)
            z_proj(0, 1)
            pe.wait_ge(c_zs, 1)
            dt_proj((0, 0, 0))
            decay_sums(0)
            for t in range(NT):
                segment_sums(0, t)
            z_proj(0, 2)
            z_proj(0, 3)
            pe.wait_ge(s_y, NT * GROUPS + 1)
            pe.wait_ge(c_silu, HEADS)
            x_token_major(0, 0, 0)
            for_groups(step)(pe)
            g_transpose(NT * GROUPS - 1, 1)
            out_proj(NT * GROUPS - 1, 1)


            def down1(m, mb, r, g):
                pe.wait_ge(d_lo, RANK * m + r + 1)
                if mb == 0 and r == 0:
                    pe.wait_ge(d_y, NT * g + 1)
                at = 2 * KT * MLP1 + (mb * RANK + r) * H
                for t in range(NT):
                    mm = exact3(pe, down_tile[t], dhh[:, mb, r, t * P:(t + 1) * P], dhl[:, mb, r, t * P:(t + 1) * P],
                                w1h[:, at:at + H], w1l[:, at:at + H], start=mb == 0 and r == 0 and t % 2 == 0,
                                stop=mb == MB - 1 and r == RANK - 1, skip_group_check=True)
                if mb == MB - 1 and r == RANK - 1:
                    mm.then_inc(d_down, 1)

            def unit(m, mb, g, downs=True, front=None):
                m_is_1 = isinstance(m, int) and m == 1
                for r in range(RANK):
                    pe.wait_ge(d_mul, RANK if m_is_1 and r == 0 else RANK * m + r - 1)
                    gate_and_up(m, mb, r, g, ps_gate[r % 2], ps_up[r % 2])
                    if m_is_1 and r == RANK - 1:
                        pe.wait_ge(c_y3, NT * GROUPS + 1)
                        pe.wait_ge(c_st, NT * GROUPS + 1)
                    if front is not None and r == (RANK - 1 if m_is_1 else 1):
                        x3_transpose(front, ps_t)
                    if downs:
                        down1(m - 2, mb, r, g - 1)

            pe.wait_ge(c_btk, NT * GROUPS + 1)
            pe.wait_ge(c_xtk, NT * GROUPS + 1)
            unit(1, 1, 0, downs=False, front=1)
            pe.wait_ge(c_w1l, GROUPS)
            pe.wait_ge(c_yo, NT * GROUPS + 1)
            pe.wait_ge(c_g1, NT * GROUPS + 1)
            for m in range(MB, 2 * MB):
                unit(m, m % MB, m // MB, downs=m >= MB, front=m // MB + 1 if m % MB else None)
            with pe.Fori(2, GROUPS - 1) as g:
                unit(MB * g, 0, g)
                unit(MB * g + 1, 1, g, front=g + 1)
            unit(MB * GROUPS - 2, 0, GROUPS - 1)
            unit(MB * GROUPS - 1, 1, GROUPS - 1)
            for m in range(MB * GROUPS - 2, MB * GROUPS):
                for r in range(RANK):
                    down1(m, m % MB, r, GROUPS - 1)


_INS = ["x", "codes", "scales", "w_in", "conv_w", "conv_b", "dt_bias", "a_log", "d_skip", "norm_w", "w_out",
        "w_mlp1"]


def layout(i):
    import numpy as np

    def by_block(a):
        return a.reshape(a.shape[0], 8, P, 2).transpose(0, 1, 3, 2).reshape(a.shape[0], 4, 512)

    g, u = (by_block(i[f"L0_ffn_{n}_W_packed"].T) for n in ("gate", "up"))
    gs, us = (by_block(i[f"L0_ffn_{n}_scales"].T) for n in ("gate", "up"))
    d = i["L0_ffn_down_W_packed"].T.reshape(4, 2, P, H).transpose(2, 0, 1, 3).reshape(P, 4, 512)
    ds = i["L0_ffn_down_scales"].T.reshape(4, 2, 8, H).transpose(2, 0, 1, 3).reshape(8, 4, 512)
    return {
        "x": i["L0_attn_x"].reshape(T, H),
        "codes": np.stack([g, u, d], 2).reshape(P, JOBS, 512).transpose(1, 0, 2),
        "scales": np.stack([gs, us, ds], 2).reshape(8, JOBS, 512).transpose(1, 0, 2),
        "w_in": i["L1_attn_W_in"].T.reshape(KT, P, D_IN).transpose(1, 0, 2),
        "conv_w": i["L1_attn_W_conv"].reshape(XB, P, TAPS).transpose(1, 0, 2),
        "conv_b": i["L1_attn_b_conv"].reshape(XB, P).T,
        "dt_bias": i["L1_attn_dt_bias"].reshape(1, HEADS),
        "a_log": i["L1_attn_A_log"].reshape(1, HEADS),
        "d_skip": i["L1_attn_D"].reshape(1, HEADS),
        "norm_w": i["L1_attn_norm_w"].reshape(HEADS, HEADDIM).T,
        "w_out": i["L1_attn_W_out"].T.reshape(HEADS, HEADDIM, H).transpose(1, 0, 2),
        "w_mlp1": np.concatenate(
            [i[f"L1_ffn_w_{n}"].reshape(KT, P, MB, P, RANK).transpose(1, 2, 4, 0, 3).reshape(P, -1) for n in ("gate", "up")]
            + [i["L1_ffn_w_down"].reshape(MB, P, RANK, H).transpose(1, 0, 2, 3).reshape(P, -1)], 1)
        .reshape(P, GROUPS, -1).transpose(1, 0, 2),
    }


def kernel(**inputs):
    import numpy as np
    import concourse.bacc as bacc
    from concourse.bass_utils import run_bass_kernel_spmd

    nc = bacc.Bacc("TRN2", target_bir_lowering=False, num_devices=1)
    laid = layout({k: np.asarray(v) for k, v in inputs.items()})
    arrays, args = {}, []
    for name in _INS:
        a = np.ascontiguousarray(laid[name])
        arrays[f"in_{name}"] = a
        args.append(nc.dram_tensor(f"in_{name}", a.shape, mybir.dt.from_np(a.dtype), kind="ExternalInput").ap())
    args.append(nc.dram_tensor("out_0", (T, H), F32, kind="ExternalOutput").ap())
    build(nc, *args)
    r = run_bass_kernel_spmd(nc, [arrays], core_ids=[0])
    return r.results[0]["out_0"].reshape(BATCH, SEQ, H)
```
